# Optimizing a Trainium2 kernel written in Bass

```python
import numpy as np
import jax
import jax.numpy as jnp

def _softmax(x, axis=-1):
    return jax.nn.softmax(x, axis=axis)

def _gelu(x):
    return jax.nn.gelu(x, approximate=True)

def _silu(x):
    return jax.nn.silu(x)

def _sigmoid(x):
    return jax.nn.sigmoid(x)

def _layernorm(x, axis=-1, eps=1e-05):
    m = jnp.mean(x, axis=axis, keepdims=True)
    v = jnp.var(x, axis=axis, keepdims=True)
    return (x - m) / jnp.sqrt(v + eps)

def _scatter_add(tgt, idx, src, axis=0):
    return tgt.at[idx].add(src)

def _segment_sum(src, seg, n):
    return jax.ops.segment_sum(src, seg, n)
kernel_name = 'mk_gnn_resnorm_d2_gnn_r8_02ce21'

def setup_inputs(seed: int=0):
    np.random.seed(seed)
    _w = jnp.asarray

    def _rec_inputs():
        import jax
        import jax.numpy as jnp
        _gk = jax.random.key(seed)
        x = -0.0005121 + 1.001 * jax.random.normal(jax.random.fold_in(_gk, 1), (12500, 160), jnp.float32)
        src = jax.random.randint(jax.random.fold_in(_gk, 2), (200000,), 0, 12500, jnp.int32)
        dst = jax.random.randint(jax.random.fold_in(_gk, 3), (200000,), 0, 12500, jnp.int32)
        _o = jnp.argsort(dst, stable=True)
        src = src[_o]
        dst = dst[_o]
        edge_attr_3 = 0.00262751 + 0.999568 * jax.random.normal(jax.random.fold_in(_gk, 12), (200000, 3), jnp.float32)
        edge_attr_4 = 0.000735704 + 1.0001 * jax.random.normal(jax.random.fold_in(_gk, 13), (200000, 4), jnp.float32)
        edge_attr_64 = jax.random.uniform(jax.random.fold_in(_gk, 14), (200000, 64), jnp.float32, 0.0, 1)
        node_vec1 = -0.00719938 + 0.999885 * jax.random.normal(jax.random.fold_in(_gk, 16), (12500, 1), jnp.float32)
        return (x, src, dst, edge_attr_3, edge_attr_4, edge_attr_64, node_vec1)
    x, src, dst, edge_attr_3, edge_attr_4, edge_attr_64, node_vec1 = _rec_inputs()

    def _L0_gnn_setup():
        import jax, jax.numpy as jnp
        import numpy as np
        N = 2500
        E = 80000
        INV_SQRT3 = 0.5773502691896258
        INV8 = 0.125
        INV_SQRT32 = 0.17677669529663687
        INV64 = 0.015625
        INV32 = 0.03125
        INV_SQRT2048 = 0.022097086912079608
        key = jax.random.key(seed)
        ks = jax.random.split(key, 16)
        f32 = jnp.float32
        return {'node_features': jax.random.normal(ks[0], (N, 160), f32), 'edge_index': jax.random.randint(ks[1], (2, E), 0, N), 'edge_attr_tensor': jax.random.normal(ks[2], (E, 4), f32), 'node_attr_scalar_raw': jax.random.normal(ks[3], (N, 1), f32), 'Wm_ss': jax.random.normal(ks[4], (64, 64), f32), 'Wm_vv': jax.random.normal(ks[5], (32, 64), f32), 'Wm_sv': jax.random.normal(ks[6], (64, 32), f32), 'Wm_vs': jax.random.normal(ks[7], (32, 32), f32), 'Lm_s': jax.random.normal(ks[8], (64, 64), f32), 'Lm_v': jax.random.normal(ks[9], (32, 32), f32), 'Wu_ss': jax.random.normal(ks[10], (64, 64, 64), f32), 'Wu_vv': jax.random.normal(ks[11], (32, 32, 64), f32), 'Wu_sv': jax.random.normal(ks[12], (64, 32, 32), f32), 'Wu_vs': jax.random.normal(ks[13], (32, 64, 32), f32), 'Lu_s': jax.random.normal(ks[14], (64, 64), f32), 'Lu_v': jax.random.normal(ks[15], (32, 32), f32)}
    _L0_gnn_all = _L0_gnn_setup()
    _L0_gnn_in = {k: v for k, v in _L0_gnn_all.items() if k in ('Wm_ss', 'Wm_vv', 'Wm_sv', 'Wm_vs', 'Lm_s', 'Lm_v', 'Wu_ss', 'Wu_vv', 'Wu_sv', 'Wu_vs', 'Lu_s', 'Lu_v')}
    del _L0_gnn_all

    def _L1_gnn_setup():
        import jax, jax.numpy as jnp
        import numpy as np
        N, E = (1250, 20000)
        C0, C1 = (64, 32)
        H, A = (8, 8)
        H0, H1 = (8, 4)
        M0, M1 = (128, 64)
        NG, RH = (64, 64)
        WN = C0 + C0 + C1 + C1 + C1
        DS, DV = (C0 + C1, C0 + 2 * C1)
        EPS = 1e-05
        SQ3 = np.float32(np.sqrt(3.0))
        SQ2 = np.float32(np.sqrt(2.0))

        def _split(x):
            return (x[:, :C0], x[:, C0:].reshape(x.shape[0], C1, 3))

        def _merge(s, v):
            return jnp.concatenate([s, v.reshape(v.shape[0], -1)], axis=1)

        def _eq_ln(x, w0, b0, w1):
            s, v = _split(x)
            s = s - s.mean(axis=1, keepdims=True)
            s = s * jax.lax.rsqrt(jnp.square(s).mean(axis=1, keepdims=True) + EPS) * w0 + b0
            v = v * jax.lax.rsqrt(jnp.square(v).mean(axis=(1, 2), keepdims=True) + EPS) * w1[None, :, None]
            return (s, v)

        def _eq_lin(s, v, ws, bs, wv):
            return (s @ ws + bs, jnp.einsum('nud,uk->nkd', v, wv))

        def _ln(x, g, b):
            xc = x - x.mean(-1, keepdims=True)
            return xc * jax.lax.rsqrt(jnp.square(xc).mean(-1, keepdims=True) + EPS) * g + b

        def _smooth_leaky(x, alpha=0.2):
            return 0.5 * (1 + alpha) * x + 0.5 * (1 - alpha) * x * (2.0 * jax.nn.sigmoid(x) - 1.0)

        def _forward(node_input, node_attr, edge_vec, edge_scalars, edge_src, edge_dst, ln1_w0, ln1_b0, ln1_w1, ln2_w0, ln2_b0, ln2_w1, msrc_ws, msrc_wv, mdst_ws, mdst_bs, mdst_wv, rw1, rb1, rg1, rbe1, rw2, rb2, rg2, rbe2, rw3, roff, lin_ws, lin_bs, lin_wv, alpha_dot, proj_ws, proj_bs, proj_wv, f1_ws, f1_bs, f1_wv, f2_ws, f2_bs, f2_wv):
            n = node_input.shape[0]
            s, v = _eq_ln(node_input, ln1_w0, ln1_b0, ln1_w1)
            src_s = s @ msrc_ws
            src_v = jnp.einsum('nud,uk->nkd', v, msrc_wv)
            dst_s = s @ mdst_ws + mdst_bs
            dst_v = jnp.einsum('nud,uk->nkd', v, mdst_wv)
            ms = src_s[edge_src] + dst_s[edge_dst]
            mv = src_v[edge_src] + dst_v[edge_dst]
            h = jax.nn.silu(_ln(edge_scalars @ rw1 + rb1, rg1, rbe1))
            h = jax.nn.silu(_ln(h @ rw2 + rb2, rg2, rbe2))
            w = h @ rw3 + roff
            rhat = edge_vec * jax.lax.rsqrt(jnp.sum(jnp.square(edge_vec), -1, keepdims=True) + 1e-12)
            Y1 = SQ3 * rhat
            w1, w2, w3, w4, w5 = jnp.split(w, [C0, 2 * C0, 2 * C0 + C1, 2 * C0 + 2 * C1], axis=1)
            o0a = w1 * ms
            o0b = w4 * (jnp.einsum('eud,ed->eu', mv, Y1) / SQ3)
            o1a = (w2 * ms)[:, :, None] * Y1[:, None, :]
            o1b = w3[:, :, None] * mv
            o1c = w5[:, :, None] * (jnp.cross(mv, Y1[:, None, :]) / SQ2)
            ds = jnp.concatenate([o0a, o0b], axis=1)
            dv = jnp.concatenate([o1a, o1b, o1c], axis=1)
            ls, lv = _eq_lin(ds, dv, lin_ws, lin_bs, lin_wv)
            e = ls.shape[0]
            alpha = ls[:, :H * A].reshape(e, H, A)
            vs = ls[:, H * A:].reshape(e, H, H0)
            vv = lv.reshape(e, H, H1, 3)
            a = jnp.einsum('ehk,hk->eh', _smooth_leaky(alpha), alpha_dot)
            amax = jax.lax.stop_gradient(jax.ops.segment_max(a, edge_dst, num_segments=n))
            a = jnp.exp(a - amax[edge_dst])
            a = a / (jax.ops.segment_sum(a, edge_dst, num_segments=n)[edge_dst] + 1e-12)
            ns = jax.ops.segment_sum(vs * a[..., None], edge_dst, num_segments=n).reshape(n, H * H0)
            nv = jax.ops.segment_sum(vv * a[..., None, None], edge_dst, num_segments=n).reshape(n, H * H1, 3)
            ps, pv = _eq_lin(ns, nv, proj_ws, proj_bs, proj_wv)
            x = node_input + _merge(ps, pv)
            s2, v2 = _eq_ln(x, ln2_w0, ln2_b0, ln2_w1)
            a0 = node_attr[:, :1]
            fs, fv = _eq_lin(s2, v2, f1_ws, f1_bs, f1_wv)
            fs = fs * a0
            fv = fv * a0[:, :, None]
            sc = jax.nn.silu(fs[:, :M0])
            fv = fv * jax.nn.sigmoid(fs[:, M0:])[:, :, None]
            os_, ov = _eq_lin(sc, fv, f2_ws, f2_bs, f2_wv)
            os_ = os_ * a0
            ov = ov * a0[:, :, None]
            return x + _merge(os_, ov)
        key = jax.random.key(seed)
        ks = iter(jax.random.split(key, 24))

        def nrm(shape, fan):
            return jax.random.normal(next(ks), shape, jnp.float32) / np.float32(np.sqrt(fan))
        inp = {}
        inp['node_input'] = jax.random.normal(next(ks), (N, C0 + 3 * C1), jnp.float32)
        inp['node_attr'] = jnp.ones((N, 1), jnp.float32)
        inp['edge_vec'] = jax.random.normal(next(ks), (E, 3), jnp.float32)
        inp['edge_scalars'] = jax.random.uniform(next(ks), (E, NG), dtype=jnp.float32)
        inp['edge_src'] = jax.random.randint(next(ks), (E,), 0, N)
        inp['edge_dst'] = jax.random.randint(next(ks), (E,), 0, N)
        inp['ln1_w0'] = jnp.ones((C0,), jnp.float32)
        inp['ln1_b0'] = jnp.zeros((C0,), jnp.float32)
        inp['ln1_w1'] = jnp.ones((C1,), jnp.float32)
        inp['ln2_w0'] = jnp.ones((C0,), jnp.float32)
        inp['ln2_b0'] = jnp.zeros((C0,), jnp.float32)
        inp['ln2_w1'] = jnp.ones((C1,), jnp.float32)
        inp['msrc_ws'] = nrm((C0, C0), C0)
        inp['msrc_wv'] = nrm((C1, C1), C1)
        inp['mdst_ws'] = nrm((C0, C0), C0)
        inp['mdst_bs'] = jnp.zeros((C0,), jnp.float32)
        inp['mdst_wv'] = nrm((C1, C1), C1)
        inp['rw1'] = nrm((NG, RH), NG)
        inp['rb1'] = jnp.zeros((RH,), jnp.float32)
        inp['rg1'] = jnp.ones((RH,), jnp.float32)
        inp['rbe1'] = jnp.zeros((RH,), jnp.float32)
        inp['rw2'] = nrm((RH, RH), RH)
        inp['rb2'] = jnp.zeros((RH,), jnp.float32)
        inp['rg2'] = jnp.ones((RH,), jnp.float32)
        inp['rbe2'] = jnp.zeros((RH,), jnp.float32)
        inp['rw3'] = nrm((RH, WN), RH)
        inp['roff'] = 0.1 * jax.random.normal(next(ks), (WN,), jnp.float32)
        inp['lin_ws'] = nrm((DS, H * A + H * H0), DS)
        inp['lin_bs'] = jnp.zeros((H * A + H * H0,), jnp.float32)
        inp['lin_wv'] = nrm((DV, H * H1), DV)
        inp['alpha_dot'] = nrm((H, A), A)
        inp['proj_ws'] = nrm((H * H0, C0), H * H0)
        inp['proj_bs'] = jnp.zeros((C0,), jnp.float32)
        inp['proj_wv'] = nrm((H * H1, C1), H * H1)
        inp['f1_ws'] = nrm((C0, M0 + M1), C0)
        inp['f1_bs'] = jnp.zeros((M0 + M1,), jnp.float32)
        inp['f1_wv'] = nrm((C1, M1), C1)
        inp['f2_ws'] = nrm((M0, C0), M0)
        inp['f2_bs'] = jnp.zeros((C0,), jnp.float32)
        inp['f2_wv'] = nrm((M1, C1), M1)
        return inp
    _L1_gnn_all = _L1_gnn_setup()
    _L1_gnn_in = {k: v for k, v in _L1_gnn_all.items() if k in ('ln1_w0', 'ln1_b0', 'ln1_w1', 'ln2_w0', 'ln2_b0', 'ln2_w1', 'msrc_ws', 'msrc_wv', 'mdst_ws', 'mdst_bs', 'mdst_wv', 'rw1', 'rb1', 'rg1', 'rbe1', 'rw2', 'rb2', 'rg2', 'rbe2', 'rw3', 'roff', 'lin_ws', 'lin_bs', 'lin_wv', 'alpha_dot', 'proj_ws', 'proj_bs', 'proj_wv', 'f1_ws', 'f1_bs', 'f1_wv', 'f2_ws', 'f2_bs', 'f2_wv')}
    del _L1_gnn_all
    return {'x': x, 'src': src, 'dst': dst, 'edge_attr_3': edge_attr_3, 'edge_attr_4': edge_attr_4, 'edge_attr_64': edge_attr_64, 'node_vec1': node_vec1, 'L0_gnn_Wm_ss': _L0_gnn_in['Wm_ss'], 'L0_gnn_Wm_vv': _L0_gnn_in['Wm_vv'], 'L0_gnn_Wm_sv': _L0_gnn_in['Wm_sv'], 'L0_gnn_Wm_vs': _L0_gnn_in['Wm_vs'], 'L0_gnn_Lm_s': _L0_gnn_in['Lm_s'], 'L0_gnn_Lm_v': _L0_gnn_in['Lm_v'], 'L0_gnn_Wu_ss': _L0_gnn_in['Wu_ss'], 'L0_gnn_Wu_vv': _L0_gnn_in['Wu_vv'], 'L0_gnn_Wu_sv': _L0_gnn_in['Wu_sv'], 'L0_gnn_Wu_vs': _L0_gnn_in['Wu_vs'], 'L0_gnn_Lu_s': _L0_gnn_in['Lu_s'], 'L0_gnn_Lu_v': _L0_gnn_in['Lu_v'], 'L1_gnn_ln1_w0': _L1_gnn_in['ln1_w0'], 'L1_gnn_ln1_b0': _L1_gnn_in['ln1_b0'], 'L1_gnn_ln1_w1': _L1_gnn_in['ln1_w1'], 'L1_gnn_ln2_w0': _L1_gnn_in['ln2_w0'], 'L1_gnn_ln2_b0': _L1_gnn_in['ln2_b0'], 'L1_gnn_ln2_w1': _L1_gnn_in['ln2_w1'], 'L1_gnn_msrc_ws': _L1_gnn_in['msrc_ws'], 'L1_gnn_msrc_wv': _L1_gnn_in['msrc_wv'], 'L1_gnn_mdst_ws': _L1_gnn_in['mdst_ws'], 'L1_gnn_mdst_bs': _L1_gnn_in['mdst_bs'], 'L1_gnn_mdst_wv': _L1_gnn_in['mdst_wv'], 'L1_gnn_rw1': _L1_gnn_in['rw1'], 'L1_gnn_rb1': _L1_gnn_in['rb1'], 'L1_gnn_rg1': _L1_gnn_in['rg1'], 'L1_gnn_rbe1': _L1_gnn_in['rbe1'], 'L1_gnn_rw2': _L1_gnn_in['rw2'], 'L1_gnn_rb2': _L1_gnn_in['rb2'], 'L1_gnn_rg2': _L1_gnn_in['rg2'], 'L1_gnn_rbe2': _L1_gnn_in['rbe2'], 'L1_gnn_rw3': _L1_gnn_in['rw3'], 'L1_gnn_roff': _L1_gnn_in['roff'], 'L1_gnn_lin_ws': _L1_gnn_in['lin_ws'], 'L1_gnn_lin_bs': _L1_gnn_in['lin_bs'], 'L1_gnn_lin_wv': _L1_gnn_in['lin_wv'], 'L1_gnn_alpha_dot': _L1_gnn_in['alpha_dot'], 'L1_gnn_proj_ws': _L1_gnn_in['proj_ws'], 'L1_gnn_proj_bs': _L1_gnn_in['proj_bs'], 'L1_gnn_proj_wv': _L1_gnn_in['proj_wv'], 'L1_gnn_f1_ws': _L1_gnn_in['f1_ws'], 'L1_gnn_f1_bs': _L1_gnn_in['f1_bs'], 'L1_gnn_f1_wv': _L1_gnn_in['f1_wv'], 'L1_gnn_f2_ws': _L1_gnn_in['f2_ws'], 'L1_gnn_f2_bs': _L1_gnn_in['f2_bs'], 'L1_gnn_f2_wv': _L1_gnn_in['f2_wv']}

def reference(x, src, dst, edge_attr_3, edge_attr_4, edge_attr_64, node_vec1, L0_gnn_Wm_ss, L0_gnn_Wm_vv, L0_gnn_Wm_sv, L0_gnn_Wm_vs, L0_gnn_Lm_s, L0_gnn_Lm_v, L0_gnn_Wu_ss, L0_gnn_Wu_vv, L0_gnn_Wu_sv, L0_gnn_Wu_vs, L0_gnn_Lu_s, L0_gnn_Lu_v, L1_gnn_ln1_w0, L1_gnn_ln1_b0, L1_gnn_ln1_w1, L1_gnn_ln2_w0, L1_gnn_ln2_b0, L1_gnn_ln2_w1, L1_gnn_msrc_ws, L1_gnn_msrc_wv, L1_gnn_mdst_ws, L1_gnn_mdst_bs, L1_gnn_mdst_wv, L1_gnn_rw1, L1_gnn_rb1, L1_gnn_rg1, L1_gnn_rbe1, L1_gnn_rw2, L1_gnn_rb2, L1_gnn_rg2, L1_gnn_rbe2, L1_gnn_rw3, L1_gnn_roff, L1_gnn_lin_ws, L1_gnn_lin_bs, L1_gnn_lin_wv, L1_gnn_alpha_dot, L1_gnn_proj_ws, L1_gnn_proj_bs, L1_gnn_proj_wv, L1_gnn_f1_ws, L1_gnn_f1_bs, L1_gnn_f1_wv, L1_gnn_f2_ws, L1_gnn_f2_bs, L1_gnn_f2_wv):
    import jax
    import jax.numpy as jnp

    def _L0_gnn_ref(node_features, edge_index, edge_attr_tensor, node_attr_scalar_raw, Wm_ss, Wm_vv, Wm_sv, Wm_vs, Lm_s, Lm_v, Wu_ss, Wu_vv, Wu_sv, Wu_vs, Lu_s, Lu_v):
        import jax, jax.numpy as jnp
        import numpy as np
        N = 2500
        E = 80000
        INV_SQRT3 = 0.5773502691896258
        INV8 = 0.125
        INV_SQRT32 = 0.17677669529663687
        INV64 = 0.015625
        INV32 = 0.03125
        INV_SQRT2048 = 0.022097086912079608
        n = node_features.shape[0]
        e = edge_attr_tensor.shape[0]
        row, col = (edge_index[0], edge_index[1])
        r_vec = edge_attr_tensor[:, :3]
        dist = edge_attr_tensor[:, 3:4]
        xj = node_features[col]
        s = xj[:, :64]
        v = xj[:, 64:].reshape(e, 32, 3)
        m0 = s @ Wm_ss * dist * INV8 + jnp.einsum('eui,ei->eu', v, r_vec) @ Wm_vv * (INV_SQRT3 * INV_SQRT32)
        m1 = (s @ Wm_sv)[:, :, None] * r_vec[:, None, :] * INV8 + jnp.einsum('eui,uw->ewi', v, Wm_vs) * dist[:, :, None] * INV_SQRT32
        m0 = m0 + s @ Lm_s * INV8
        m1 = m1 + jnp.einsum('eui,uw->ewi', v, Lm_v) * INV_SQRT32
        msg = jnp.concatenate([m0, m1.reshape(e, 96)], axis=-1)
        agg = jax.ops.segment_sum(msg, row, num_segments=n)
        a0 = agg[:, :64]
        a1 = agg[:, 64:].reshape(n, 32, 3)
        xs = node_features[:, :64]
        xv = node_features[:, 64:].reshape(n, 32, 3)
        u0 = jnp.einsum('nu,nv,uvw->nw', xs, a0, Wu_ss) * INV64 + jnp.einsum('nui,nvi,uvw->nw', xv, a1, Wu_vv) * (INV_SQRT3 * INV32)
        u1 = jnp.einsum('nu,nvi,uvw->nwi', xs, a1, Wu_sv) * INV_SQRT2048 + jnp.einsum('nui,nv,uvw->nwi', xv, a0, Wu_vs) * INV_SQRT2048
        u0 = u0 + xs @ Lu_s * INV8
        u1 = u1 + jnp.einsum('nui,uw->nwi', xv, Lu_v) * INV_SQRT32
        upd = jnp.concatenate([u0, u1.reshape(n, 96)], axis=-1)
        return node_features + upd

    def _L1_gnn_ref(node_input, node_attr, edge_vec, edge_scalars, edge_src, edge_dst, ln1_w0, ln1_b0, ln1_w1, ln2_w0, ln2_b0, ln2_w1, msrc_ws, msrc_wv, mdst_ws, mdst_bs, mdst_wv, rw1, rb1, rg1, rbe1, rw2, rb2, rg2, rbe2, rw3, roff, lin_ws, lin_bs, lin_wv, alpha_dot, proj_ws, proj_bs, proj_wv, f1_ws, f1_bs, f1_wv, f2_ws, f2_bs, f2_wv):
        import jax, jax.numpy as jnp
        import numpy as np
        N, E = (1250, 20000)
        C0, C1 = (64, 32)
        H, A = (8, 8)
        H0, H1 = (8, 4)
        M0, M1 = (128, 64)
        NG, RH = (64, 64)
        WN = C0 + C0 + C1 + C1 + C1
        DS, DV = (C0 + C1, C0 + 2 * C1)
        EPS = 1e-05
        SQ3 = np.float32(np.sqrt(3.0))
        SQ2 = np.float32(np.sqrt(2.0))

        def _split(x):
            return (x[:, :C0], x[:, C0:].reshape(x.shape[0], C1, 3))

        def _merge(s, v):
            return jnp.concatenate([s, v.reshape(v.shape[0], -1)], axis=1)

        def _eq_ln(x, w0, b0, w1):
            s, v = _split(x)
            s = s - s.mean(axis=1, keepdims=True)
            s = s * jax.lax.rsqrt(jnp.square(s).mean(axis=1, keepdims=True) + EPS) * w0 + b0
            v = v * jax.lax.rsqrt(jnp.square(v).mean(axis=(1, 2), keepdims=True) + EPS) * w1[None, :, None]
            return (s, v)

        def _eq_lin(s, v, ws, bs, wv):
            return (s @ ws + bs, jnp.einsum('nud,uk->nkd', v, wv))

        def _ln(x, g, b):
            xc = x - x.mean(-1, keepdims=True)
            return xc * jax.lax.rsqrt(jnp.square(xc).mean(-1, keepdims=True) + EPS) * g + b

        def _smooth_leaky(x, alpha=0.2):
            return 0.5 * (1 + alpha) * x + 0.5 * (1 - alpha) * x * (2.0 * jax.nn.sigmoid(x) - 1.0)

        def _forward(node_input, node_attr, edge_vec, edge_scalars, edge_src, edge_dst, ln1_w0, ln1_b0, ln1_w1, ln2_w0, ln2_b0, ln2_w1, msrc_ws, msrc_wv, mdst_ws, mdst_bs, mdst_wv, rw1, rb1, rg1, rbe1, rw2, rb2, rg2, rbe2, rw3, roff, lin_ws, lin_bs, lin_wv, alpha_dot, proj_ws, proj_bs, proj_wv, f1_ws, f1_bs, f1_wv, f2_ws, f2_bs, f2_wv):
            n = node_input.shape[0]
            s, v = _eq_ln(node_input, ln1_w0, ln1_b0, ln1_w1)
            src_s = s @ msrc_ws
            src_v = jnp.einsum('nud,uk->nkd', v, msrc_wv)
            dst_s = s @ mdst_ws + mdst_bs
            dst_v = jnp.einsum('nud,uk->nkd', v, mdst_wv)
            ms = src_s[edge_src] + dst_s[edge_dst]
            mv = src_v[edge_src] + dst_v[edge_dst]
            h = jax.nn.silu(_ln(edge_scalars @ rw1 + rb1, rg1, rbe1))
            h = jax.nn.silu(_ln(h @ rw2 + rb2, rg2, rbe2))
            w = h @ rw3 + roff
            rhat = edge_vec * jax.lax.rsqrt(jnp.sum(jnp.square(edge_vec), -1, keepdims=True) + 1e-12)
            Y1 = SQ3 * rhat
            w1, w2, w3, w4, w5 = jnp.split(w, [C0, 2 * C0, 2 * C0 + C1, 2 * C0 + 2 * C1], axis=1)
            o0a = w1 * ms
            o0b = w4 * (jnp.einsum('eud,ed->eu', mv, Y1) / SQ3)
            o1a = (w2 * ms)[:, :, None] * Y1[:, None, :]
            o1b = w3[:, :, None] * mv
            o1c = w5[:, :, None] * (jnp.cross(mv, Y1[:, None, :]) / SQ2)
            ds = jnp.concatenate([o0a, o0b], axis=1)
            dv = jnp.concatenate([o1a, o1b, o1c], axis=1)
            ls, lv = _eq_lin(ds, dv, lin_ws, lin_bs, lin_wv)
            e = ls.shape[0]
            alpha = ls[:, :H * A].reshape(e, H, A)
            vs = ls[:, H * A:].reshape(e, H, H0)
            vv = lv.reshape(e, H, H1, 3)
            a = jnp.einsum('ehk,hk->eh', _smooth_leaky(alpha), alpha_dot)
            amax = jax.lax.stop_gradient(jax.ops.segment_max(a, edge_dst, num_segments=n))
            a = jnp.exp(a - amax[edge_dst])
            a = a / (jax.ops.segment_sum(a, edge_dst, num_segments=n)[edge_dst] + 1e-12)
            ns = jax.ops.segment_sum(vs * a[..., None], edge_dst, num_segments=n).reshape(n, H * H0)
            nv = jax.ops.segment_sum(vv * a[..., None, None], edge_dst, num_segments=n).reshape(n, H * H1, 3)
            ps, pv = _eq_lin(ns, nv, proj_ws, proj_bs, proj_wv)
            x = node_input + _merge(ps, pv)
            s2, v2 = _eq_ln(x, ln2_w0, ln2_b0, ln2_w1)
            a0 = node_attr[:, :1]
            fs, fv = _eq_lin(s2, v2, f1_ws, f1_bs, f1_wv)
            fs = fs * a0
            fv = fv * a0[:, :, None]
            sc = jax.nn.silu(fs[:, :M0])
            fv = fv * jax.nn.sigmoid(fs[:, M0:])[:, :, None]
            os_, ov = _eq_lin(sc, fv, f2_ws, f2_bs, f2_wv)
            os_ = os_ * a0
            ov = ov * a0[:, :, None]
            return x + _merge(os_, ov)
        return _forward(node_input, node_attr, edge_vec, edge_scalars, edge_src, edge_dst, ln1_w0, ln1_b0, ln1_w1, ln2_w0, ln2_b0, ln2_w1, msrc_ws, msrc_wv, mdst_ws, mdst_bs, mdst_wv, rw1, rb1, rg1, rbe1, rw2, rb2, rg2, rbe2, rw3, roff, lin_ws, lin_bs, lin_wv, alpha_dot, proj_ws, proj_bs, proj_wv, f1_ws, f1_bs, f1_wv, f2_ws, f2_bs, f2_wv)
    edge_index = jnp.stack([src, dst])
    x = _layernorm(x + _L0_gnn_ref(x, edge_index, edge_attr_4, node_vec1, L0_gnn_Wm_ss, L0_gnn_Wm_vv, L0_gnn_Wm_sv, L0_gnn_Wm_vs, L0_gnn_Lm_s, L0_gnn_Lm_v, L0_gnn_Wu_ss, L0_gnn_Wu_vv, L0_gnn_Wu_sv, L0_gnn_Wu_vs, L0_gnn_Lu_s, L0_gnn_Lu_v), axis=-1)
    x = _layernorm(x + _L1_gnn_ref(x, node_vec1, edge_attr_3, edge_attr_64, src, dst, L1_gnn_ln1_w0, L1_gnn_ln1_b0, L1_gnn_ln1_w1, L1_gnn_ln2_w0, L1_gnn_ln2_b0, L1_gnn_ln2_w1, L1_gnn_msrc_ws, L1_gnn_msrc_wv, L1_gnn_mdst_ws, L1_gnn_mdst_bs, L1_gnn_mdst_wv, L1_gnn_rw1, L1_gnn_rb1, L1_gnn_rg1, L1_gnn_rbe1, L1_gnn_rw2, L1_gnn_rb2, L1_gnn_rg2, L1_gnn_rbe2, L1_gnn_rw3, L1_gnn_roff, L1_gnn_lin_ws, L1_gnn_lin_bs, L1_gnn_lin_wv, L1_gnn_alpha_dot, L1_gnn_proj_ws, L1_gnn_proj_bs, L1_gnn_proj_wv, L1_gnn_f1_ws, L1_gnn_f1_bs, L1_gnn_f1_wv, L1_gnn_f2_ws, L1_gnn_f2_bs, L1_gnn_f2_wv), axis=-1)
    return x

_drawn_inputs = setup_inputs


def setup_inputs(seed=0):
    import zlib

    import numpy as np

    out = dict(_drawn_inputs(seed))
    spreads = {'L1_gnn_ln1_w0': (1.0, 0.2),
     'L1_gnn_ln1_b0': (0.0, 0.267),
     'L1_gnn_ln1_w1': (1.0, 0.2),
     'L1_gnn_ln2_w0': (1.0, 0.2),
     'L1_gnn_ln2_b0': (0.0, 0.326),
     'L1_gnn_ln2_w1': (1.0, 0.2),
     'L1_gnn_mdst_bs': (0.0, 0.317),
     'L1_gnn_rb1': (0.0, 0.1),
     'L1_gnn_rg1': (1.0, 0.2),
     'L1_gnn_rbe1': (0.0, 0.314),
     'L1_gnn_rb2': (0.0, 0.1),
     'L1_gnn_rg2': (1.0, 0.2),
     'L1_gnn_rbe2': (0.0, 0.1),
     'L1_gnn_lin_bs': (0.0, 0.1),
     'L1_gnn_proj_bs': (0.0, 0.1),
     'L1_gnn_f1_bs': (0.0, 0.32),
     'L1_gnn_f2_bs': (0.0, 0.308)}
    factors = {}
    for name, (base, spread) in spreads.items():
        noise = np.random.default_rng([zlib.crc32(name.encode()), seed]).standard_normal(out[name].shape)
        drawn = base * np.exp(spread * noise) if base else spread * noise
        out[name] = jnp.asarray(drawn.astype(out[name].dtype))
    for name, factor in factors.items():
        out[name] = (out[name] * factor).astype(out[name].dtype)
    return out
```

```python
from contextlib import ExitStack

import numpy as np

import concourse.bass as bass
from concourse import mybir
from concourse.alu_op_type import AluOpType as ALU

F32 = mybir.dt.float32
I32 = mybir.dt.int32
BF16 = mybir.dt.bfloat16
ACT = mybir.ActivationFunctionType
AX = mybir.AxisListType

N, E = 12500, 200000
R = 125
NT, ET = N // R, E // R
GT = 4
S, V = 64, 32
V3 = 3 * V
X = S + V3
COPIES = 4
DUMP = N
HALF = 62
MSG0 = X + V
MSG1 = X + 8
HEADS = 8
CH = 16
EC = E // CH
BIG = 1e30
EPS = 1e-5


def strict_ranks():
    c = np.zeros((128, 8), np.float32)
    for j in range(R):
        if j < HALF:
            c[j, 0] = 2.0 ** -j
            c[j, 2] = 2.0 ** (j - 1) / 1.25
        else:
            c[j, 1] = 2.0 ** -(j - HALF)
            c[j, 2] = 2.0 ** HALF
            c[j, 3] = 2.0 ** (j - HALF - 1) / 1.25
        c[j, 4] = DUMP + j
    return c


class Chain:

    def __init__(self, eng, sem, per, t):
        self.eng, self.sem, self.per, self.n = eng, sem, per, 0
        self.base = t * per if isinstance(t, int) else eng.snap(t * per)

    def __call__(self, ins):
        ins.then_inc(self.sem, 1)
        self.n += 1
        return ins

    def sync(self):
        self.eng.wait_ge(self.sem, self.base + self.n)

    def end(self):
        assert self.n == self.per, (self.n, self.per)


class Mem:

    def __init__(self, nc, ctx):
        self.nc, self.ctx, self.sems = nc, ctx, []
        ctx.callback(self.clear)

    def clear(self):
        if self.sems:
            self.nc.clear_and_free_semaphores(self.sems)
            self.nc.all_engine_barrier()

    def sb(self, name, shape, dt=F32):
        return self.ctx.enter_context(self.nc.sbuf_tensor(name, shape, dt))

    def sem(self, name):
        self.sems.append(self.nc.alloc_semaphore(name))
        return self.sems[-1]


def row_of(v, n):
    return v.rearrange("(a n) -> a n", a=1)[:, 0:n]


def col_of(v):
    return v.rearrange("(n a) -> n a", a=1)


def bc(ap, count, at):
    shape = list(ap.shape)
    return ap.unsqueeze(at).broadcast_to(shape[:at] + [count] + shape[at:])


def gate(eng, k):
    eng.wait_ge(k["ready"], 4)


class Settle:

    def __init__(self, m, k, name):
        self.k, self.cell, self.done = k, m.sb(name + "_cell", [1, 1]), m.sem(name + "_settled")

    def __call__(self, pool, n):
        pool.wait_ge(self.done, n)
        z = self.k["zeros"][0:1, 0:1]
        pool.tensor_tensor(self.cell[:], z, z, ALU.add).then_inc(self.done, 1)


def constants(nc, m, ranks):
    k = dict(ident=m.sb("ident", [128, 128]), ranks=m.sb("ranks_sb", [128, 8]), ready=m.sem("ready"),
             loaded=m.sem("ranks_loaded"), zeros=m.sb("zeros", [128, 2048]), ones=m.sb("ones", [128, 128]))
    with nc.Block() as block:
        @block.gpsimd
        def _(pool):
            pool.memset(k["ident"][:], 0.0).then_inc(k["ready"], 1)
            pool.memset(k["zeros"][:], 0.0).then_inc(k["ready"], 1)
            pool.memset(k["ones"][:], 1.0).then_inc(k["ready"], 1)
            pool.wait_ge(k["ready"], 3)
            pool.affine_select(out=k["ident"][:], in_=k["ident"][:], compare_op=ALU.not_equal, fill=1.0,
                               base=0, pattern=[[-1, 128]], channel_multiplier=1).then_inc(k["ready"], 1)
            pool.wait_ge(k["ready"], 4)

        @block.sync
        def _(sp):
            sp.dma_start(k["ranks"][:], ranks).then_inc(k["loaded"], 16)
            sp.wait_ge(k["loaded"], 16)
    return k


def clear(nc, m, k, name, table):
    done = m.sem(name)
    flat = table.rearrange("c r w -> (c r w)")
    per = flat.shape[0] // 128
    flat = flat.rearrange("(p w) -> p w", p=128)
    n = -(-per // 2048)
    with nc.Block() as block:
        @block.sync
        def _(sp):
            for i in range(n):
                w = min(2048, per - i * 2048)
                sp.dma_start(flat[:, i * 2048:i * 2048 + w], k["zeros"][:, 0:w]).then_inc(done, 16)
            sp.wait_ge(done, 16 * n)


def edge_rows(nc, m, k, ps, name, src, comps, dt, out_f=None, out_i=None):
    TC = 100
    own = ExitStack()
    with own:
        mm = Mem(nc, own)
        raw = mm.sb(name + "_raw", [TC, 2, R * comps], dt)
        flt = mm.sb(name + "_flt", [TC, 2, R * comps]) if dt != F32 else raw
        got = [m.sem(f"{name}_got{p}") for p in range(2)]
        cast, turned, kept = m.sem(name + "_cast"), m.sem(name + "_turned"), m.sem(name + "_kept")
        view = src.rearrange("(c t r) k -> c t (r k)", t=TC, r=R)
        with nc.Block() as block:
            @block.sync
            def _(sp):
                for c in range(CH):
                    if c >= 2:
                        sp.wait_ge(turned, c - 1)
                    sp.dma_start(raw[:, c % 2, :], view[c]).then_inc(got[c % 2], 16)

            @block.tensor
            def _(pe):
                for c in range(CH):
                    if dt == F32:
                        pe.wait_ge(got[c % 2], 16 * (c // 2 + 1))
                    else:
                        pe.wait_ge(cast, c + 1)
                    if c >= 2:
                        pe.wait_ge(kept, c - 1)
                    v = flt[:, c % 2, :].rearrange("t (r k) -> t k r", k=comps)
                    for j in range(comps):
                        last = pe.transpose(ps[0:R, 2 * (c % 2) + j // 4, 128 * (j % 4):128 * (j % 4) + TC],
                                            v[:, j, :], k["ident"][0:TC, 0:TC])
                    last.then_inc(turned, 1)

            @block.vector
            def _(dve):
                def convert(c):
                    if dt != F32:
                        dve.wait_ge(got[c % 2], 16 * (c // 2 + 1))
                        if c >= 2:
                            dve.wait_ge(turned, c - 1)
                        dve.tensor_copy(flt[:, c % 2, :], raw[:, c % 2, :]).then_inc(cast, 1)
                convert(0)
                for c in range(CH):
                    if c + 1 < CH:
                        convert(c + 1)
                    dve.wait_ge(turned, c + 1)
                    outs = [o for o in (out_f, out_i) if o is not None]
                    for o in outs:
                        for j in range(comps):
                            last = dve.tensor_copy(o[:, j, TC * c:TC * c + TC],
                                                   ps[0:R, 2 * (c % 2) + j // 4, 128 * (j % 4):128 * (j % 4) + TC])
                    last.then_inc(kept, 1)
                dve.wait_ge(kept, CH)


class Scatter:

    def __init__(self, nc, m, k, ps, name, width, index, index_dram, sums, bank):
        self.nc, self.k, self.ps, self.w, self.bank = nc, k, ps, width, bank
        self.index, self.sums = index, sums
        self.rows_dram = index_dram.rearrange("(g n) -> g n", n=GT * R)
        W = width + 2
        self.u = m.sb(name + "_u", [R, 2, GT, W])
        self.q = m.sb(name + "_q", [R, 2, GT, R])
        self.row = m.sb(name + "_row", [128, 2, GT * R], I32)
        self.total = m.sb(name + "_total", [R, 2, GT, W])
        self.small = m.sb(name + "_small", [R, 2, 2, GT])
        self.place = m.sb(name + "_place", [R, 2, GT], I32)
        pair = lambda what: [m.sem(f"{name}_{what}{p}") for p in range(2)]
        self.row_here, self.q_ready, self.u_ready = pair("row_here"), pair("q_ready"), pair("u_ready")
        self.summed, self.total_ready, self.placed = pair("summed"), pair("total_ready"), pair("placed")
        self.settle = [Settle(m, k, f"{name}_add{p}") for p in range(2)]
        self.back, self.ranked = pair("back"), m.sem(name + "_ranked")
        self.added = [[m.sem(f"{name}_added{p}{c}") for c in range(GT)] for p in range(2)]

    def load(self, sp, p, t):
        gate(sp, self.k)
        sp.wait_ge(self.q_ready[p], t)
        sp.dma_start(self.row[:, p, :], self.rows_dram[bass.ds(2 * t + p, 1), :].broadcast_to([128, GT * R])
                     ).then_inc(self.row_here[p], 16)

    def ranks(self, dve):
        for p in range(2):
            for c in range(GT):
                last = dve.tensor_copy(self.u[:, p, c, self.w:self.w + 2], self.k["ranks"][0:R, 0:2])
        last.then_inc(self.ranked, 1)
        dve.wait_ge(self.ranked, 1)

    def equal(self, dve, p, t):
        gate(dve, self.k)
        dve.wait_ge(self.row_here[p], 16 * t + 16)
        dve.wait_ge(self.summed[p], t)
        for c in range(GT):
            last = dve.tensor_scalar(self.q[:, p, c, :], self.row[0:R, p, R * c:R * c + R],
                                     self.index[:, 0, bass.ds(8 * t + 4 * p + c, 1)], None, ALU.is_equal)
        last.then_inc(self.q_ready[p], 1)

    def add_equal(self, pe, p, t):
        gate(pe, self.k)
        pe.wait_ge(self.q_ready[p], t + 1)
        pe.wait_ge(self.u_ready[p], t + 1)
        pe.wait_ge(self.total_ready[p], t)
        for c in range(GT):
            last = pe.matmul(self.ps[0:R, self.bank + 2 * p + c // 2, 256 * (c % 2):256 * (c % 2) + self.w + 2],
                             self.q[:, p, c, :], self.u[:, p, c, :], start=True, stop=True)
        last.then_inc(self.summed[p], 1)

    def evacuate(self, act, p, t):
        gate(act, self.k)
        act.wait_ge(self.summed[p], t + 1)
        act.wait_ge(self.placed[p], t)
        for c in range(GT):
            act.wait_ge(self.added[p][c], 16 * t)
        for b in range(2):
            src = self.ps[0:R, self.bank + 2 * p + b, :].rearrange("n (a w) -> n a w", a=2)[:, :, 0:self.w + 2]
            last = act.activation(self.total[:, p, 2 * b:2 * b + 2, :], src, ACT.Copy)
        last.then_inc(self.total_ready[p], 1)

    def places(self, dve, p, t):
        ranks, tot, small = self.k["ranks"], self.total[:, p, :, :], self.small[:, p, :, :]
        idx = self.index[:, 0, bass.ds(8 * t + 4 * p, GT)]
        step = Chain(dve, self.back[p], 4, t)
        gate(dve, self.k)
        dve.wait_ge(self.total_ready[p], t + 1)
        for c in range(GT):
            dve.wait_ge(self.added[p][c], 16 * t)
        step(dve.tensor_scalar(small[:, 0, :], tot[:, :, self.w], ranks[0:R, 2:3], None, ALU.mult))
        step(dve.tensor_scalar(small[:, 1, :], idx, -1.0, ranks[0:R, 4:5], ALU.mult, ALU.add))
        step.sync()
        step(dve.scalar_tensor_tensor(out=small[:, 0, :], in0=tot[:, :, self.w + 1], scalar=ranks[0:R, 3:4],
                                      in1=small[:, 0, :], op0=ALU.mult, op1=ALU.add))
        step.sync()
        step(dve.scalar_tensor_tensor(out=small[:, 1, :], in0=small[:, 0, :], scalar=1.0, in1=small[:, 1, :],
                                      op0=ALU.is_gt, op1=ALU.mult))
        step.sync()
        step.end()
        dve.tensor_tensor(self.place[:, p, :], small[:, 1, :], idx, ALU.add).then_inc(self.placed[p], 1)

    def add(self, pool, p, t):
        pool.wait_ge(self.placed[p], t + 1)
        pool.wait_ge(self.total_ready[p], t + 1)
        for c in range(GT):
            if c % 2 == 0:
                pool.wait_ge(self.added[1 - p][c], 16 * t + 16 * p)
                pool.wait_ge(self.added[1 - p][c + 1], 16 * t + 16 * p)
                self.settle[p](pool, 2 * t + c // 2)
            pool.indirect_dma_start(self.sums[c], bass.IndirectOffsetOnAxis(ap=self.place[:, p, c:c + 1], axis=0),
                                    self.total[:, p, c, 0:self.w], None, compute_op=ALU.add
                                    ).then_inc(self.added[p][c], 16)

    def finish(self, pool):
        for p in range(2):
            for c in range(GT):
                pool.wait_ge(self.added[p][c], 16 * (ET // GT // 2))


def layer0_edges(nc, m, k, ps, W, T0, dstI, srcF, src, attr, sums, es, H):
    own = ExitStack()
    with own:
        mm = Mem(nc, own)
        sc = Scatter(nc, mm, k, ps, "e0", MSG0, srcF, src, sums, 0)
        rows = mm.sb("e0_rows", [R, 2, GT, 448])
        at = mm.sb("e0_at", [R, 2, GT], I32)
        prod = mm.sb("e0_prod", [R, 2, GT, 3, V])
        prodD = mm.sb("e0_prodD", [R, 2, GT, 3, V])
        here = [[m.sem(f"e0_here{p}{c}") for c in range(GT)] for p in range(2)]
        at_ready = [m.sem(f"e0_at_ready{p}") for p in range(2)]
        steps = [m.sem(f"e0_steps{p}") for p in range(2)]
        settle = [Settle(mm, k, f"e0_gather{p}") for p in range(2)]
        GP = ET // GT // 2

        def gather(pool, p, t):
            pool.wait_ge(sc.u_ready[p], t)
            for c in range(GT):
                pool.wait_ge(here[p][c], 16 * t)
            settle[p](pool, 2 * t)
            pool.tensor_copy(at[:, p, :], dstI[:, 0, bass.ds(8 * t + 4 * p, GT)]).then_inc(at_ready[p], 1)
            for c in range(GT):
                if c == 0:
                    pool.wait_ge(at_ready[p], t + 1)
                    settle[p](pool, 2 * t + 1)
                pool.indirect_dma_start(rows[:, p, c, :], None, T0, bass.IndirectOffsetOnAxis(
                    ap=at[:, p, c:c + 1], axis=0)).then_inc(here[p][c], 16)

        def messages(dve, p, t):
            sc.equal(dve, p, t)
            u, g, pr, pd = sc.u[:, p], rows[:, p], prod[:, p], prodD[:, p]
            step = Chain(dve, steps[p], 8, t)
            col = 8 * t + 4 * p
            gate(dve, k)
            for c in range(GT):
                dve.wait_ge(here[p][c], 16 * t + 16)
            r = attr[:, 0:3, bass.ds(col, GT)].rearrange("n i c -> n c i")
            r4 = bc(r, V, 3)
            step(dve.tensor_tensor(pr[:], g[:, :, 352:448].rearrange("n c (i u) -> n c i u", i=3), r4, ALU.mult))
            step(dve.tensor_tensor(pd[:], bc(g[:, :, 320:352], 3, 2), r4, ALU.mult))
            for c in range(GT):
                step(dve.scalar_tensor_tensor(out=u[:, c, 0:X], in0=g[:, c, 0:X],
                                              scalar=attr[:, 3, bass.ds(col + c, 1)], in1=g[:, c, X:2 * X],
                                              op0=ALU.mult, op1=ALU.add))
            step.sync()
            step(dve.tensor_tensor(u[:, :, S:X].rearrange("n c (i u) -> n c i u", i=3),
                                   u[:, :, S:X].rearrange("n c (i u) -> n c i u", i=3), pd[:], ALU.add))
            step(dve.tensor_tensor(pr[:, :, 0, :], pr[:, :, 0, :], pr[:, :, 1, :], ALU.add))
            step.sync()
            step.end()
            dve.tensor_tensor(u[:, :, X:X + V], pr[:, :, 0, :], pr[:, :, 2, :], ALU.add).then_inc(sc.u_ready[p], 1)

        net = Radial(mm, k, ps, W, es, H)
        rounds = GP // 2
        with nc.Block() as block:
            @block.sync
            def _(sp):
                for p in range(2):
                    sc.load(sp, p, 0)
                net.load(sp, 0)
                with sp.Fori(0, rounds - 1) as t:
                    for p in range(2):
                        sc.load(sp, p, 2 * t + 1)
                    net.load(sp, t + 1)
                    for p in range(2):
                        sc.load(sp, p, 2 * t + 2)
                    net.store(sp, t)
                for p in range(2):
                    sc.load(sp, p, 2 * rounds - 1)
                net.store(sp, rounds - 1)
                net.finish(sp)

            @block.gpsimd
            def _(pool):
                gather(pool, 0, 0)
                gather(pool, 1, 0)
                with pool.Fori(0, GP - 1) as t:
                    for p in range(2):
                        gather(pool, p, t + 1)
                        sc.add(pool, p, t)
                for p in range(2):
                    sc.add(pool, p, GP - 1)
                sc.finish(pool)

            @block.vector
            def _(dve):
                def round_(t, last):
                    for s in range(4):
                        p, g = s % 2, 2 * t + s // 2
                        if p == 0:
                            messages(dve, 1, g)
                        elif not (last and s == 3):
                            messages(dve, 0, g + 1)
                        sc.places(dve, p, g)
                        if s % 2:
                            net.normalise(dve, t, s // 2 + 1)
                sc.ranks(dve)
                messages(dve, 0, 0)
                with dve.Fori(0, rounds - 1) as t:
                    round_(t, False)
                round_(rounds - 1, True)

            @block.tensor
            def _(pe):
                with pe.Fori(0, rounds) as t:
                    for s in range(4):
                        net.products(pe, t, s)
                        sc.add_equal(pe, s % 2, 2 * t + s // 2)

            @block.scalar
            def _(act):
                with act.Fori(0, rounds) as t:
                    for s in range(4):
                        net.squares_and_roots(act, t, s)
                        sc.evacuate(act, s % 2, 2 * t + s // 2)
                        if s % 2:
                            net.silu(act, t, s // 2 + 1)


def run_edges(nc, sc, messages, GP, load):
    with nc.Block() as block:
        @block.sync
        def _(sp):
            with sp.Fori(0, GP) as t:
                for p in range(2):
                    load(sp, p, t)
                    sc.load(sp, p, t)

        @block.gpsimd
        def _(pool):
            with pool.Fori(0, GP) as t:
                for p in range(2):
                    sc.add(pool, p, t)
            sc.finish(pool)

        @block.vector
        def _(dve):
            sc.ranks(dve)
            messages(dve, 0, 0)
            with dve.Fori(0, GP - 1) as t:
                messages(dve, 1, t)
                sc.places(dve, 0, t)
                messages(dve, 0, t + 1)
                sc.places(dve, 1, t)
            messages(dve, 1, GP - 1)
            sc.places(dve, 0, GP - 1)
            sc.places(dve, 1, GP - 1)

        @block.tensor
        def _(pe):
            with pe.Fori(0, GP) as t:
                for p in range(2):
                    sc.add_equal(pe, p, t)

        @block.scalar
        def _(act):
            with act.Fori(0, GP) as t:
                for p in range(2):
                    sc.evacuate(act, p, t)


class Radial:

    def __init__(self, m, k, ps, W, es, H):
        self.k, self.ps, self.W, self.H = k, ps, W, H
        self.raw = m.sb("r_raw", [R, 2, GT, 2, S])
        self.xT, self.sq, self.std, self.rstd, self.y, self.h, self.h2 = (
            m.sb("r_" + n, [128, 2, GT * R]) for n in ("xT", "sq", "std", "rstd", "y", "h", "h2"))
        self.here = [m.sem(f"r_here{p}") for p in range(2)]
        self.stored = [m.sem(f"r_stored{p}") for p in range(2)]
        both = lambda names: [f"{n}{p}" for n in names for p in range(2)]
        self.pe_s = Steps(m, k, "r_pe", both(["turned", "h1_", "v1_", "h2_", "v2_"]))
        self.ac_s = Steps(m, k, "r_act", both(["xT", "sq1_", "std1_", "silu1_", "sq2_", "std2_", "silu2_"]))
        self.dv_s = Steps(m, k, "r_dve", both(["r1_", "y1_", "r2_", "y2_"]))
        self.view = es.rearrange("(g h j r) k -> g h r j k", h=2, j=GT, r=R)

    def load(self, sp, t):
        if not isinstance(t, int):
            self.pe_s.wait(sp, t - 1, "turned1")
        for p in range(2):
            for half in range(2):
                sp.dma_start(self.raw[:, p, :, half, :], self.view[bass.ds(2 * t + p, 1), half].rearrange(
                    "g r j k -> (g r) j k")).then_inc(self.here[p], 16)

    def store(self, sp, t):
        for p in range(2):
            self.ac_s.wait(sp, t, f"silu2_{p}")
            sp.dma_start(self.H[bass.ds(2 * t + p, 1)].rearrange("g q n -> (g q) n"), self.h2[:, p, :]
                         ).then_inc(self.stored[p], 16)

    def finish(self, sp):
        for p in range(2):
            sp.wait_ge(self.stored[p], 16 * (ET // (4 * GT)))

    def products(self, pe, t, s):
        ps, W, lay = self.ps, self.W, s // 2 + 1
        for p in range(2):
            if s == 0:
                gate(pe, self.k)
                pe.wait_ge(self.here[p], 32 * t + 32)
                pe.wait_ge(self.ac_s.sem, t * len(self.ac_s.names))
                for j in range(GT):
                    last = pe.transpose(ps[:, 4 + p, R * j:R * j + R], self.raw[:, p, j].rearrange("r h k -> r (h k)"),
                                        self.k["ident"][0:R, 0:R])
                self.pe_s.done(last, f"turned{p}")
        for p in range(2):
            if s % 2 == 0:
                src, ready = (self.xT, "xT") if s == 0 else (self.h, "silu1_")
                self.ac_s.wait(pe, t, f"{ready}{p}")
                self.pe_s.done(pe.matmul(ps[:, 6 + p, 0:GT * R], W[f"r{lay}"][:], src[:, p, :],
                                         start=True, stop=True), f"h{lay}_{p}")
            else:
                self.ac_s.wait(pe, t, f"sq{lay}_{p}")
                self.pe_s.done(pe.matmul(ps[:, 4 + p, 0:GT * R], W["avg"][:], self.sq[:, p, :], start=True,
                                         stop=True), f"v{lay}_{p}")

    def squares_and_roots(self, act, t, s):
        ps, W, lay = self.ps, self.W, s // 2 + 1
        if s == 0:
            for p in range(2):
                self.pe_s.wait(act, t, f"turned{p}")
                self.ac_s.done(act.activation(self.xT[:, p, :], ps[:, 4 + p, 0:GT * R], ACT.Copy), f"xT{p}")
        for p in range(2):
            if s % 2 == 0:
                b = 3 * (lay - 1)
                self.pe_s.wait(act, t, f"h{lay}_{p}")
                self.ac_s.done(act.activation(self.sq[:, p, :], ps[:, 6 + p, 0:GT * R], ACT.Square,
                                              bias=W["rb"][:, b:b + 1]), f"sq{lay}_{p}")
            else:
                self.pe_s.wait(act, t, f"v{lay}_{p}")
                self.ac_s.done(act.activation(self.std[:, p, :], ps[:, 4 + p, 0:GT * R], ACT.Sqrt,
                                              bias=W["eps"][:]), f"std{lay}_{p}")

    def normalise(self, dve, t, lay):
        b = 3 * (lay - 1)
        for p in range(2):
            self.ac_s.wait(dve, t, f"std{lay}_{p}")
            self.dv_s.done(dve.reciprocal(self.rstd[:, p, :], self.std[:, p, :]), f"r{lay}_{p}")
        for p in range(2):
            self.dv_s.wait(dve, t, f"r{lay}_{p}")
            self.dv_s.done(dve.scalar_tensor_tensor(out=self.y[:, p, :], in0=self.ps[:, 6 + p, 0:GT * R],
                                                    scalar=self.W["rb"][:, b:b + 1], in1=self.rstd[:, p, :],
                                                    op0=ALU.add, op1=ALU.mult), f"y{lay}_{p}")

    def silu(self, act, t, lay):
        b = 3 * (lay - 1)
        for p in range(2):
            self.dv_s.wait(act, t, f"y{lay}_{p}")
            if lay == 2:
                gate(act, self.k)
                act.wait_ge(self.stored[p], 16 * t)
            self.ac_s.done(act.activation((self.h if lay == 1 else self.h2)[:, p, :], self.y[:, p, :], ACT.Silu,
                                          bias=self.W["rb"][:, b + 2:b + 3], scale=self.W["rb"][:, b + 1:b + 2]),
                           f"silu{lay}_{p}")


def layer0_tables(nc, m, k, ps, x, W, T0):
    own = ExitStack()
    with own:
        mm = Mem(nc, own)
        xt = mm.sb("n0_x", [R, 2, X])
        out = mm.sb("n0_out", [R, 2, 448])
        sT, vT = mm.sb("n0_sT", [S, 2, R]), mm.sb("n0_vT", [V3, 2, R])
        got = [m.sem(f"n0_got{p}") for p in range(2)]
        stored = [m.sem(f"n0_stored{p}") for p in range(2)]
        turned = [m.sem(f"n0_turned{p}") for p in range(2)]
        kept = [m.sem(f"n0_kept{p}") for p in range(2)]
        product = [m.sem(f"n0_product{p}") for p in range(2)]
        full = [m.sem(f"n0_full{p}") for p in range(2)]
        split = [m.sem(f"n0_split{p}") for p in range(2)]
        with nc.Block() as block:
            @block.sync
            def _(sp):
                with sp.Fori(0, NT // 2) as t:
                    for p in range(2):
                        gate(sp, k)
                        sp.wait_ge(turned[p], t)
                        sp.wait_ge(full[p], t * 2)
                        sp.dma_start(xt[:, p, :], x[bass.ds((2 * t + p) * R, R), :]).then_inc(got[p], 16)

            @block.tensor
            def _(pe):
                with pe.Fori(0, NT // 2) as t:
                    for p in range(2):
                        gate(pe, k)
                        pe.wait_ge(got[p], 16 * t + 16)
                        pe.wait_ge(kept[p], 2 * t)
                        pe.wait_ge(split[p], t + 1)
                        pe.transpose(ps[0:V3, p, 128:128 + R], out[:, p, 352:448], k["ident"][0:R, 0:R])
                        pe.transpose(ps[0:S, p, 0:R], xt[:, p, 0:S], k["ident"][0:R, 0:R]).then_inc(turned[p], 1)
                        gate(pe, k)
                        pe.wait_ge(kept[p], 2 * t + 2)
                        pe.wait_ge(full[p], 2 * t)
                        pe.matmul(ps[0:R, 2 + p, 0:160], sT[:, p, :], W["s"][:], start=True, stop=True)
                        pe.matmul(ps[0:R, 4 + p, 0:192], vT[:, p, :], W["v"][:], start=True,
                                  stop=True).then_inc(product[p], 1)

            @block.scalar
            def _(act):
                with act.Fori(0, NT // 2) as t:
                    for p in range(2):
                        act.wait_ge(turned[p], t + 1)
                        act.wait_ge(product[p], t)
                        act.activation(sT[:, p, :], ps[0:S, p, 0:R], ACT.Copy).then_inc(kept[p], 1)
                        act.activation(vT[:, p, :], ps[0:V3, p, 128:128 + R], ACT.Copy).then_inc(kept[p], 1)
                        act.wait_ge(product[p], t + 1)
                        act.wait_ge(stored[p], 16 * t)
                        act.activation(out[:, p, 0:320].rearrange("n (a w) -> n a w", a=2)[:, :, 0:S],
                                       ps[0:R, 2 + p, 0:128].rearrange("n (a w) -> n a w", a=2),
                                       ACT.Copy)
                        act.activation(out[:, p, 320:352], ps[0:R, 2 + p, 128:160], ACT.Copy).then_inc(full[p], 1)

            @block.vector
            def _(dve):
                with dve.Fori(0, NT // 2) as t:
                    for p in range(2):
                        gate(dve, k)
                        dve.wait_ge(got[p], 16 * t + 16)
                        dve.wait_ge(stored[p], 16 * t)
                        dve.tensor_copy(out[:, p, 352:448].rearrange("n (i u) -> n i u", i=3),
                                        xt[:, p, S:X].rearrange("n (u i) -> n i u", i=3)).then_inc(split[p], 1)
                    for p in range(2):
                        gate(dve, k)
                        dve.wait_ge(product[p], t + 1)
                        dve.tensor_copy(out[:, p, 0:320].rearrange("n (a w) -> n a w", a=2)[:, :, S:X],
                                        ps[0:R, 4 + p, 0:192].rearrange("n (a w) -> n a w", a=2)
                                        ).then_inc(full[p], 1)

            @block.gpsimd
            def _(pool):
                with pool.Fori(0, NT // 2) as t:
                    for p in range(2):
                        gate(pool, k)
                        pool.wait_ge(full[p], 2 * t + 2)
                        pool.dma_start(T0[bass.ds((2 * t + p) * R, R), :], out[:, p, :]).then_inc(stored[p], 16)
                for p in range(2):
                    pool.wait_ge(stored[p], 16 * (NT // 2))


class Steps:

    def __init__(self, m, k, name, names):
        self.k, self.sem, self.names, self.at = k, m.sem(name), names, 0

    def done(self, ins, what):
        assert self.names[self.at % len(self.names)] == what, (what, self.names[self.at % len(self.names)])
        self.at += 1
        return ins.then_inc(self.sem, 1)

    def wait(self, eng, t, what):
        gate(eng, self.k)
        eng.wait_ge(self.sem, t * len(self.names) + self.names.index(what) + 1)


class Vector(Chain):

    def __init__(self, k, sem, per, marks, t):
        self.k, self.eng, self.sem, self.per, self.n, self.marks, self.t = k, None, sem, per, 0, marks, t
        self.base = t * per

    def sync(self):
        gate(self.eng, self.k)
        self.eng.wait_ge(self.sem, self.base + self.n)

    def mark(self, name):
        self.marks[name] = self.n


def marked(eng, k, sem, per, marks, t, name):
    gate(eng, k)
    eng.wait_ge(sem, t * per + marks[name])


def load_weights(nc, m, k, name, loads, also=()):
    done, zeroed = m.sem(name + "_loaded"), m.sem(name + "_zeroed")
    tiles = list(also)
    for tile, *_ in loads:
        if all(tile is not x for x in tiles):
            tiles.append(tile)
    with nc.Block() as block:
        @block.gpsimd
        def _(pool):
            for tile in tiles:
                pool.memset(tile[:], 0.0).then_inc(zeroed, 1)
            pool.wait_ge(zeroed, len(tiles))

        @block.sync
        def _(sp):
            sp.wait_ge(zeroed, len(tiles))
            for _, to, of in loads:
                sp.dma_start(to, of).then_inc(done, 16)
            sp.wait_ge(done, 16 * len(loads))


def scale_all(nc, m, k, name, scales):
    done = m.sem(name + "_scaled")
    with nc.Block() as block:
        @block.vector
        def _(dve):
            for ap, by in scales:
                dve.tensor_scalar(ap, ap, float(by), None, ALU.mult).then_inc(done, 1)
            dve.wait_ge(done, len(scales))


def diagonal(tile, col, src, wide=V):
    return [(tile, tile[V * i:V * i + V, col + wide * i:col + wide * i + wide], src) for i in range(3)]


PER1 = 53


def node_update0(nc, m, k, ps, W, x, sums, X1, TS, TD):
    own = ExitStack()
    with own:
        mm = Mem(nc, own)
        sb = mm.sb
        xt, ag = sb("n1_x", [R, 2, X]), sb("n1_ag", [R, 2, COPIES, MSG0])
        a, xd = sb("n1_a", [R, MSG0]), sb("n1_xd", [R, V3])
        vrT, sT, vT, a0T = sb("n1_vrT", [V, R]), sb("n1_sT", [S, R]), sb("n1_vT", [V3, R]), sb("n1_a0T", [S, R])
        z, zv, zp = sb("n1_z", [R, S * S]), sb("n1_zv", [R, V * V]), sb("n1_zp", [R, 2, V * V])
        zT = sb("n1_zT", [128, 40, R])
        prod = sb("n1_prod", [R, 2, 512])
        part = sb("n1_part", [R, 2, 3, V])
        y, stat, st2, y1 = sb("n1_y", [R, X]), sb("n1_stat", [R, 2, 6]), sb("n1_st2", [R, 16]), sb("n1_y1", [R, 2, X])
        sq = sb("n1_sq", [R, V3])
        norm = sb("n1_norm", [R, X])
        snT, vnT = sb("n1_snT", [S, R]), sb("n1_vnT", [V3, R])
        out = sb("n1_out", [R, 2, 2, X])
        here = [mm.sem(f"n1_here{p}") for p in range(2)]
        stored = [mm.sem(f"n1_stored{p}") for p in range(2)]
        vec, marks = mm.sem("n1_vec"), {}
        pe_s = Steps(mm, k, "n1_pe", ["turned", "vr", "a0", "g"] + [f"z{i}" for i in range(10)] +
                     ["u0", "norm", "tables"])
        ac_s = Steps(mm, k, "n1_act", ["turned", "a0"] + [f"z{i}" for i in range(10)] +
                     ["root1", "root2", "norm", "out"])

        with nc.Block() as block:
            @block.vector
            def _(dve):
                with dve.Fori(0, NT // 2) as tt:
                    for p in range(2):
                        t = 2 * tt + p
                        v = Vector(k, vec, PER1, marks, t)
                        v.eng = dve
                        gate(dve, k)
                        dve.wait_ge(here[p], 80 * tt + 80)
                        v(dve.tensor_tensor(a[:], ag[:, p, 0, :], ag[:, p, 1, :], ALU.add))
                        v(dve.tensor_copy(xd[:].rearrange("n (i u) -> n i u", i=3),
                                          xt[:, p, S:X].rearrange("n (u i) -> n i u", i=3)))
                        v.sync()
                        v(dve.tensor_tensor(a[:], a[:], ag[:, p, 2, :], ALU.add))
                        v.sync()
                        v(dve.tensor_tensor(a[:], a[:], ag[:, p, 3, :], ALU.add))
                        v.mark("summed")
                        pe_s.wait(dve, t, "vr")
                        v.sync()
                        v(dve.tensor_tensor(a[:, 0:S], a[:, 0:S], ps[0:R, 1, 0:S], ALU.add))
                        v.mark("a0")
                        v.sync()
                        v(dve.tensor_tensor(z[:].rearrange("n (u v) -> n u v", u=S), bc(xt[:, p, 0:S], S, 2),
                                            bc(a[:, 0:S], S, 1), ALU.mult))
                        v.mark("z")
                        for i in range(3):
                            xv = bc(xd[:, V * i:V * i + V], V, 2)
                            av = bc(a[:, S + V * i:S + V * i + V], V, 1)
                            to = zv[:] if i == 0 else zp[:, i - 1, :]
                            v(dve.tensor_tensor(to.rearrange("n (u v) -> n u v", u=V), xv, av, ALU.mult))
                        v.sync()
                        v(dve.tensor_tensor(zv[:], zv[:], zp[:, 0, :], ALU.add))
                        v.sync()
                        v(dve.tensor_tensor(zv[:], zv[:], zp[:, 1, :], ALU.add))
                        v.mark("zv")
                        pe_s.wait(dve, t, "g")
                        for i in range(3):
                            for g in range(4):
                                by = a[:, S + V * i:S + V * i + V] if g < 2 else xd[:, V * i:V * i + V]
                                if i + g:
                                    v.sync()
                                v(dve.tensor_tensor(prod[:, g % 2, :].rearrange("n (w v) -> n w v", v=V),
                                                    ps[0:R, 2 + g, :].rearrange("n (w v) -> n w v", v=V),
                                                    bc(by, 16, 1), ALU.mult))
                                v.sync()
                                v(dve.tensor_reduce(part[:, g // 2, i, 16 * (g % 2):16 * (g % 2) + 16],
                                                    prod[:, g % 2, :].rearrange("n (w v) -> n w v", v=V),
                                                    AX.X, ALU.add))
                        v.mark("g")
                        v.sync()
                        p0, p1 = (part[:, q].rearrange("n i w -> n (i w)") for q in range(2))
                        v(dve.tensor_tensor(p0, p0, p1, ALU.add))
                        v(dve.tensor_scalar(y[:, 0:S], xt[:, p, 0:S], 2.0, None, ALU.mult))
                        v(dve.tensor_scalar(y[:, S:X], xd[:], 2.0, None, ALU.mult))
                        v.sync()
                        v(dve.tensor_tensor(y[:, S:X], y[:, S:X], p0, ALU.add))
                        pe_s.wait(dve, t, "u0")
                        v.sync()
                        v(dve.tensor_tensor(y[:], y[:], ps[0:R, 1, 128:128 + X], ALU.add))
                        v.sync()
                        v(dve.bn_stats(stat[:, 0, :], y[:]))
                        v.sync()
                        v(dve.memset(st2[:, 12:13], 0.0))
                        v(dve.bn_aggr(st2[:, 0:2], stat[:, 0, :]))
                        v.mark("var1")
                        ac_s.wait(dve, t, "root1")
                        v(dve.reciprocal(st2[:, 3:4], st2[:, 2:3]))
                        v.sync()
                        gate(dve, k)
                        dve.wait_ge(stored[p], 48 * tt)
                        v(dve.tensor_scalar(y1[:, p, :], y[:], st2[:, 0:1], st2[:, 3:4], ALU.subtract, ALU.mult))
                        v.mark("x1")
                        v.sync()
                        v(dve.bn_stats(stat[:, 1, :], y1[:, p, 0:S]))
                        v(dve.tensor_tensor(sq[:], y1[:, p, S:X], y1[:, p, S:X], ALU.mult))
                        v.sync()
                        v(dve.tensor_reduce(st2[:, 6:7], sq[:], AX.X, ALU.add))
                        v(dve.bn_aggr(st2[:, 4:6], stat[:, 1, :]))
                        v.sync()
                        v(dve.tensor_scalar(st2[:, 6:7], st2[:, 6:7], 1.0 / V3, None, ALU.mult))
                        v.mark("var2")
                        ac_s.wait(dve, t, "root2")
                        v(dve.reciprocal(st2[:, 10:12], st2[:, 8:10]))
                        v.sync()
                        v(dve.tensor_scalar(norm[:, 0:S], y1[:, p, 0:S], st2[:, 4:5], st2[:, 10:11],
                                            ALU.subtract, ALU.mult))
                        v(dve.tensor_scalar(norm[:, S:X], y1[:, p, S:X], st2[:, 11:12], None, ALU.mult))
                        v.mark("norm")
                        ac_s.wait(dve, t, "out")
                        v.sync()
                        v.end()

            def got(eng, t, name):
                marked(eng, k, vec, PER1, marks, t, name)

            @block.sync
            def _(sp):
                with sp.Fori(0, NT // 2) as tt:
                    for p in range(2):
                        t = 2 * tt + p
                        gate(sp, k)
                        sp.wait_ge(vec, PER1 * 2 * tt)
                        rows = bass.ds(t * R, R)
                        sp.dma_start(xt[:, p, :], x[rows, :]).then_inc(here[p], 16)
                        for c in range(COPIES):
                            sp.dma_start(ag[:, p, c, :], sums[c][rows, :]).then_inc(here[p], 16)
                    for p in range(2):
                        t = 2 * tt + p
                        rows = bass.ds(t * R, R)
                        got(sp, t, "x1")
                        sp.dma_start(X1[rows, :], y1[:, p, :]).then_inc(stored[p], 16)
                        ac_s.wait(sp, t, "out")
                        sp.dma_start(TS[rows, :], out[:, p, 0, :]).then_inc(stored[p], 16)
                        sp.dma_start(TD[rows, :], out[:, p, 1, :]).then_inc(stored[p], 16)
                for p in range(2):
                    sp.wait_ge(stored[p], 48 * (NT // 2))

            @block.tensor
            def _(pe):
                I = k["ident"]
                with pe.Fori(0, NT // 2) as tt:
                    for p in range(2):
                        t = 2 * tt + p
                        got(pe, t, "summed")
                        pe.transpose(ps[0:V, 0, 0:R], a[:, X:MSG0], I[0:R, 0:R])
                        pe.transpose(ps[0:S, 0, 128:128 + R], xt[:, p, 0:S], I[0:R, 0:R])
                        pe_s.done(pe.transpose(ps[0:V3, 0, 256:256 + R], xd[:], I[0:R, 0:R]), "turned")
                        ac_s.wait(pe, t, "turned")
                        pe_s.done(pe.matmul(ps[0:R, 1, 0:S], vrT[:], W["wvv"][:], start=True, stop=True), "vr")
                        got(pe, t, "a0")
                        pe_s.done(pe.transpose(ps[:, 0, 384:384 + R], a[:, 0:128], I[0:R, 0:R]), "a0")
                        ac_s.wait(pe, t, "a0")
                        for g in range(2):
                            pe.matmul(ps[0:R, 2 + g, :], sT[:], W["usv"][:, 512 * g:512 * g + 512], start=True, stop=True)
                        for g in range(2):
                            last = pe.matmul(ps[0:R, 4 + g, :], a0T[:], W["uvs"][:, 512 * g:512 * g + 512],
                                             start=True, stop=True)
                        pe_s.done(last, "g")
                        for b in range(10):
                            if b == 0:
                                got(pe, t, "z")
                            if b == 8:
                                got(pe, t, "zv")
                            if b >= 2:
                                ac_s.wait(pe, t, f"z{b - 2}")
                            for c in range(4):
                                src = z[:, 512 * b + 128 * c:512 * b + 128 * c + 128] if b < 8 else \
                                    zv[:, 512 * (b - 8) + 128 * c:512 * (b - 8) + 128 * c + 128]
                                last = pe.transpose(ps[:, 6 + b % 2, R * c:R * c + R], src, I[0:R, 0:R])
                            pe_s.done(last, f"z{b}")
                        ac_s.wait(pe, t, "z9")
                        u0 = ps[0:R, 1, 128:128 + S]
                        for b in range(40):
                            w = W["uss"][:, b, :] if b < 32 else W["uvv"][:, b - 32, :]
                            pe.matmul(u0, zT[:, b, :], w, start=(b == 0), stop=False)
                        pe.matmul(u0, sT[:], W["lus"][:], start=False, stop=True)
                        pe_s.done(pe.matmul(ps[0:R, 1, 128 + S:128 + X], vT[:], W["luv"][:], start=True, stop=True), "u0")
                        got(pe, t, "norm")
                        pe.transpose(ps[0:V3, 0, 128:128 + R], norm[:, S:X], I[0:R, 0:R])
                        pe_s.done(pe.transpose(ps[0:S, 0, 0:R], norm[:, 0:S], I[0:R, 0:R]), "norm")
                        ac_s.wait(pe, t, "norm")
                        pe.matmul(ps[0:R, 6, 0:S], snT[:], W["msd"][:, 0:S], start=True, stop=True)
                        pe.matmul(ps[0:R, 6, S:2 * S], snT[:], W["msd"][:, S:2 * S], start=True, stop=False)
                        pe.matmul(ps[0:R, 6, S:2 * S], k["ones"][0:1, 0:R], W["rows"][0:1, 0:S], start=False, stop=True)
                        pe_s.done(pe.matmul(ps[0:R, 6, 128:320], vnT[:], W["mv"][:], start=True, stop=True), "tables")

            @block.scalar
            def _(act):
                with act.Fori(0, NT // 2) as tt:
                    for p in range(2):
                        t = 2 * tt + p
                        pe_s.wait(act, t, "turned")
                        act.activation(vrT[:], ps[0:V, 0, 0:R], ACT.Copy)
                        act.activation(sT[:], ps[0:S, 0, 128:128 + R], ACT.Copy)
                        ac_s.done(act.activation(vT[:], ps[0:V3, 0, 256:256 + R], ACT.Copy), "turned")
                        pe_s.wait(act, t, "a0")
                        ac_s.done(act.activation(a0T[:], ps[0:S, 0, 384:384 + R], ACT.Copy), "a0")
                        for b in range(10):
                            pe_s.wait(act, t, f"z{b}")
                            ac_s.done(act.activation(zT[:, 4 * b:4 * b + 4, :].rearrange("q c n -> q (c n)"),
                                                     ps[:, 6 + b % 2, 0:4 * R], ACT.Copy), f"z{b}")
                        got(act, t, "var1")
                        ac_s.done(act.activation(st2[:, 2:3], st2[:, 1:2], ACT.Sqrt, bias=W["eps"][0:R, :]), "root1")
                        got(act, t, "var2")
                        ac_s.done(act.activation(st2[:, 8:10], st2[:, 5:7], ACT.Sqrt, bias=W["eps"][0:R, :]), "root2")
                        pe_s.wait(act, t, "norm")
                        act.activation(snT[:], ps[0:S, 0, 0:R], ACT.Identity, bias=W["ln1"][0:S, 1:2],
                                       scale=W["ln1"][0:S, 0:1])
                        ac_s.done(act.activation(vnT[:], ps[0:V3, 0, 128:128 + R], ACT.Copy,
                                                 scale=W["ln1"][0:V3, 2:3]), "norm")
                        pe_s.wait(act, t, "tables")
                        gate(act, k)
                        act.wait_ge(stored[p], 48 * tt)
                        act.activation(out[:, p, :, 0:S], ps[0:R, 6, 0:128].rearrange("n (a w) -> n a w", a=2), ACT.Copy)
                        ac_s.done(act.activation(out[:, p, :, S:X], ps[0:R, 6, 128:320].rearrange("n (a w) -> n a w", a=2),
                                                 ACT.Copy), "out")



INV_SQRT3, INV8, INV_SQRT32 = 0.5773502691896258, 0.125, 0.17677669529663687
INV64, INV32, INV_SQRT2048 = 0.015625, 0.03125, 0.022097086912079608
SQ3, SQ2 = float(np.sqrt(3.0)), float(np.sqrt(2.0))


def weights0(nc, m, k, w):
    W = dict(s=m.sb("w_s", [S, 160]), v=m.sb("w_v", [V3, 192]), wvv=m.sb("w_vv", [V, S]))
    loads = [(W["s"], W["s"][:, 0:64], w["Wm_ss"]), (W["s"], W["s"][:, 64:128], w["Lm_s"]),
             (W["s"], W["s"][:, 128:160], w["Wm_sv"]), (W["wvv"], W["wvv"][:], w["Wm_vv"])]
    loads += diagonal(W["v"], 0, w["Wm_vs"]) + diagonal(W["v"], 96, w["Lm_v"])
    load_weights(nc, m, k, "w0", loads)
    scale_all(nc, m, k, "w0", [(W["s"][:], INV8), (W["v"][:], INV_SQRT32), (W["wvv"][:], INV_SQRT3 * INV_SQRT32)])
    return W


def weights1(nc, m, k, w, W):
    own = ExitStack()
    with own:
        mm = Mem(nc, own)
        for n, shape in dict(uss=[128, V, S], uvv=[128, 8, S], usv=[S, 1024], uvs=[S, 1024], lus=[S, S],
                             luv=[V3, V3], msd=[S, 2 * S], mv=[V3, 2 * V3]).items():
            W[n] = m.sb("w_" + n, shape)
        rsv, rvs = mm.sb("raw_sv", [S, V, V]), mm.sb("raw_vs", [S, V, V])
        loads = [(W["uss"], W["uss"][:], w["Wu_ss"].rearrange("(k a) v w -> (a v) k w", a=2)),
                 (W["uvv"], W["uvv"][:], w["Wu_vv"].rearrange("(k a) v w -> (a v) k w", a=4)),
                 (rsv, rsv[:], w["Wu_sv"]), (rvs, rvs[:], w["Wu_vs"].rearrange("u v w -> v u w")),
                 (W["lus"], W["lus"][:], w["Lu_s"]), (W["msd"], W["msd"][:, 0:S], w["msrc_ws"]),
                 (W["msd"], W["msd"][:, S:2 * S], w["mdst_ws"])]
        loads += diagonal(W["luv"], 0, w["Lu_v"]) + diagonal(W["mv"], 0, w["msrc_wv"]) + \
            diagonal(W["mv"], V3, w["mdst_wv"])
        at = 0
        W["row_at"] = {}
        for n in ("mdst_bs", "proj_bs", "f1_bs", "f2_bs"):
            wide = w[n].shape[0]
            loads.append((W["rows"], W["rows"][0:1, at:at + wide], row_of(w[n], wide)))
            W["row_at"][n] = (at, at + wide)
            at += wide
        for n in ("ln1", "ln2"):
            loads += [(W[n], W[n][0:S, 0:1], col_of(w[n + "_w0"])), (W[n], W[n][0:S, 1:2], col_of(w[n + "_b0"]))]
            loads += [(W[n], W[n][V * i:V * i + V, 2:3], col_of(w[n + "_w1"])) for i in range(3)]
        load_weights(nc, m, k, "w1", loads)
        turned = mm.sem("w1_permuted")
        with nc.Block() as block:
            @block.vector
            def _(dve):
                dve.memset(W["eps"][:], EPS).then_inc(turned, 1)
                dve.tensor_copy(W["usv"][:].rearrange("u (w v) -> u w v", v=V),
                                rsv[:].rearrange("u v w -> u w v")).then_inc(turned, 1)
                dve.tensor_copy(W["uvs"][:].rearrange("v (w u) -> v w u", u=V),
                                rvs[:].rearrange("v u w -> v w u")).then_inc(turned, 1)
                dve.wait_ge(turned, 3)
        scale_all(nc, m, k, "w1", [(W["uss"][:], INV64), (W["uvv"][:], INV_SQRT3 * INV32),
                                   (W["usv"][:], INV_SQRT2048), (W["uvs"][:], INV_SQRT2048),
                                   (W["lus"][:], INV8), (W["luv"][:], INV_SQRT32)])
    return W


def weights2(nc, m, k, ps, w, W):
    for n, shape in dict(r1=[128, 128], r2=[128, 128], avg=[128, 128], rb=[128, 8], r3=[128, 224], ls=[97, 136],
                         la=[S, V], lb=[V3, V3], lc=[V3, 128], ad=[128, S]).items():
        W[n] = m.sb("w_" + n, shape)
    W["off3"], W["one3"] = m.sb("w_off3", [3, 224], BF16), m.sb("w_one3", [3, R], BF16)
    loads = []
    for h in range(2):
        lo = slice(S * h, S * h + S)
        loads += [(W["r1"], W["r1"][lo, lo], w["rw1"]), (W["r2"], W["r2"][lo, lo], w["rw2"]),
                  (W["r3"], W["r3"][lo, :], w["rw3"])]
        for j, n in enumerate(("rb1", "rg1", "rbe1", "rb2", "rg2", "rbe2")):
            loads.append((W["rb"], W["rb"][lo, j:j + 1], col_of(w[n])))
    loads += [(W["ls"], W["ls"][0:96, 0:128], w["lin_ws"]), (W["ls"], W["ls"][96:97, 0:128], row_of(w["lin_bs"], 128)),
              (W["la"], W["la"][:], w["lin_wv"][0:S, :]),
              (W["ad"], W["ad"][:], w["alpha_dot"].rearrange("(a h) k -> a (h k)", a=1).broadcast_to([128, S]))]
    loads += diagonal(W["lb"], 0, w["lin_wv"][S:S + V, :])
    for j, i in enumerate((1, 2, 0, 1)):
        loads.append((W["lc"], W["lc"][V * i:V * i + V, V * j:V * j + V], w["lin_wv"][S + V:S + 2 * V, :]))
    rest, part, total = (m.sb("w2_" + n, [3, 224]) for n in ("rest", "part", "total"))
    loads.append((rest, rest[:], w["roff"].rearrange("(a n) -> a n", a=1).broadcast_to([3, 224])))
    load_weights(nc, m, k, "w2", loads, [W["avg"]])
    scale_all(nc, m, k, "w2", [(W["la"][:], SQ3), (W["lc"][:], SQ3 / SQ2)])
    done, turned = m.sem("w2_done"), m.sem("w2_turned")
    mean = m.sb("w2_mean", [128, 8])
    tmp = m.sb("w2_tmp", [97, S])
    with nc.Block() as block:
        @block.vector
        def _(dve):
            n = 0

            def step(ins):
                nonlocal n
                n += 1
                ins.then_inc(done, 1)
                dve.wait_ge(done, n)
            for h in range(2):
                lo = slice(S * h, S * h + S)
                step(dve.memset(W["avg"][lo, lo], 1.0 / S))
            for j, r in enumerate(("r1", "r2")):
                step(dve.tensor_reduce(mean[:, j:j + 1], W[r][:], AX.X, ALU.add))
                step(dve.tensor_scalar(mean[:, j:j + 1], mean[:, j:j + 1], 1.0 / S, None, ALU.mult))
                for h in range(2):
                    lo = slice(S * h, S * h + S)
                    step(dve.tensor_scalar(W[r][lo, lo], W[r][lo, lo], mean[lo, j:j + 1], None, ALU.subtract))
            step(dve.tensor_tensor(tmp[:], W["ls"][:, 0:S], W["ad"][0:97, :], ALU.mult))
            step(dve.tensor_reduce(W["ls"][:, 128:136], tmp[:].rearrange("u (h k) -> u h k", h=HEADS), AX.X, ALU.add))
            step(dve.tensor_scalar(W["ls"][:, 128:136], W["ls"][:, 128:136], 0.2, None, ALU.mult))
            step(dve.tensor_scalar(W["ad"][:], W["ad"][:], 0.8, None, ALU.mult))
            step(dve.memset(W["one3"][:], 1.0))
            step(dve.memset(total[:], 0.0))
            for i in range(3):
                step(dve.tensor_copy(W["off3"][:], rest[:]))
                step(dve.tensor_copy(part[:], W["off3"][:]))
                step(dve.scalar_tensor_tensor(out=total[:], in0=part[:], scalar=k["ident"][0:3, i:i + 1], in1=total[:],
                                              op0=ALU.mult, op1=ALU.add))
                step(dve.tensor_tensor(rest[:], rest[:], part[:], ALU.subtract))
            step(dve.tensor_copy(W["off3"][:], total[:]))
            dve.wait_ge(turned, 1)
            step(dve.tensor_tensor(W["rb"][:, 0:6:3], W["rb"][:, 0:6:3], ps[:, 0, 0:6:3], ALU.subtract))

        @block.tensor
        def _(pe):
            pe.wait_ge(done, 2)
            pe.matmul(ps[:, 0, 0:6], W["avg"][:], W["rb"][:, 0:6], start=True, stop=True).then_inc(turned, 1)
            pe.wait_ge(turned, 1)


def directions(nc, m, k, W, a3, yx):
    own = ExitStack()
    with own:
        mm = Mem(nc, own)
        sq, tot = mm.sb("dir_sq", [R, 3, ET]), mm.sb("dir_tot", [R, 2, ET])
        tiny = mm.sb("dir_tiny", [R, 1])
        vec, root = mm.sem("dir_vec"), mm.sem("dir_root")
        with nc.Block() as block:
            @block.vector
            def _(dve):
                n = 0

                def step(ins):
                    nonlocal n
                    n += 1
                    ins.then_inc(vec, 1)
                    dve.wait_ge(vec, n)
                step(dve.memset(tiny[:], 1e-12))
                step(dve.tensor_tensor(sq[:], a3[:], a3[:], ALU.mult))
                step(dve.tensor_tensor(tot[:, 0, :], sq[:, 0, :], sq[:, 1, :], ALU.add))
                step(dve.tensor_tensor(tot[:, 0, :], tot[:, 0, :], sq[:, 2, :], ALU.add))
                dve.wait_ge(root, 1)
                step(dve.reciprocal(tot[:, 0, :], tot[:, 1, :]))
                for j in range(5):
                    step(dve.tensor_tensor(yx[:, j, :], a3[:, j % 3, :], tot[:, 0, :], ALU.mult))

            @block.scalar
            def _(act):
                act.wait_ge(vec, 4)
                act.activation(tot[:, 1, :], tot[:, 0, :], ACT.Sqrt, bias=tiny[:]).then_inc(root, 1)
                act.wait_ge(root, 1)


def layer1_edges(nc, m, k, ps, W, TS, TD, srcI, dstI, H, yx, a_sb, VAL):
    own = ExitStack()
    GP = ET // GT // 2
    with own:
        mm = Mem(nc, own)
        sb = mm.sb
        at = sb("e1_at", [R, 2, 2, GT], I32)
        rows = sb("e1_rows", [R, 2, 2, GT, X])
        hh = sb("e1_h", [128, 2, GT * R])
        m_ = sb("e1_m", [R, 2, GT, X])
        d1, d2 = sb("e1_d1", [R, GT, 97]), sb("e1_d2", [R, GT, S])
        d3, d5, dot = (sb("e1_" + n, [R, GT, 3, V]) for n in ("d3", "d5", "dot"))
        T = {n: sb("e1_T" + n, [r, GT * R]) for n, r in (("1", 97), ("2", S), ("3", V3), ("5", V3))}
        silu, asum = sb("e1_silu", [R, GT, S]), sb("e1_asum", [R, GT, HEADS])
        cA, cB, cC = (sb("e1_" + n, [R, GT, 3, V]) for n in ("cA", "cB", "cC"))
        val = sb("e1_val", [R, 2, GT, X])
        here = [[mm.sem(f"e1_here{p}{c}") for c in range(2 * GT)] for p in range(2)]
        at_ready = [mm.sem(f"e1_at_ready{p}") for p in range(2)]
        settle = [Settle(mm, k, f"e1_gather{p}") for p in range(2)]
        h_here = [mm.sem(f"e1_h_here{q}") for q in range(2)]
        stored = [mm.sem(f"e1_stored{p}") for p in range(2)]
        one = mm.sem("e1_one")
        added = [mm.sem(f"e1_added{p}") for p in range(2)]
        pe_s = [Steps(mm, k, f"e1_pe{p}", ["w", "t0", "t1", "t2", "ls", "lv"]) for p in range(2)]
        ac_s = [Steps(mm, k, f"e1_act{p}", ["t0", "t1", "t2", "t3", "silu", "vs"]) for p in range(2)]
        A_, B_ = 4, 8
        turned = [mm.sem(f"e1_turned{p}") for p in range(2)]
        sa, sc = [mm.sem(f"e1_front{p}") for p in range(2)], [mm.sem(f"e1_back{p}") for p in range(2)]

        def gather(pool, p, t):
            pool.wait_ge(added[p], t)
            for c in range(2 * GT):
                pool.wait_ge(here[p][c], 16 * t)
            settle[p](pool, 2 * t)
            pool.tensor_copy(at[:, p, 0, :], srcI[:, 0, bass.ds(8 * t + 4 * p, GT)])
            pool.tensor_copy(at[:, p, 1, :], dstI[:, 0, bass.ds(8 * t + 4 * p, GT)]).then_inc(at_ready[p], 1)
            pool.wait_ge(at_ready[p], t + 1)
            settle[p](pool, 2 * t + 1)
            for q, table in enumerate((TS, TD)):
                for c in range(GT):
                    pool.indirect_dma_start(rows[:, p, q, c, :], None, table, bass.IndirectOffsetOnAxis(
                        ap=at[:, p, q, c:c + 1], axis=0)).then_inc(here[p][GT * q + c], 16)

        def front(dve, p, t):
            v = Chain(dve, sa[p], A_, t)
            for c in range(2 * GT):
                dve.wait_ge(here[p][c], 16 * t + 16)
            dve.tensor_tensor(m_[:, p], rows[:, p, 0], rows[:, p, 1], ALU.add).then_inc(added[p], 1)
            dve.wait_ge(added[p], t + 1)
            s = m_[:, p, :, 0:S]
            vv = m_[:, p, :, S:X].rearrange("n c (i u) -> n c i u", i=3)
            yv = bc(yx[:, 0:3, bass.ds(8 * t + 4 * p, GT)].rearrange("n i c -> n c i"), V, 3)
            dve.wait_ge(turned[1 - p], t + p)
            v(dve.tensor_tensor(dot[:], vv, yv, ALU.mult))
            v.sync()
            v(dve.tensor_tensor(dot[:, :, 0, :], dot[:, :, 0, :], dot[:, :, 1, :], ALU.add))
            pe_s[p].wait(dve, t, "w")
            w = [ps[0:R, b, 0:448].rearrange("n (c w) -> n c w", c=2) for b in range(2)]
            cc = [slice(0, 2), slice(2, 4)]
            for b in range(2):
                dve.tensor_tensor(d1[:, cc[b], 0:S], w[b][:, :, 0:S], s[:, cc[b], :], ALU.mult)
                dve.tensor_tensor(d2[:, cc[b], :], w[b][:, :, S:2 * S], s[:, cc[b], :], ALU.mult)
            v.sync()
            v(dve.tensor_tensor(dot[:, :, 0, :], dot[:, :, 0, :], dot[:, :, 2, :], ALU.add))
            for b in range(2):
                dve.tensor_tensor(d3[:, cc[b]], bc(w[b][:, :, 128:160], 3, 2), vv[:, cc[b]], ALU.mult)
                dve.tensor_tensor(d5[:, cc[b]], bc(w[b][:, :, 192:224], 3, 2), vv[:, cc[b]], ALU.mult)
            v.sync()
            for b in range(2):
                last = dve.tensor_tensor(d1[:, cc[b], S:S + V], w[b][:, :, 160:192], dot[:, cc[b], 0, :], ALU.mult)
            v(last)
            v.end()

        def back(dve, p, t):
            v = Chain(dve, sc[p], B_, t)
            ac_s[p].wait(dve, t, "silu")
            v(dve.tensor_tensor(silu[:], silu[:], bc(W["ad"][0:R, :], GT, 1), ALU.mult))
            v.sync()
            v(dve.tensor_reduce(asum[:], silu[:].rearrange("n c (h k) -> n c h k", h=HEADS), AX.X, ALU.add))
            y = [bc(yx[:, j:j + 3, bass.ds(8 * t + 4 * p, GT)].rearrange("n i c -> n c i"), V, 3) for j in range(3)]
            pe_s[p].wait(dve, t, "lv")
            v.sync()
            v(dve.tensor_tensor(a_sb[:, bass.ds(8 * t + 4 * p, GT), :], asum[:],
                                ps[0:R, 7, 0:GT * HEADS].rearrange("n (c h) -> n c h", c=GT), ALU.add))
            lv = [ps[0:R, 5 + b, :].rearrange("n (c w) -> n c w", c=2) for b in range(2)]
            for b in range(2):
                cc = slice(2 * b, 2 * b + 2)
                part = lambda lo: lv[b][:, :, lo:lo + V3].rearrange("n c (i u) -> n c i u", i=3)
                dve.tensor_tensor(cC[:, cc], bc(lv[b][:, :, 0:V], 3, 2), y[0][:, cc], ALU.mult)
                dve.tensor_tensor(cA[:, cc], part(128), y[2][:, cc], ALU.mult)
                last = dve.tensor_tensor(cB[:, cc], part(160), y[1][:, cc], ALU.mult)
            v(last)
            v.sync()
            for b in range(2):
                cc = slice(2 * b, 2 * b + 2)
                part = lambda lo: lv[b][:, :, lo:lo + V3].rearrange("n c (i u) -> n c i u", i=3)
                v(dve.tensor_tensor(cC[:, cc], part(V), cC[:, cc], ALU.add))
            v(dve.tensor_tensor(cA[:], cA[:], cB[:], ALU.subtract))
            v.sync()
            dve.wait_ge(stored[p], 16 * t)
            ac_s[p].wait(dve, t, "vs")
            v(dve.tensor_tensor(val[:, p, :, S:X].rearrange("n c (i u) -> n c i u", i=3), cA[:], cC[:], ALU.add))
            v.end()

        with nc.Block() as block:
            @block.sync
            def _(sp):
                def load(q, t):
                    gate(sp, k)
                    sp.dma_start(hh[:, q, :], H[bass.ds(t, 1)].rearrange("g q n -> (g q) n")).then_inc(h_here[q], 16)
                load(0, 0)
                load(1, 1)

                def store(t):
                    for p in range(2):
                        gate(sp, k)
                        sp.wait_ge(sc[p], B_ * t + B_)
                        sp.dma_start(VAL[bass.ds(2 * t + p, 1)].rearrange("g r w -> (g r) w"),
                                     val[:, p].rearrange("r c w -> r (c w)")).then_inc(stored[p], 16)

                with sp.Fori(0, GP // 2 - 1) as t2:
                    for q in range(2):
                        store(2 * t2 + q)
                        load(q, 2 * t2 + q + 2)
                for q in range(2):
                    store(GP - 2 + q)
                for p in range(2):
                    sp.wait_ge(stored[p], 16 * GP)

            @block.gpsimd
            def _(pool):
                gather(pool, 0, 0)
                gather(pool, 1, 0)
                with pool.Fori(0, GP - 1) as t:
                    for p in range(2):
                        gather(pool, p, t + 1)

            @block.vector
            def _(dve):
                for c in range(GT):
                    last = dve.tensor_copy(d1[:, c, 96:97], k["ones"][0:R, 0:1])
                last.then_inc(one, 1)
                dve.wait_ge(one, 1)
                front(dve, 0, 0)
                with dve.Fori(0, GP - 1) as t:
                    front(dve, 1, t)
                    back(dve, 0, t)
                    front(dve, 0, t + 1)
                    back(dve, 1, t)
                front(dve, 1, GP - 1)
                back(dve, 0, GP - 1)
                back(dve, 1, GP - 1)

            @block.tensor
            def _(pe):
                I = k["ident"]

                def weights(p, t, q, t2):
                    if p == 0:
                        pe.wait_ge(h_here[q], 16 * t2 + 16)
                        pe.wait_ge(sa[1], A_ * t)
                    else:
                        pe.wait_ge(sa[0], A_ * t + A_)
                    for c in range(GT):
                        to = ps[0:R, c // 2, 224 * (c % 2):224 * (c % 2) + 224]
                        pe.matmul(to, hh[S * p:S * p + S, q, R * c:R * c + R], W["r3"][S * p:S * p + S, :],
                                  start=True, stop=False)
                        last = pe.matmul(to, W["one3"][:], W["off3"][:], start=False, stop=True)
                    pe_s[p].done(last, "w")

                def maps(p, t):
                    pe.wait_ge(sa[p], A_ * t + A_)
                    for j, d in enumerate((d1, d2, d3, d5)):
                        if j >= 2:
                            ac_s[p].wait(pe, t, f"t{j - 2}")
                        for c in range(GT):
                            src = d[:, c].rearrange("n i u -> n (i u)") if j > 1 else d[:, c, :]
                            wide = src.shape[1]
                            last = pe.transpose(ps[0:wide, 2 + j % 2, R * c:R * c + R], src, I[0:R, 0:R])
                        if j < 3:
                            pe_s[p].done(last, f"t{j}")
                        else:
                            last.then_inc(turned[p], 1)
                    ac_s[p].wait(pe, t, "t3")
                    if p == 0:
                        pe.wait_ge(sc[1], B_ * t)
                        pe.wait_ge(ac_s[1].sem, 6 * t)
                    else:
                        pe.wait_ge(sc[0], B_ * t + B_)
                        pe.wait_ge(ac_s[0].sem, 6 * t + 6)
                    for c in range(GT):
                        e = slice(R * c, R * c + R)
                        last = pe.matmul(ps[0:R, 4, 128 * c:128 * c + 128], T["1"][:, e], W["ls"][:, 0:128],
                                         start=True, stop=True)
                    pe_s[p].done(last, "ls")
                    for c in range(GT):
                        e = slice(R * c, R * c + R)
                        lv = ps[0:R, 5 + c // 2, 256 * (c % 2):256 * (c % 2) + 256]
                        pe.matmul(ps[0:R, 7, HEADS * c:HEADS * c + HEADS], T["1"][:, e], W["ls"][:, 128:136],
                                  start=True, stop=True)
                        pe.matmul(lv[:, 0:V], T["2"][:, e], W["la"][:], start=True, stop=True)
                        pe.matmul(lv[:, V:128], T["3"][:, e], W["lb"][:], start=True, stop=True)
                        last = pe.matmul(lv[:, 128:256], T["5"][:, e], W["lc"][:], start=True, stop=True)
                    pe_s[p].done(last, "lv")

                weights(0, 0, 0, 0)
                with pe.Fori(0, GP // 2 - 1) as t2:
                    for q in range(2):
                        weights(1, 2 * t2 + q, q, t2)
                        maps(0, 2 * t2 + q)
                        weights(0, 2 * t2 + q + 1, 1 - q, t2 + q)
                        maps(1, 2 * t2 + q)
                t2 = GP // 2 - 1
                for q in range(2):
                    weights(1, 2 * t2 + q, q, t2)
                    maps(0, 2 * t2 + q)
                    if q == 0:
                        weights(0, 2 * t2 + 1, 1, t2)
                    maps(1, 2 * t2 + q)

            @block.scalar
            def _(act):
                with act.Fori(0, GP) as t:
                    for p in range(2):
                        for j, n in enumerate("1235"):
                            if j < 3:
                                pe_s[p].wait(act, t, f"t{j}")
                            else:
                                act.wait_ge(turned[p], t + 1)
                            ac_s[p].done(act.activation(T[n][:], ps[0:T[n].shape[0], 2 + j % 2, 0:GT * R], ACT.Copy),
                                         f"t{j}")
                        pe_s[p].wait(act, t, "ls")
                        ls = ps[0:R, 4, :].rearrange("n (c w) -> n c w", c=GT)
                        if p == 0:
                            act.wait_ge(sc[1], B_ * t)
                        else:
                            act.wait_ge(sc[0], B_ * t + B_)
                        ac_s[p].done(act.activation(silu[:], ls[:, :, 0:S], ACT.Silu), "silu")
                        act.wait_ge(stored[p], 16 * t)
                        ac_s[p].done(act.activation(val[:, p, :, 0:S], ls[:, :, S:128], ACT.Copy), "vs")


def softmax_weights(nc, m, k, ps, a_sb, dst, scratch):
    own = ExitStack()
    TC = ET // CH
    NB = TC // GT
    HP = HEADS * CH
    with own:
        mm = Mem(nc, own)
        sb = mm.sb
        aT = sb("sm_aT", [HP, EC])
        d = sb("sm_dst", [HP, EC], I32)
        mask = d[:].bitcast(F32)
        stage = sb("sm_stage", [R, 2, GT, HP])
        penalty = sb("sm_penalty", [HP, 2, 1250])
        ends = sb("sm_ends", [HP, 4])
        flags = sb("sm_flags", [HEADS, 8, CH])
        marks = sb("sm_marks", [HEADS, 2, CH], I32)
        vec, turned, kept = mm.sem("sm_vec"), mm.sem("sm_turned"), mm.sem("sm_kept")
        here, moved, back, done = mm.sem("sm_here"), mm.sem("sm_moved"), mm.sem("sm_back"), mm.sem("sm_done")
        again = mm.sem("sm_again")
        chunk = dst.rearrange("(c n) -> c n", c=CH)

        def load_dst(sp, sem):
            for c in range(CH):
                sp.dma_start(d[HEADS * c:HEADS * c + HEADS, :], chunk[c:c + 1, :].broadcast_to([HEADS, EC])
                             ).then_inc(sem, 16)

        with nc.Block() as block:
            @block.sync
            def _(sp):
                load_dst(sp, here)
                for j, at in enumerate((0, EC - 1)):
                    sp.dma_start(marks[:, j, :], chunk[:, at:at + 1].rearrange("c n -> n c").broadcast_to([HEADS, CH]),
                                 allow_slow_non_contiguous=True).then_inc(here, 16)
                sp.wait_ge(here, 16 * (CH + 2))

            @block.vector
            def _(dve):
                v4 = a_sb[:].rearrange("r (c j) h -> r j c h", c=CH)
                for b in range(NB):
                    if b >= 2:
                        dve.wait_ge(turned, b - 1)
                    dve.tensor_copy(stage[:, b % 2].rearrange("r j (c h) -> r j c h", c=CH),
                                    v4[:, GT * b:GT * b + GT]).then_inc(vec, 1)
                dve.wait_ge(vec, NB)

            @block.tensor
            def _(pe):
                for b in range(NB):
                    pe.wait_ge(vec, b + 1)
                    if b >= 2:
                        pe.wait_ge(kept, b - 1)
                    for j in range(GT):
                        last = pe.transpose(ps[:, b % 2, R * j:R * j + R], stage[:, b % 2, j, :],
                                            k["ident"][0:R, 0:R])
                    last.then_inc(turned, 1)

            @block.scalar
            def _(act):
                for b in range(NB):
                    act.wait_ge(turned, b + 1)
                    act.activation(aT[:, GT * R * b:GT * R * b + GT * R], ps[:, b % 2, 0:GT * R], ACT.Copy
                                   ).then_inc(kept, 1)
                act.wait_ge(kept, NB)

        with nc.Block() as block:
            @block.vector
            def _(dve):
                n = NB

                def step(ins):
                    nonlocal n
                    n += 1
                    ins.then_inc(vec, 1)
                    dve.wait_ge(vec, n)
                step(dve.tensor_copy(ends[:, 0:1], d[:, 0:1]))
                step(dve.tensor_copy(ends[:, 1:2], d[:, EC - 1:EC]))
                step(dve.tensor_tensor(mask[:, 0:EC - 1], d[:, 0:EC - 1], d[:, 1:EC], ALU.not_equal))
                step(dve.tensor_scalar(mask[:, 0:EC - 1], mask[:, 0:EC - 1], -BIG, None, ALU.mult))
                step(dve.tensor_tensor_scan(aT[:, 1:EC], mask[:, 0:EC - 1], aT[:, 1:EC], aT[:, 0:1], ALU.add, ALU.max))
                step(dve.tensor_tensor_scan(aT[:, EC - 2::-1], mask[:, EC - 2::-1], aT[:, EC - 2::-1],
                                            aT[:, EC - 1:EC], ALU.add, ALU.max))
                step(dve.tensor_copy(ends[:, 2:3], aT[:, 0:1]))
                step(dve.tensor_copy(ends[:, 3:4], aT[:, EC - 1:EC]))
                dve.wait_ge(moved, 64)
                f = [flags[:, j, :] for j in range(8)]
                step(dve.memset(flags[:, 2:8, :], -BIG))
                step(dve.tensor_tensor(f[2][:, 1:CH], marks[:, 1, 0:CH - 1], marks[:, 0, 1:CH], ALU.not_equal))
                step(dve.tensor_scalar(f[2][:, 1:CH], f[2][:, 1:CH], -BIG, None, ALU.mult))
                step(dve.tensor_tensor(f[3], marks[:, 0, :], marks[:, 1, :], ALU.not_equal))
                step(dve.tensor_scalar(f[3], f[3], -BIG, None, ALU.mult))
                step(dve.tensor_tensor(f[6], f[2], f[3], ALU.add))
                step(dve.tensor_tensor_scan(f[4], f[6], f[1], -BIG, ALU.add, ALU.max))
                step(dve.tensor_tensor(f[7][:, 0:CH - 1], f[2][:, 1:CH], f[3][:, 0:CH - 1], ALU.add))
                step(dve.tensor_tensor_scan(f[5][:, ::-1], f[7][:, ::-1], f[0][:, ::-1], -BIG, ALU.add, ALU.max))
                step(dve.memset(flags[:, 6:8, :], -BIG))
                step(dve.tensor_tensor(f[6][:, 1:CH], f[4][:, 0:CH - 1], f[2][:, 1:CH], ALU.add))
                step(dve.tensor_tensor(f[7][:, 0:CH - 1], f[5][:, 1:CH], f[2][:, 1:CH], ALU.add))
                dve.wait_ge(back, 32)
                dve.wait_ge(again, 16 * CH)

            @block.sync
            def _(sp):
                sp.wait_ge(vec, NB + 8)
                for j in range(2):
                    sp.dma_start(scratch[j:j + 1, :].rearrange("a q -> q a"), ends[:, 2 + j:3 + j],
                                 allow_slow_non_contiguous=True).then_inc(moved, 16)
                sp.wait_ge(moved, 32)
                for j in range(2):
                    sp.dma_start(flags[:, j, :], scratch[j].rearrange("(c h) -> h c", c=CH),
                                 allow_slow_non_contiguous=True).then_inc(moved, 16)
                sp.wait_ge(moved, 64)
                load_dst(sp, again)
                sp.wait_ge(vec, NB + 20)
                for j in range(2):
                    sp.dma_start(scratch[2 + j].rearrange("(c h) -> h c", c=CH), flags[:, 6 + j, :],
                                 allow_slow_non_contiguous=True).then_inc(moved, 16)
                sp.wait_ge(moved, 96)
                for j in range(2):
                    sp.dma_start(ends[:, 2 + j:3 + j], scratch[2 + j:3 + j, :].rearrange("a q -> q a"),
                                 allow_slow_non_contiguous=True).then_inc(back, 16)
                sp.wait_ge(back, 32)

        with nc.Block() as block:
            @block.vector
            def _(dve):
                n = 0

                def step(ins):
                    nonlocal n
                    n += 1
                    ins.then_inc(done, 1)
                    dve.wait_ge(done, n)
                W_ = 1250
                for a in range(0, EC, W_):
                    for j in range(2):
                        p = penalty[:, j, :]
                        step(dve.tensor_scalar(p, d[:, a:a + W_], ends[:, j:j + 1], -BIG, ALU.not_equal, ALU.mult))
                        step(dve.scalar_tensor_tensor(out=aT[:, a:a + W_], in0=p, scalar=ends[:, 2 + j:3 + j],
                                                      in1=aT[:, a:a + W_], op0=ALU.add, op1=ALU.max))
                v4 = a_sb[:].rearrange("r (c j) h -> r j c h", c=CH)
                base = n
                for b in range(NB):
                    dve.wait_ge(turned, NB + b + 1)
                    dve.tensor_tensor(v4[:, GT * b:GT * b + GT], v4[:, GT * b:GT * b + GT],
                                      ps[0:R, b % 2, :].rearrange("r (j c h) -> r j c h", j=GT, c=CH), ALU.subtract
                                      ).then_inc(done, 1)
                dve.wait_ge(done, base + NB)

            @block.tensor
            def _(pe):
                fixed = 4 * (EC // 1250)
                for b in range(NB):
                    pe.wait_ge(done, fixed + max(b - 1, 0))
                    for j in range(GT):
                        at = GT * R * b + R * j
                        last = pe.transpose(ps[0:R, b % 2, HP * j:HP * j + HP], aT[:, at:at + R], k["ident"][:, :])
                    last.then_inc(turned, 1)

            @block.scalar
            def _(act):
                fixed = 4 * (EC // 1250)
                act.wait_ge(done, fixed + NB)
                per = ET // 4
                for q in range(4):
                    w = a_sb[:, per * q:per * q + per, :].rearrange("r t h -> r (t h)")
                    act.activation(w, w, ACT.Exp).then_inc(kept, 1)
                act.wait_ge(kept, NB + 4)


def layer1_sums(nc, m, k, ps, a_sb, dstF, dst, VAL, sums):
    own = ExitStack()
    with own:
        mm = Mem(nc, own)
        sc = Scatter(nc, mm, k, ps, "e2", MSG1, dstF, dst, sums, 0)
        val = mm.sb("e2_val", [R, 2, GT * X])
        here = [mm.sem(f"e2_here{p}") for p in range(2)]
        GP = ET // GT // 2

        def load(sp, p, t):
            gate(sp, k)
            sp.wait_ge(sc.u_ready[p], t)
            sp.dma_start(val[:, p, :], VAL[bass.ds(2 * t + p, 1)].rearrange("g r w -> (g r) w")
                         ).then_inc(here[p], 16)

        def messages(dve, p, t):
            sc.equal(dve, p, t)
            gate(dve, k)
            dve.wait_ge(here[p], 16 * t + 16)
            u, v = sc.u[:, p], val[:, p, :].rearrange("r (c w) -> r c w", c=GT)
            e = a_sb[:, bass.ds(8 * t + 4 * p, GT), :]
            for lo, per in ((0, 8), (S, 4), (S + V, 4), (S + 2 * V, 4)):
                at = slice(lo, lo + HEADS * per)
                dve.tensor_tensor(u[:, :, at].rearrange("r c (h q) -> r c h q", h=HEADS),
                                  v[:, :, at].rearrange("r c (h q) -> r c h q", h=HEADS), bc(e, per, 3), ALU.mult)
            dve.tensor_scalar(u[:, :, X:MSG1], e, 1.0, None, ALU.mult).then_inc(sc.u_ready[p], 1)

        run_edges(nc, sc, messages, GP, load)


PER2 = 29


def weights3(nc, m, k, w, W):
    for n, shape in dict(pws=[S, S], pwv=[V3, V3], f1s=[S, 192], f1v=[V3, 192], f2s=[128, S], f2a=[128, S],
                         f2b=[S, V]).items():
        W[n] = m.sb("w_" + n, shape)
    loads = [(W["pws"], W["pws"][:], w["proj_ws"]), (W["f1s"], W["f1s"][:], w["f1_ws"]),
             (W["f2s"], W["f2s"][:], w["f2_ws"]), (W["f2b"], W["f2b"][:], w["f2_wv"])]
    loads += diagonal(W["pwv"], 0, w["proj_wv"])
    loads += [(W["f1v"], W["f1v"][V * i:V * i + V, S * i:S * i + S], w["f1_wv"]) for i in range(3)]
    loads += [(W["f2a"], W["f2a"][S * i:S * i + S, V * i:V * i + V], w["f2_wv"]) for i in range(2)]
    load_weights(nc, m, k, "w3", loads)


def node_update1(nc, m, k, ps, W, X1, nodevec, sums, out):
    own = ExitStack()
    with own:
        mm = Mem(nc, own)
        sb = mm.sb
        xt, ag, nv = sb("n2_x", [R, 2, X]), sb("n2_ag", [R, 2, COPIES, MSG1]), sb("n2_nv", [R, 2, 2])
        a, rec = sb("n2_a", [R, MSG1]), sb("n2_rec", [R, HEADS])
        x2, sq, norm = sb("n2_x2", [R, X]), sb("n2_sq", [R, V3]), sb("n2_norm", [R, X])
        stat, st2 = sb("n2_stat", [R, 2, 6]), sb("n2_st2", [R, 16])
        sT, vT, sT2, vT2 = sb("n2_sT", [S, R]), sb("n2_vT", [V3, R]), sb("n2_sT2", [S, R]), sb("n2_vT2", [V3, R])
        sc, sg, fv = sb("n2_sc", [R, 128]), sb("n2_sg", [R, S]), sb("n2_fv", [R, 192])
        scT, fvT, fwT = sb("n2_scT", [128, R]), sb("n2_fvT", [128, R]), sb("n2_fwT", [S, R])
        y, y2 = sb("n2_y", [R, X]), sb("n2_y2", [R, 2, X])
        here = [mm.sem(f"n2_here{p}") for p in range(2)]
        stored = [mm.sem(f"n2_stored{p}") for p in range(2)]
        vec, marks = mm.sem("n2_vec"), {}
        pe_s = Steps(mm, k, "n2_pe", ["turned", "proj", "norm", "f1", "mid", "f2"])
        ac_s = Steps(mm, k, "n2_act", ["turned", "root1", "norm", "gates", "mid", "root2"])

        def got(eng, t, name):
            marked(eng, k, vec, PER2, marks, t, name)

        with nc.Block() as block:
            @block.vector
            def _(dve):
                with dve.Fori(0, NT // 2) as tt:
                    for p in range(2):
                        t = 2 * tt + p
                        v = Vector(k, vec, PER2, marks, t)
                        v.eng = dve
                        gate(dve, k)
                        dve.wait_ge(here[p], 96 * tt + 96)
                        v(dve.tensor_tensor(a[:], ag[:, p, 0, :], ag[:, p, 1, :], ALU.add))
                        for c in (2, 3):
                            v.sync()
                            v(dve.tensor_tensor(a[:], a[:], ag[:, p, c, :], ALU.add))
                        v(dve.tensor_scalar(nv[:, p, 1:2], nv[:, p, 0:1], 0.5, None, ALU.mult))
                        v.sync()
                        v(dve.tensor_scalar(rec[:], a[:, X:MSG1], 1e-12, None, ALU.add))
                        v.sync()
                        v(dve.reciprocal(rec[:], rec[:]))
                        v.sync()
                        v(dve.tensor_tensor(a[:, 0:S].rearrange("n (h q) -> n h q", h=HEADS),
                                            a[:, 0:S].rearrange("n (h q) -> n h q", h=HEADS), bc(rec[:], 8, 2), ALU.mult))
                        for i in range(3):
                            at = a[:, S + V * i:S + V * i + V].rearrange("n (h q) -> n h q", h=HEADS)
                            v(dve.tensor_tensor(at, at, bc(rec[:], 4, 2), ALU.mult))
                        v.mark("weighted")
                        pe_s.wait(dve, t, "proj")
                        v(dve.tensor_tensor(x2[:], xt[:, p, :], ps[0:R, 1, 0:X], ALU.add))
                        v.sync()
                        v(dve.tensor_tensor(sq[:], x2[:, S:X], x2[:, S:X], ALU.mult))
                        v(dve.bn_stats(stat[:, 0, :], x2[:, 0:S]))
                        v.sync()
                        v(dve.tensor_reduce(st2[:, 2:3], sq[:], AX.X, ALU.add))
                        v(dve.bn_aggr(st2[:, 0:2], stat[:, 0, :]))
                        v.sync()
                        v(dve.tensor_scalar(st2[:, 2:3], st2[:, 2:3], 1.0 / V3, None, ALU.mult))
                        v.mark("var1")
                        v(dve.tensor_tensor(y[:], xt[:, p, :], x2[:], ALU.add))
                        ac_s.wait(dve, t, "root1")
                        v(dve.reciprocal(st2[:, 6:8], st2[:, 4:6]))
                        v.sync()
                        v(dve.tensor_scalar(norm[:, 0:S], x2[:, 0:S], st2[:, 0:1], st2[:, 6:7], ALU.subtract, ALU.mult))
                        v(dve.tensor_scalar(norm[:, S:X], x2[:, S:X], st2[:, 7:8], None, ALU.mult))
                        v.mark("norm")
                        ac_s.wait(dve, t, "gates")
                        v(dve.tensor_scalar(sg[:], sg[:], 1.0, nv[:, p, 1:2], ALU.add, ALU.mult))
                        v.sync()
                        v(dve.tensor_tensor(fv[:].rearrange("n (i u) -> n i u", i=3),
                                            ps[0:R, 3, 0:192].rearrange("n (i u) -> n i u", i=3), bc(sg[:], 3, 1),
                                            ALU.mult))
                        v.mark("gated")
                        pe_s.wait(dve, t, "f2")
                        v(dve.scalar_tensor_tensor(out=y[:], in0=ps[0:R, 5, 0:X], scalar=nv[:, p, 0:1], in1=y[:],
                                                   op0=ALU.mult, op1=ALU.add))
                        v.sync()
                        v(dve.bn_stats(stat[:, 1, :], y[:]))
                        v.sync()
                        v(dve.memset(st2[:, 14:15], 0.0))
                        v(dve.bn_aggr(st2[:, 8:10], stat[:, 1, :]))
                        v.mark("var2")
                        ac_s.wait(dve, t, "root2")
                        v(dve.reciprocal(st2[:, 11:12], st2[:, 10:11]))
                        v.sync()
                        gate(dve, k)
                        dve.wait_ge(stored[p], 16 * tt)
                        v(dve.tensor_scalar(y2[:, p, 0:S], y[:, 0:S], st2[:, 8:9], st2[:, 11:12], ALU.subtract, ALU.mult))
                        v(dve.tensor_scalar(y2[:, p, S:X].rearrange("n (u i) -> n i u", i=3),
                                            y[:, S:X].rearrange("n (i u) -> n i u", i=3), st2[:, 8:9], st2[:, 11:12],
                                            ALU.subtract, ALU.mult))
                        v.mark("out")
                        v.sync()
                        v.end()

            @block.sync
            def _(sp):
                with sp.Fori(0, NT // 2) as tt:
                    for p in range(2):
                        t = 2 * tt + p
                        rows = bass.ds(t * R, R)
                        gate(sp, k)
                        sp.wait_ge(vec, PER2 * 2 * tt)
                        sp.dma_start(xt[:, p, :], X1[rows, :]).then_inc(here[p], 16)
                        sp.dma_start(nv[:, p, 0:1], nodevec[rows, :]).then_inc(here[p], 16)
                        for c in range(COPIES):
                            sp.dma_start(ag[:, p, c, :], sums[c][rows, :]).then_inc(here[p], 16)
                    for p in range(2):
                        t = 2 * tt + p
                        got(sp, t, "out")
                        sp.dma_start(out[bass.ds(t * R, R), :], y2[:, p, :]).then_inc(stored[p], 16)
                for p in range(2):
                    sp.wait_ge(stored[p], 16 * (NT // 2))

            @block.tensor
            def _(pe):
                I = k["ident"]
                one = k["ones"][0:1, 0:R]

                def bias(n, lo=0, hi=None):
                    a0, b0 = W["row_at"][n]
                    return W["rows"][0:1, a0:b0]

                with pe.Fori(0, NT // 2) as tt:
                    for p in range(2):
                        t = 2 * tt + p
                        got(pe, t, "weighted")
                        pe.transpose(ps[0:V3, 0, 128:128 + R], a[:, S:X], I[0:R, 0:R])
                        pe_s.done(pe.transpose(ps[0:S, 0, 0:R], a[:, 0:S], I[0:R, 0:R]), "turned")
                        ac_s.wait(pe, t, "turned")
                        pe.matmul(ps[0:R, 1, 0:S], sT[:], W["pws"][:], start=True, stop=False)
                        pe.matmul(ps[0:R, 1, 0:S], one, bias("proj_bs"), start=False, stop=True)
                        pe_s.done(pe.matmul(ps[0:R, 1, S:X], vT[:], W["pwv"][:], start=True, stop=True), "proj")
                        got(pe, t, "norm")
                        pe.transpose(ps[0:V3, 0, 128:128 + R], norm[:, S:X], I[0:R, 0:R])
                        pe_s.done(pe.transpose(ps[0:S, 0, 0:R], norm[:, 0:S], I[0:R, 0:R]), "norm")
                        ac_s.wait(pe, t, "norm")
                        pe.matmul(ps[0:R, 2, 0:192], sT2[:], W["f1s"][:], start=True, stop=False)
                        pe.matmul(ps[0:R, 2, 0:192], one, bias("f1_bs"), start=False, stop=True)
                        pe_s.done(pe.matmul(ps[0:R, 3, 0:192], vT2[:], W["f1v"][:], start=True, stop=True), "f1")
                        got(pe, t, "gated")
                        pe.transpose(ps[:, 4, 0:R], sc[:], I[0:R, 0:R])
                        pe.transpose(ps[:, 4, 128:128 + R], fv[:, 0:128], I[0:R, 0:R])
                        pe_s.done(pe.transpose(ps[0:S, 4, 256:256 + R], fv[:, 128:192], I[0:R, 0:R]), "mid")
                        ac_s.wait(pe, t, "mid")
                        pe.matmul(ps[0:R, 5, 0:S], scT[:], W["f2s"][:], start=True, stop=False)
                        pe.matmul(ps[0:R, 5, 0:S], one, bias("f2_bs"), start=False, stop=True)
                        pe.matmul(ps[0:R, 5, S:S + 2 * V], fvT[:], W["f2a"][:], start=True, stop=True)
                        pe_s.done(pe.matmul(ps[0:R, 5, S + 2 * V:X], fwT[:], W["f2b"][:], start=True, stop=True), "f2")

            @block.scalar
            def _(act):
                with act.Fori(0, NT // 2) as tt:
                    for p in range(2):
                        t = 2 * tt + p
                        pe_s.wait(act, t, "turned")
                        act.activation(sT[:], ps[0:S, 0, 0:R], ACT.Copy)
                        ac_s.done(act.activation(vT[:], ps[0:V3, 0, 128:128 + R], ACT.Copy), "turned")
                        got(act, t, "var1")
                        ac_s.done(act.activation(st2[:, 4:6], st2[:, 1:3], ACT.Sqrt, bias=W["eps"][0:R, :]), "root1")
                        pe_s.wait(act, t, "norm")
                        act.activation(sT2[:], ps[0:S, 0, 0:R], ACT.Identity, bias=W["ln2"][0:S, 1:2],
                                       scale=W["ln2"][0:S, 0:1])
                        ac_s.done(act.activation(vT2[:], ps[0:V3, 0, 128:128 + R], ACT.Copy,
                                                 scale=W["ln2"][0:V3, 2:3]), "norm")
                        pe_s.wait(act, t, "f1")
                        act.activation(sc[:], ps[0:R, 2, 0:128], ACT.Silu, scale=nv[:, p, 0:1])
                        ac_s.done(act.activation(sg[:], ps[0:R, 2, 128:192], ACT.Tanh, scale=nv[:, p, 1:2]), "gates")
                        pe_s.wait(act, t, "mid")
                        act.activation(scT[:], ps[:, 4, 0:R], ACT.Copy)
                        act.activation(fvT[:], ps[:, 4, 128:128 + R], ACT.Copy)
                        ac_s.done(act.activation(fwT[:], ps[0:S, 4, 256:256 + R], ACT.Copy), "mid")
                        got(act, t, "var2")
                        ac_s.done(act.activation(st2[:, 10:11], st2[:, 9:10], ACT.Sqrt, bias=W["eps"][0:R, :]), "root2")


WEIGHTS0 = ["Wm_ss", "Wm_vv", "Wm_sv", "Wm_vs", "Lm_s", "Lm_v", "Wu_ss", "Wu_vv", "Wu_sv", "Wu_vs", "Lu_s", "Lu_v"]
WEIGHTS1 = ["ln1_w0", "ln1_b0", "ln1_w1", "ln2_w0", "ln2_b0", "ln2_w1", "msrc_ws", "msrc_wv", "mdst_ws", "mdst_bs",
            "mdst_wv", "rw1", "rb1", "rg1", "rbe1", "rw2", "rb2", "rg2", "rbe2", "rw3", "roff", "lin_ws", "lin_bs",
            "lin_wv", "alpha_dot", "proj_ws", "proj_bs", "proj_wv", "f1_ws", "f1_bs", "f1_wv", "f2_ws", "f2_bs",
            "f2_wv"]
ROWS = 12672


def program(nc, x, src, dst, ea3, ea4, ea64, nodevec, ranks, w, out):
    def table(name, *shape):
        return nc.dram_tensor(name, shape, F32, kind="Internal").ap()

    with ExitStack() as ctx:
        m = Mem(nc, ctx)
        ps = ctx.enter_context(nc.psum_tensor("ps", [128, 8, 512], F32))
        k = constants(nc, m, ranks)
        T0 = table("T0", N, 448)
        sums0 = [table(f"sums0_{c}", ROWS, MSG0) for c in range(COPIES)]
        sums1 = [table(f"sums1_{c}", ROWS, MSG1) for c in range(COPIES)]
        X1, TS, TD = (table(n, N, X) for n in ("X1", "TS", "TD"))
        H = table("H", ET // (2 * GT), 128, GT * R)
        VAL = table("VAL", ET // GT, R, GT * X)
        scratch = table("scratch", 4, HEADS * CH)
        for c in range(COPIES):
            clear(nc, m, k, f"clear0_{c}", sums0[c].rearrange("(a r) w -> a r w", a=1))
            clear(nc, m, k, f"clear1_{c}", sums1[c].rearrange("(a r) w -> a r w", a=1))
        src1, dst1 = (v.rearrange("(n a) -> n a", a=1) for v in (src, dst))
        dstI = m.sb("dstI", [R, 1, ET], I32)
        edge_rows(nc, m, k, ps, "dst", dst1, 1, I32, None, dstI)
        W = {n: m.sb("w_" + n, shape) for n, shape in dict(rows=[1, 1024], ln1=[V3, 3], ln2=[V3, 3],
                                                           eps=[128, 1]).items()}
        weights2(nc, m, k, ps, w, W)
        with ExitStack() as c0:
            m0 = Mem(nc, c0)
            W.update(weights0(nc, m0, k, w))
            weights1(nc, m0, k, w, W)
            layer0_tables(nc, m0, k, ps, x, W, T0)
            with ExitStack() as c1:
                m1 = Mem(nc, c1)
                srcF, attr = m1.sb("srcF", [R, 1, ET]), m1.sb("attr", [R, 4, ET])
                edge_rows(nc, m1, k, ps, "src", src1, 1, I32, srcF, None)
                edge_rows(nc, m1, k, ps, "ea4", ea4, 4, F32, attr, None)
                layer0_edges(nc, m1, k, ps, W, T0, dstI, srcF, src, attr, sums0, ea64, H)
            node_update0(nc, m0, k, ps, W, x, sums0, X1, TS, TD)
        with ExitStack() as c0:
            m0 = Mem(nc, c0)
            a_sb = m0.sb("logits", [R, ET, HEADS])
            with ExitStack() as c1:
                m1 = Mem(nc, c1)
                srcI, yx = m1.sb("srcI", [R, 1, ET], I32), m1.sb("yx", [R, 5, ET])
                edge_rows(nc, m1, k, ps, "src_again", src1, 1, I32, None, srcI)
                with ExitStack() as c2:
                    m2 = Mem(nc, c2)
                    a3 = m2.sb("a3", [R, 3, ET])
                    edge_rows(nc, m2, k, ps, "ea3", ea3, 3, F32, a3, None)
                    directions(nc, m2, k, W, a3, yx)
                layer1_edges(nc, m1, k, ps, W, TS, TD, srcI, dstI, H, yx, a_sb, VAL)
            softmax_weights(nc, m0, k, ps, a_sb, dst, scratch)
            dstF = m0.sb("dstF", [R, 1, ET])
            edge_rows(nc, m0, k, ps, "dst_again", dst1, 1, I32, dstF, None)
            layer1_sums(nc, m0, k, ps, a_sb, dstF, dst, VAL, sums1)
        with ExitStack() as c0:
            m0 = Mem(nc, c0)
            weights3(nc, m0, k, w, W)
            node_update1(nc, m0, k, ps, W, X1, nodevec, sums1, out)


def kernel(**inputs):
    import concourse.bacc as bacc
    from concourse.bass_utils import run_bass_kernel_spmd

    nc = bacc.Bacc("TRN2", target_bir_lowering=False, num_devices=1)
    arrays = {}

    def given(name, a):
        a = np.ascontiguousarray(a)
        arrays[name] = a
        return nc.dram_tensor(name, a.shape, mybir.dt.from_np(a.dtype), kind="ExternalInput").ap()

    plain = [given("in_" + n, inputs[n]) for n in
             ("x", "src", "dst", "edge_attr_3", "edge_attr_4", "edge_attr_64", "node_vec1")]
    ranks = given("ranks", strict_ranks())
    w = {n: given("in_" + n, inputs["L0_gnn_" + n]) for n in WEIGHTS0}
    w.update({n: given("in_" + n, inputs["L1_gnn_" + n]) for n in WEIGHTS1})
    out = nc.dram_tensor("out", (N, X), F32, kind="ExternalOutput").ap()
    program(nc, *plain, ranks, w, out)
    result = run_bass_kernel_spmd(nc, [arrays], core_ids=[0])
    return result.results[0]["out"]
```

```python
from contextlib import ExitStack

import numpy as np

import concourse.bass as bass
from concourse import mybir
from concourse.alu_op_type import AluOpType as ALU

F32 = mybir.dt.float32
I32 = mybir.dt.int32
BF16 = mybir.dt.bfloat16
ACT = mybir.ActivationFunctionType
AX = mybir.AxisListType

N, E = 12500, 200000
R = 125
NT, ET = N // R, E // R
GT = 4
S, V = 64, 32
V3 = 3 * V
X = S + V3
COPIES = 4
DUMP = N
HALF = 62
MSG0 = X + V
MSG1 = X + 8
HEADS = 8
CH = 16
EC = E // CH
BIG = 1e30
EPS = 1e-5


def strict_ranks():
    c = np.zeros((128, 8), np.float32)
    for j in range(R):
        if j < HALF:
            c[j, 0] = 2.0 ** -j
            c[j, 2] = 2.0 ** (j - 1) / 1.25
        else:
            c[j, 1] = 2.0 ** -(j - HALF)
            c[j, 2] = 2.0 ** HALF
            c[j, 3] = 2.0 ** (j - HALF - 1) / 1.25
        c[j, 4] = DUMP + j
    return c


class Chain:

    def __init__(self, eng, sem, per, t):
        self.eng, self.sem, self.per, self.n = eng, sem, per, 0
        self.base = t * per if isinstance(t, int) else eng.snap(t * per)

    def __call__(self, ins):
        ins.then_inc(self.sem, 1)
        self.n += 1
        return ins

    def sync(self):
        self.eng.wait_ge(self.sem, self.base + self.n)

    def end(self):
        assert self.n == self.per, (self.n, self.per)


class Mem:

    def __init__(self, nc, ctx):
        self.nc, self.ctx, self.sems = nc, ctx, []
        ctx.callback(self.clear)

    def clear(self):
        if self.sems:
            self.nc.clear_and_free_semaphores(self.sems)
            self.nc.all_engine_barrier()

    def sb(self, name, shape, dt=F32):
        return self.ctx.enter_context(self.nc.sbuf_tensor(name, shape, dt))

    def sem(self, name):
        self.sems.append(self.nc.alloc_semaphore(name))
        return self.sems[-1]


def row_of(v, n):
    return v.rearrange("(a n) -> a n", a=1)[:, 0:n]


def col_of(v):
    return v.rearrange("(n a) -> n a", a=1)


def bc(ap, count, at):
    shape = list(ap.shape)
    return ap.unsqueeze(at).broadcast_to(shape[:at] + [count] + shape[at:])


def gate(eng, k):
    eng.wait_ge(k["ready"], 4)


class Settle:

    def __init__(self, m, k, name):
        self.k, self.cell, self.done = k, m.sb(name + "_cell", [1, 1]), m.sem(name + "_settled")

    def __call__(self, pool, n):
        pool.wait_ge(self.done, n)
        z = self.k["zeros"][0:1, 0:1]
        pool.tensor_tensor(self.cell[:], z, z, ALU.add).then_inc(self.done, 1)


def constants(nc, m, ranks):
    k = dict(ident=m.sb("ident", [128, 128]), ranks=m.sb("ranks_sb", [128, 8]), ready=m.sem("ready"),
             loaded=m.sem("ranks_loaded"), zeros=m.sb("zeros", [128, 2048]), ones=m.sb("ones", [128, 128]))
    with nc.Block() as block:
        @block.gpsimd
        def _(pool):
            pool.memset(k["ident"][:], 0.0).then_inc(k["ready"], 1)
            pool.memset(k["zeros"][:], 0.0).then_inc(k["ready"], 1)
            pool.memset(k["ones"][:], 1.0).then_inc(k["ready"], 1)
            pool.wait_ge(k["ready"], 3)
            pool.affine_select(out=k["ident"][:], in_=k["ident"][:], compare_op=ALU.not_equal, fill=1.0,
                               base=0, pattern=[[-1, 128]], channel_multiplier=1).then_inc(k["ready"], 1)
            pool.wait_ge(k["ready"], 4)

        @block.sync
        def _(sp):
            sp.dma_start(k["ranks"][:], ranks).then_inc(k["loaded"], 16)
            sp.wait_ge(k["loaded"], 16)
    return k


def clear(nc, m, k, name, table):
    done = m.sem(name)
    flat = table.rearrange("c r w -> (c r w)")
    per = flat.shape[0] // 128
    flat = flat.rearrange("(p w) -> p w", p=128)
    n = -(-per // 2048)
    with nc.Block() as block:
        @block.sync
        def _(sp):
            for i in range(n):
                w = min(2048, per - i * 2048)
                sp.dma_start(flat[:, i * 2048:i * 2048 + w], k["zeros"][:, 0:w]).then_inc(done, 16)
            sp.wait_ge(done, 16 * n)


def edge_rows(nc, m, k, ps, name, src, comps, dt, out_f=None, out_i=None):
    TC = 100
    own = ExitStack()
    with own:
        mm = Mem(nc, own)
        raw = mm.sb(name + "_raw", [TC, 2, R * comps], dt)
        flt = mm.sb(name + "_flt", [TC, 2, R * comps]) if dt != F32 else raw
        got = [m.sem(f"{name}_got{p}") for p in range(2)]
        cast, turned, kept = m.sem(name + "_cast"), m.sem(name + "_turned"), m.sem(name + "_kept")
        view = src.rearrange("(c t r) k -> c t (r k)", t=TC, r=R)
        with nc.Block() as block:
            @block.sync
            def _(sp):
                for c in range(CH):
                    if c >= 2:
                        sp.wait_ge(turned, c - 1)
                    sp.dma_start(raw[:, c % 2, :], view[c]).then_inc(got[c % 2], 16)

            @block.tensor
            def _(pe):
                for c in range(CH):
                    if dt == F32:
                        pe.wait_ge(got[c % 2], 16 * (c // 2 + 1))
                    else:
                        pe.wait_ge(cast, c + 1)
                    if c >= 2:
                        pe.wait_ge(kept, c - 1)
                    v = flt[:, c % 2, :].rearrange("t (r k) -> t k r", k=comps)
                    for j in range(comps):
                        last = pe.transpose(ps[0:R, 2 * (c % 2) + j // 4, 128 * (j % 4):128 * (j % 4) + TC],
                                            v[:, j, :], k["ident"][0:TC, 0:TC])
                    last.then_inc(turned, 1)

            @block.vector
            def _(dve):
                def convert(c):
                    if dt != F32:
                        dve.wait_ge(got[c % 2], 16 * (c // 2 + 1))
                        if c >= 2:
                            dve.wait_ge(turned, c - 1)
                        dve.tensor_copy(flt[:, c % 2, :], raw[:, c % 2, :]).then_inc(cast, 1)
                convert(0)
                for c in range(CH):
                    if c + 1 < CH:
                        convert(c + 1)
                    dve.wait_ge(turned, c + 1)
                    outs = [o for o in (out_f, out_i) if o is not None]
                    for o in outs:
                        for j in range(comps):
                            last = dve.tensor_copy(o[:, j, TC * c:TC * c + TC],
                                                   ps[0:R, 2 * (c % 2) + j // 4, 128 * (j % 4):128 * (j % 4) + TC])
                    last.then_inc(kept, 1)
                dve.wait_ge(kept, CH)


class Scatter:

    def __init__(self, nc, m, k, ps, name, width, index, index_dram, sums, bank):
        self.nc, self.k, self.ps, self.w, self.bank = nc, k, ps, width, bank
        self.index, self.sums = index, sums
        self.rows_dram = index_dram.rearrange("(g n) -> g n", n=GT * R)
        W = width + 2
        self.u = m.sb(name + "_u", [R, 2, GT, W])
        self.q = m.sb(name + "_q", [R, 2, GT, R])
        self.row = m.sb(name + "_row", [128, 2, GT * R], I32)
        self.total = m.sb(name + "_total", [R, 2, GT, W])
        self.small = m.sb(name + "_small", [R, 2, 2, GT])
        self.place = m.sb(name + "_place", [R, 2, GT], I32)
        pair = lambda what: [m.sem(f"{name}_{what}{p}") for p in range(2)]
        self.row_here, self.q_ready, self.u_ready = pair("row_here"), pair("q_ready"), pair("u_ready")
        self.summed, self.total_ready, self.placed = pair("summed"), pair("total_ready"), pair("placed")
        self.settle = [Settle(m, k, f"{name}_add{p}") for p in range(2)]
        self.back, self.ranked = pair("back"), m.sem(name + "_ranked")
        self.added = [[m.sem(f"{name}_added{p}{c}") for c in range(GT)] for p in range(2)]

    def load(self, sp, p, t):
        gate(sp, self.k)
        sp.wait_ge(self.q_ready[p], t)
        sp.dma_start(self.row[:, p, :], self.rows_dram[bass.ds(2 * t + p, 1), :].broadcast_to([128, GT * R])
                     ).then_inc(self.row_here[p], 16)

    def ranks(self, dve):
        for p in range(2):
            for c in range(GT):
                last = dve.tensor_copy(self.u[:, p, c, self.w:self.w + 2], self.k["ranks"][0:R, 0:2])
        last.then_inc(self.ranked, 1)
        dve.wait_ge(self.ranked, 1)

    def equal(self, dve, p, t):
        gate(dve, self.k)
        dve.wait_ge(self.row_here[p], 16 * t + 16)
        dve.wait_ge(self.summed[p], t)
        for c in range(GT):
            last = dve.tensor_scalar(self.q[:, p, c, :], self.row[0:R, p, R * c:R * c + R],
                                     self.index[:, 0, bass.ds(8 * t + 4 * p + c, 1)], None, ALU.is_equal)
        last.then_inc(self.q_ready[p], 1)

    def add_equal(self, pe, p, t):
        gate(pe, self.k)
        pe.wait_ge(self.q_ready[p], t + 1)
        pe.wait_ge(self.u_ready[p], t + 1)
        pe.wait_ge(self.total_ready[p], t)
        for c in range(GT):
            last = pe.matmul(self.ps[0:R, self.bank + 2 * p + c // 2, 256 * (c % 2):256 * (c % 2) + self.w + 2],
                             self.q[:, p, c, :], self.u[:, p, c, :], start=True, stop=True)
        last.then_inc(self.summed[p], 1)

    def evacuate(self, act, p, t):
        gate(act, self.k)
        act.wait_ge(self.summed[p], t + 1)
        act.wait_ge(self.placed[p], t)
        for c in range(GT):
            act.wait_ge(self.added[p][c], 16 * t)
        for b in range(2):
            src = self.ps[0:R, self.bank + 2 * p + b, :].rearrange("n (a w) -> n a w", a=2)[:, :, 0:self.w + 2]
            last = act.activation(self.total[:, p, 2 * b:2 * b + 2, :], src, ACT.Copy)
        last.then_inc(self.total_ready[p], 1)

    def places(self, dve, p, t):
        ranks, tot, small = self.k["ranks"], self.total[:, p, :, :], self.small[:, p, :, :]
        idx = self.index[:, 0, bass.ds(8 * t + 4 * p, GT)]
        step = Chain(dve, self.back[p], 4, t)
        gate(dve, self.k)
        dve.wait_ge(self.total_ready[p], t + 1)
        for c in range(GT):
            dve.wait_ge(self.added[p][c], 16 * t)
        step(dve.tensor_scalar(small[:, 0, :], tot[:, :, self.w], ranks[0:R, 2:3], None, ALU.mult))
        step(dve.tensor_scalar(small[:, 1, :], idx, -1.0, ranks[0:R, 4:5], ALU.mult, ALU.add))
        step.sync()
        step(dve.scalar_tensor_tensor(out=small[:, 0, :], in0=tot[:, :, self.w + 1], scalar=ranks[0:R, 3:4],
                                      in1=small[:, 0, :], op0=ALU.mult, op1=ALU.add))
        step.sync()
        step(dve.scalar_tensor_tensor(out=small[:, 1, :], in0=small[:, 0, :], scalar=1.0, in1=small[:, 1, :],
                                      op0=ALU.is_gt, op1=ALU.mult))
        step.sync()
        step.end()
        dve.tensor_tensor(self.place[:, p, :], small[:, 1, :], idx, ALU.add).then_inc(self.placed[p], 1)

    def add(self, pool, p, t):
        pool.wait_ge(self.placed[p], t + 1)
        pool.wait_ge(self.total_ready[p], t + 1)
        for c in range(GT):
            if c % 2 == 0:
                pool.wait_ge(self.added[1 - p][c], 16 * t + 16 * p)
                pool.wait_ge(self.added[1 - p][c + 1], 16 * t + 16 * p)
                self.settle[p](pool, 2 * t + c // 2)
            pool.indirect_dma_start(self.sums[c], bass.IndirectOffsetOnAxis(ap=self.place[:, p, c:c + 1], axis=0),
                                    self.total[:, p, c, 0:self.w], None, compute_op=ALU.add
                                    ).then_inc(self.added[p][c], 16)

    def finish(self, pool):
        for p in range(2):
            for c in range(GT):
                pool.wait_ge(self.added[p][c], 16 * (ET // GT // 2))


def layer0_edges(nc, m, k, ps, W, T0, dstI, srcF, src, attr, sums, es, H):
    own = ExitStack()
    with own:
        mm = Mem(nc, own)
        sc = Scatter(nc, mm, k, ps, "e0", MSG0, srcF, src, sums, 0)
        rows = mm.sb("e0_rows", [R, 2, GT, 448])
        at = mm.sb("e0_at", [R, 2, GT], I32)
        prod = mm.sb("e0_prod", [R, 2, GT, 3, V])
        prodD = mm.sb("e0_prodD", [R, 2, GT, 3, V])
        here = [[m.sem(f"e0_here{p}{c}") for c in range(GT)] for p in range(2)]
        at_ready = [m.sem(f"e0_at_ready{p}") for p in range(2)]
        steps = [m.sem(f"e0_steps{p}") for p in range(2)]
        settle = [Settle(mm, k, f"e0_gather{p}") for p in range(2)]
        GP = ET // GT // 2

        def gather(pool, p, t):
            pool.wait_ge(sc.u_ready[p], t)
            for c in range(GT):
                pool.wait_ge(here[p][c], 16 * t)
            settle[p](pool, 2 * t)
            pool.tensor_copy(at[:, p, :], dstI[:, 0, bass.ds(8 * t + 4 * p, GT)]).then_inc(at_ready[p], 1)
            for c in range(GT):
                if c == 0:
                    pool.wait_ge(at_ready[p], t + 1)
                    settle[p](pool, 2 * t + 1)
                pool.indirect_dma_start(rows[:, p, c, :], None, T0, bass.IndirectOffsetOnAxis(
                    ap=at[:, p, c:c + 1], axis=0)).then_inc(here[p][c], 16)

        def messages(dve, p, t):
            sc.equal(dve, p, t)
            u, g, pr, pd = sc.u[:, p], rows[:, p], prod[:, p], prodD[:, p]
            step = Chain(dve, steps[p], 8, t)
            col = 8 * t + 4 * p
            gate(dve, k)
            for c in range(GT):
                dve.wait_ge(here[p][c], 16 * t + 16)
            r = attr[:, 0:3, bass.ds(col, GT)].rearrange("n i c -> n c i")
            r4 = bc(r, V, 3)
            step(dve.tensor_tensor(pr[:], g[:, :, 352:448].rearrange("n c (i u) -> n c i u", i=3), r4, ALU.mult))
            step(dve.tensor_tensor(pd[:], bc(g[:, :, 320:352], 3, 2), r4, ALU.mult))
            for c in range(GT):
                step(dve.scalar_tensor_tensor(out=u[:, c, 0:X], in0=g[:, c, 0:X],
                                              scalar=attr[:, 3, bass.ds(col + c, 1)], in1=g[:, c, X:2 * X],
                                              op0=ALU.mult, op1=ALU.add))
            step.sync()
            step(dve.tensor_tensor(u[:, :, S:X].rearrange("n c (i u) -> n c i u", i=3),
                                   u[:, :, S:X].rearrange("n c (i u) -> n c i u", i=3), pd[:], ALU.add))
            step(dve.tensor_tensor(pr[:, :, 0, :], pr[:, :, 0, :], pr[:, :, 1, :], ALU.add))
            step.sync()
            step.end()
            dve.tensor_tensor(u[:, :, X:X + V], pr[:, :, 0, :], pr[:, :, 2, :], ALU.add).then_inc(sc.u_ready[p], 1)

        net = Radial(mm, k, ps, W, es, H)
        rounds = GP // 2
        with nc.Block() as block:
            @block.sync
            def _(sp):
                for p in range(2):
                    sc.load(sp, p, 0)
                net.load(sp, 0)
                with sp.Fori(0, rounds - 1) as t:
                    for p in range(2):
                        sc.load(sp, p, 2 * t + 1)
                    net.load(sp, t + 1)
                    for p in range(2):
                        sc.load(sp, p, 2 * t + 2)
                    net.store(sp, t)
                for p in range(2):
                    sc.load(sp, p, 2 * rounds - 1)
                net.store(sp, rounds - 1)
                net.finish(sp)

            @block.gpsimd
            def _(pool):
                gather(pool, 0, 0)
                gather(pool, 1, 0)
                with pool.Fori(0, GP - 1) as t:
                    for p in range(2):
                        gather(pool, p, t + 1)
                        sc.add(pool, p, t)
                for p in range(2):
                    sc.add(pool, p, GP - 1)
                sc.finish(pool)

            @block.vector
            def _(dve):
                def round_(t, last):
                    for s in range(4):
                        p, g = s % 2, 2 * t + s // 2
                        if p == 0:
                            messages(dve, 1, g)
                        elif not (last and s == 3):
                            messages(dve, 0, g + 1)
                        sc.places(dve, p, g)
                        if s % 2:
                            net.normalise(dve, t, s // 2 + 1)
                sc.ranks(dve)
                messages(dve, 0, 0)
                with dve.Fori(0, rounds - 1) as t:
                    round_(t, False)
                round_(rounds - 1, True)

            @block.tensor
            def _(pe):
                with pe.Fori(0, rounds) as t:
                    for s in range(4):
                        net.products(pe, t, s)
                        sc.add_equal(pe, s % 2, 2 * t + s // 2)

            @block.scalar
            def _(act):
                with act.Fori(0, rounds) as t:
                    for s in range(4):
                        net.squares_and_roots(act, t, s)
                        sc.evacuate(act, s % 2, 2 * t + s // 2)
                        if s % 2:
                            net.silu(act, t, s // 2 + 1)


def run_edges(nc, sc, messages, GP, load):
    with nc.Block() as block:
        @block.sync
        def _(sp):
            with sp.Fori(0, GP) as t:
                for p in range(2):
                    load(sp, p, t)
                    sc.load(sp, p, t)

        @block.gpsimd
        def _(pool):
            with pool.Fori(0, GP) as t:
                for p in range(2):
                    sc.add(pool, p, t)
            sc.finish(pool)

        @block.vector
        def _(dve):
            sc.ranks(dve)
            messages(dve, 0, 0)
            with dve.Fori(0, GP - 1) as t:
                messages(dve, 1, t)
                sc.places(dve, 0, t)
                messages(dve, 0, t + 1)
                sc.places(dve, 1, t)
            messages(dve, 1, GP - 1)
            sc.places(dve, 0, GP - 1)
            sc.places(dve, 1, GP - 1)

        @block.tensor
        def _(pe):
            with pe.Fori(0, GP) as t:
                for p in range(2):
                    sc.add_equal(pe, p, t)

        @block.scalar
        def _(act):
            with act.Fori(0, GP) as t:
                for p in range(2):
                    sc.evacuate(act, p, t)


class Radial:

    def __init__(self, m, k, ps, W, es, H):
        self.k, self.ps, self.W, self.H = k, ps, W, H
        self.raw = m.sb("r_raw", [R, 2, GT, 2, S])
        self.xT, self.sq, self.std, self.rstd, self.y, self.h, self.h2 = (
            m.sb("r_" + n, [128, 2, GT * R]) for n in ("xT", "sq", "std", "rstd", "y", "h", "h2"))
        self.here = [m.sem(f"r_here{p}") for p in range(2)]
        self.stored = [m.sem(f"r_stored{p}") for p in range(2)]
        both = lambda names: [f"{n}{p}" for n in names for p in range(2)]
        self.pe_s = Steps(m, k, "r_pe", both(["turned", "h1_", "v1_", "h2_", "v2_"]))
        self.ac_s = Steps(m, k, "r_act", both(["xT", "sq1_", "std1_", "silu1_", "sq2_", "std2_", "silu2_"]))
        self.dv_s = Steps(m, k, "r_dve", both(["r1_", "y1_", "r2_", "y2_"]))
        self.view = es.rearrange("(g h j r) k -> g h r j k", h=2, j=GT, r=R)

    def load(self, sp, t):
        if not isinstance(t, int):
            self.pe_s.wait(sp, t - 1, "turned1")
        for p in range(2):
            for half in range(2):
                sp.dma_start(self.raw[:, p, :, half, :], self.view[bass.ds(2 * t + p, 1), half].rearrange(
                    "g r j k -> (g r) j k")).then_inc(self.here[p], 16)

    def store(self, sp, t):
        for p in range(2):
            self.ac_s.wait(sp, t, f"silu2_{p}")
            sp.dma_start(self.H[bass.ds(2 * t + p, 1)].rearrange("g q n -> (g q) n"), self.h2[:, p, :]
                         ).then_inc(self.stored[p], 16)

    def finish(self, sp):
        for p in range(2):
            sp.wait_ge(self.stored[p], 16 * (ET // (4 * GT)))

    def products(self, pe, t, s):
        ps, W, lay = self.ps, self.W, s // 2 + 1
        for p in range(2):
            if s == 0:
                gate(pe, self.k)
                pe.wait_ge(self.here[p], 32 * t + 32)
                pe.wait_ge(self.ac_s.sem, t * len(self.ac_s.names))
                for j in range(GT):
                    last = pe.transpose(ps[:, 4 + p, R * j:R * j + R], self.raw[:, p, j].rearrange("r h k -> r (h k)"),
                                        self.k["ident"][0:R, 0:R])
                self.pe_s.done(last, f"turned{p}")
        for p in range(2):
            if s % 2 == 0:
                src, ready = (self.xT, "xT") if s == 0 else (self.h, "silu1_")
                self.ac_s.wait(pe, t, f"{ready}{p}")
                self.pe_s.done(pe.matmul(ps[:, 6 + p, 0:GT * R], W[f"r{lay}"][:], src[:, p, :],
                                         start=True, stop=True), f"h{lay}_{p}")
            else:
                self.ac_s.wait(pe, t, f"sq{lay}_{p}")
                self.pe_s.done(pe.matmul(ps[:, 4 + p, 0:GT * R], W["avg"][:], self.sq[:, p, :], start=True,
                                         stop=True), f"v{lay}_{p}")

    def squares_and_roots(self, act, t, s):
        ps, W, lay = self.ps, self.W, s // 2 + 1
        if s == 0:
            for p in range(2):
                self.pe_s.wait(act, t, f"turned{p}")
                self.ac_s.done(act.activation(self.xT[:, p, :], ps[:, 4 + p, 0:GT * R], ACT.Copy), f"xT{p}")
        for p in range(2):
            if s % 2 == 0:
                b = 3 * (lay - 1)
                self.pe_s.wait(act, t, f"h{lay}_{p}")
                self.ac_s.done(act.activation(self.sq[:, p, :], ps[:, 6 + p, 0:GT * R], ACT.Square,
                                              bias=W["rb"][:, b:b + 1]), f"sq{lay}_{p}")
            else:
                self.pe_s.wait(act, t, f"v{lay}_{p}")
                self.ac_s.done(act.activation(self.std[:, p, :], ps[:, 4 + p, 0:GT * R], ACT.Sqrt,
                                              bias=W["eps"][:]), f"std{lay}_{p}")

    def normalise(self, dve, t, lay):
        b = 3 * (lay - 1)
        for p in range(2):
            self.ac_s.wait(dve, t, f"std{lay}_{p}")
            self.dv_s.done(dve.reciprocal(self.rstd[:, p, :], self.std[:, p, :]), f"r{lay}_{p}")
        for p in range(2):
            self.dv_s.wait(dve, t, f"r{lay}_{p}")
            self.dv_s.done(dve.scalar_tensor_tensor(out=self.y[:, p, :], in0=self.ps[:, 6 + p, 0:GT * R],
                                                    scalar=self.W["rb"][:, b:b + 1], in1=self.rstd[:, p, :],
                                                    op0=ALU.add, op1=ALU.mult), f"y{lay}_{p}")

    def silu(self, act, t, lay):
        b = 3 * (lay - 1)
        for p in range(2):
            self.dv_s.wait(act, t, f"y{lay}_{p}")
            if lay == 2:
                gate(act, self.k)
                act.wait_ge(self.stored[p], 16 * t)
            self.ac_s.done(act.activation((self.h if lay == 1 else self.h2)[:, p, :], self.y[:, p, :], ACT.Silu,
                                          bias=self.W["rb"][:, b + 2:b + 3], scale=self.W["rb"][:, b + 1:b + 2]),
                           f"silu{lay}_{p}")


def layer0_tables(nc, m, k, ps, x, W, T0):
    own = ExitStack()
    with own:
        mm = Mem(nc, own)
        xt = mm.sb("n0_x", [R, 2, X])
        out = mm.sb("n0_out", [R, 2, 448])
        sT, vT = mm.sb("n0_sT", [S, 2, R]), mm.sb("n0_vT", [V3, 2, R])
        got = [m.sem(f"n0_got{p}") for p in range(2)]
        stored = [m.sem(f"n0_stored{p}") for p in range(2)]
        turned = [m.sem(f"n0_turned{p}") for p in range(2)]
        kept = [m.sem(f"n0_kept{p}") for p in range(2)]
        product = [m.sem(f"n0_product{p}") for p in range(2)]
        full = [m.sem(f"n0_full{p}") for p in range(2)]
        split = [m.sem(f"n0_split{p}") for p in range(2)]
        with nc.Block() as block:
            @block.sync
            def _(sp):
                with sp.Fori(0, NT // 2) as t:
                    for p in range(2):
                        gate(sp, k)
                        sp.wait_ge(turned[p], t)
                        sp.wait_ge(full[p], t * 2)
                        sp.dma_start(xt[:, p, :], x[bass.ds((2 * t + p) * R, R), :]).then_inc(got[p], 16)

            @block.tensor
            def _(pe):
                with pe.Fori(0, NT // 2) as t:
                    for p in range(2):
                        gate(pe, k)
                        pe.wait_ge(got[p], 16 * t + 16)
                        pe.wait_ge(kept[p], 2 * t)
                        pe.wait_ge(split[p], t + 1)
                        pe.transpose(ps[0:V3, p, 128:128 + R], out[:, p, 352:448], k["ident"][0:R, 0:R])
                        pe.transpose(ps[0:S, p, 0:R], xt[:, p, 0:S], k["ident"][0:R, 0:R]).then_inc(turned[p], 1)
                        gate(pe, k)
                        pe.wait_ge(kept[p], 2 * t + 2)
                        pe.wait_ge(full[p], 2 * t)
                        pe.matmul(ps[0:R, 2 + p, 0:160], sT[:, p, :], W["s"][:], start=True, stop=True)
                        pe.matmul(ps[0:R, 4 + p, 0:192], vT[:, p, :], W["v"][:], start=True,
                                  stop=True).then_inc(product[p], 1)

            @block.scalar
            def _(act):
                with act.Fori(0, NT // 2) as t:
                    for p in range(2):
                        act.wait_ge(turned[p], t + 1)
                        act.wait_ge(product[p], t)
                        act.activation(sT[:, p, :], ps[0:S, p, 0:R], ACT.Copy).then_inc(kept[p], 1)
                        act.activation(vT[:, p, :], ps[0:V3, p, 128:128 + R], ACT.Copy).then_inc(kept[p], 1)
                        act.wait_ge(product[p], t + 1)
                        act.wait_ge(stored[p], 16 * t)
                        act.activation(out[:, p, 0:320].rearrange("n (a w) -> n a w", a=2)[:, :, 0:S],
                                       ps[0:R, 2 + p, 0:128].rearrange("n (a w) -> n a w", a=2),
                                       ACT.Copy)
                        act.activation(out[:, p, 320:352], ps[0:R, 2 + p, 128:160], ACT.Copy).then_inc(full[p], 1)

            @block.vector
            def _(dve):
                with dve.Fori(0, NT // 2) as t:
                    for p in range(2):
                        gate(dve, k)
                        dve.wait_ge(got[p], 16 * t + 16)
                        dve.wait_ge(stored[p], 16 * t)
                        dve.tensor_copy(out[:, p, 352:448].rearrange("n (i u) -> n i u", i=3),
                                        xt[:, p, S:X].rearrange("n (u i) -> n i u", i=3)).then_inc(split[p], 1)
                    for p in range(2):
                        gate(dve, k)
                        dve.wait_ge(product[p], t + 1)
                        dve.tensor_copy(out[:, p, 0:320].rearrange("n (a w) -> n a w", a=2)[:, :, S:X],
                                        ps[0:R, 4 + p, 0:192].rearrange("n (a w) -> n a w", a=2)
                                        ).then_inc(full[p], 1)

            @block.gpsimd
            def _(pool):
                with pool.Fori(0, NT // 2) as t:
                    for p in range(2):
                        gate(pool, k)
                        pool.wait_ge(full[p], 2 * t + 2)
                        pool.dma_start(T0[bass.ds((2 * t + p) * R, R), :], out[:, p, :]).then_inc(stored[p], 16)
                for p in range(2):
                    pool.wait_ge(stored[p], 16 * (NT // 2))


class Steps:

    def __init__(self, m, k, name, names):
        self.k, self.sem, self.names, self.at = k, m.sem(name), names, 0

    def done(self, ins, what):
        assert self.names[self.at % len(self.names)] == what, (what, self.names[self.at % len(self.names)])
        self.at += 1
        return ins.then_inc(self.sem, 1)

    def wait(self, eng, t, what):
        gate(eng, self.k)
        eng.wait_ge(self.sem, t * len(self.names) + self.names.index(what) + 1)


class Vector(Chain):

    def __init__(self, k, sem, per, marks, t):
        self.k, self.eng, self.sem, self.per, self.n, self.marks, self.t = k, None, sem, per, 0, marks, t
        self.base = t * per

    def sync(self):
        gate(self.eng, self.k)
        self.eng.wait_ge(self.sem, self.base + self.n)

    def mark(self, name):
        self.marks[name] = self.n


def marked(eng, k, sem, per, marks, t, name):
    gate(eng, k)
    eng.wait_ge(sem, t * per + marks[name])


def load_weights(nc, m, k, name, loads, also=()):
    done, zeroed = m.sem(name + "_loaded"), m.sem(name + "_zeroed")
    tiles = list(also)
    for tile, *_ in loads:
        if all(tile is not x for x in tiles):
            tiles.append(tile)
    with nc.Block() as block:
        @block.gpsimd
        def _(pool):
            for tile in tiles:
                pool.memset(tile[:], 0.0).then_inc(zeroed, 1)
            pool.wait_ge(zeroed, len(tiles))

        @block.sync
        def _(sp):
            sp.wait_ge(zeroed, len(tiles))
            for _, to, of in loads:
                sp.dma_start(to, of).then_inc(done, 16)
            sp.wait_ge(done, 16 * len(loads))


def scale_all(nc, m, k, name, scales):
    done = m.sem(name + "_scaled")
    with nc.Block() as block:
        @block.vector
        def _(dve):
            for ap, by in scales:
                dve.tensor_scalar(ap, ap, float(by), None, ALU.mult).then_inc(done, 1)
            dve.wait_ge(done, len(scales))


def diagonal(tile, col, src, wide=V):
    return [(tile, tile[V * i:V * i + V, col + wide * i:col + wide * i + wide], src) for i in range(3)]


FRONT, BACK = 38, 14


def node_update0(nc, m, k, ps, W, x, sums, X1, TS, TD):
    own = ExitStack()
    with own:
        mm = Mem(nc, own)
        sb = mm.sb
        xt, ag = sb("n1_x", [R, 2, X]), sb("n1_ag", [R, 2, COPIES, MSG0])
        a, xd = sb("n1_a", [R, MSG0]), sb("n1_xd", [R, V3])
        vrT, sT, vT, a0T = sb("n1_vrT", [V, R]), sb("n1_sT", [S, R]), sb("n1_vT", [V3, R]), sb("n1_a0T", [S, R])
        z, zv, zp = sb("n1_z", [R, S * S]), sb("n1_zv", [R, V * V]), sb("n1_zp", [R, 2, V * V])
        zT = sb("n1_zT", [128, 40, R])
        prod = sb("n1_prod", [R, 2, 512])
        part = sb("n1_part", [R, 2, 3, V])
        y, stat, st2, y1 = sb("n1_y", [R, 2, X]), sb("n1_stat", [R, 2, 6]), sb("n1_st2", [R, 16]), sb("n1_y1", [R, 2, X])
        sq = sb("n1_sq", [R, V3])
        norm = sb("n1_norm", [R, X])
        snT, vnT = sb("n1_snT", [S, R]), sb("n1_vnT", [V3, R])
        out = sb("n1_out", [R, 2, 2, X])
        here = [mm.sem(f"n1_here{p}") for p in range(2)]
        stored = [mm.sem(f"n1_stored{p}") for p in range(2)]
        front_s, back_s, marks_f, marks_b = mm.sem("n1_front"), mm.sem("n1_back"), {}, {}
        blocks = [f"z{i}" for i in range(10)]
        pe_f = Steps(mm, k, "n1_pe_front", ["turned", "vr", "a0", "g"] + blocks + ["u0"])
        ac_f = Steps(mm, k, "n1_act_front", ["turned", "a0"] + blocks)
        pe_b = Steps(mm, k, "n1_pe_back", ["norm", "tables"])
        ac_b = Steps(mm, k, "n1_act_back", ["root1", "root2", "norm", "out"])

        def fronted(eng, t, name):
            marked(eng, k, front_s, FRONT, marks_f, t, name)

        def backed(eng, t, name):
            marked(eng, k, back_s, BACK, marks_b, t, name)

        def pipeline(eng, both):
            both((0, 0), None)
            with eng.Fori(0, NT // 2 - 1) as h:
                both((h, 1), (h, 0))
                both((h + 1, 0), (h, 1))
            both((NT // 2 - 1, 1), (NT // 2 - 1, 0))
            both(None, (NT // 2 - 1, 1))

        with nc.Block() as block:
            @block.vector
            def _(dve):
                def chain(tile, sem, per, marks):
                    v = Vector(k, sem, per, marks, 2 * tile[0] + tile[1])
                    v.eng = dve
                    return v

                def sum_up(v, h, p):
                    gate(dve, k)
                    dve.wait_ge(here[p], 80 * h + 80)
                    v(dve.tensor_tensor(a[:], ag[:, p, 0, :], ag[:, p, 1, :], ALU.add))
                    v(dve.tensor_copy(xd[:].rearrange("n (i u) -> n i u", i=3),
                                      xt[:, p, S:X].rearrange("n (u i) -> n i u", i=3)))
                    v.sync()
                    v(dve.tensor_tensor(a[:], a[:], ag[:, p, 2, :], ALU.add))
                    v.sync()
                    v(dve.tensor_tensor(a[:], a[:], ag[:, p, 3, :], ALU.add))
                    v.mark("summed")

                def products(v, t, p):
                    pe_f.wait(dve, t, "vr")
                    v.sync()
                    v(dve.tensor_tensor(a[:, 0:S], a[:, 0:S], ps[0:R, 2, 0:S], ALU.add))
                    v.mark("a0")
                    v.sync()
                    v(dve.tensor_tensor(z[:].rearrange("n (u v) -> n u v", u=S), bc(xt[:, p, 0:S], S, 2),
                                        bc(a[:, 0:S], S, 1), ALU.mult))
                    v.mark("z")
                    for i in range(3):
                        xv = bc(xd[:, V * i:V * i + V], V, 2)
                        av = bc(a[:, S + V * i:S + V * i + V], V, 1)
                        to = zv[:] if i == 0 else zp[:, i - 1, :]
                        v(dve.tensor_tensor(to.rearrange("n (u v) -> n u v", u=V), xv, av, ALU.mult))
                    v.sync()
                    v(dve.tensor_tensor(zv[:], zv[:], zp[:, 0, :], ALU.add))
                    v.sync()
                    v(dve.tensor_tensor(zv[:], zv[:], zp[:, 1, :], ALU.add))
                    v.mark("zv")

                def vector_maps(v, t, i):
                    if i == 0:
                        pe_f.wait(dve, t, "g")
                    for g in range(4):
                        by = a[:, S + V * i:S + V * i + V] if g < 2 else xd[:, V * i:V * i + V]
                        if i + g:
                            v.sync()
                        v(dve.tensor_tensor(prod[:, g % 2, :].rearrange("n (w v) -> n w v", v=V),
                                            ps[0:R, 2 + g, :].rearrange("n (w v) -> n w v", v=V),
                                            bc(by, 16, 1), ALU.mult))
                        v.sync()
                        v(dve.tensor_reduce(part[:, g // 2, i, 16 * (g % 2):16 * (g % 2) + 16],
                                            prod[:, g % 2, :].rearrange("n (w v) -> n w v", v=V),
                                            AX.X, ALU.add))

                def residual(v, p):
                    v.sync()
                    p0, p1 = (part[:, q].rearrange("n i w -> n (i w)") for q in range(2))
                    v(dve.tensor_tensor(p0, p0, p1, ALU.add))
                    v.sync()
                    v(dve.scalar_tensor_tensor(out=y[:, p, S:X], in0=xd[:], scalar=2.0, in1=p0, op0=ALU.mult, op1=ALU.add))
                    v(dve.tensor_scalar(y[:, p, 0:S], xt[:, p, 0:S], 2.0, None, ALU.mult))
                    v.mark("end")
                    v.sync()
                    v.end()

                def moments(v, t, p):
                    pe_f.wait(dve, t, "u0")
                    v(dve.tensor_tensor(y[:, p, :], y[:, p, :], ps[0:R, 1, 128:128 + X], ALU.add))
                    v.sync()
                    v(dve.bn_stats(stat[:, 0, :], y[:, p, :]))
                    v.sync()
                    v(dve.memset(st2[:, 12:13], 0.0))
                    v(dve.bn_aggr(st2[:, 0:2], stat[:, 0, :]))
                    v.mark("var1")

                def first_norm(v, t, h, p):
                    ac_b.wait(dve, t, "root1")
                    v(dve.reciprocal(st2[:, 3:4], st2[:, 2:3]))
                    v.sync()
                    gate(dve, k)
                    dve.wait_ge(stored[p], 48 * h)
                    v(dve.tensor_scalar(y1[:, p, :], y[:, p, :], st2[:, 0:1], st2[:, 3:4], ALU.subtract, ALU.mult))
                    v.mark("x1")
                    v.sync()
                    v(dve.bn_stats(stat[:, 1, :], y1[:, p, 0:S]))
                    v(dve.tensor_tensor(sq[:], y1[:, p, S:X], y1[:, p, S:X], ALU.mult))
                    v.sync()
                    v(dve.tensor_reduce(st2[:, 6:7], sq[:], AX.X, ALU.add))
                    v(dve.bn_aggr(st2[:, 4:6], stat[:, 1, :]))
                    v.sync()
                    v(dve.tensor_scalar(st2[:, 6:7], st2[:, 6:7], 1.0 / V3, None, ALU.mult))
                    v.mark("var2")

                def second_norm(v, t, p):
                    ac_b.wait(dve, t, "root2")
                    v(dve.reciprocal(st2[:, 10:12], st2[:, 8:10]))
                    v.sync()
                    gate(dve, k)
                    dve.wait_ge(pe_b.sem, 2 * t)
                    v(dve.tensor_scalar(norm[:, 0:S], y1[:, p, 0:S], st2[:, 4:5], st2[:, 10:11],
                                        ALU.subtract, ALU.mult))
                    v(dve.tensor_scalar(norm[:, S:X], y1[:, p, S:X], st2[:, 11:12], None, ALU.mult))
                    v.mark("norm")
                    v.sync()
                    v.end()

                def both(new, old):
                    if new:
                        f, (h, p), t = chain(new, front_s, FRONT, marks_f), new, 2 * new[0] + new[1]
                        sum_up(f, h, p)
                    if old:
                        b, (h2, p2), t2 = chain(old, back_s, BACK, marks_b), old, 2 * old[0] + old[1]
                        moments(b, t2, p2)
                    if new:
                        products(f, t, p)
                    if old:
                        first_norm(b, t2, h2, p2)
                    if new:
                        vector_maps(f, t, 0)
                    if old:
                        second_norm(b, t2, p2)
                    if new:
                        vector_maps(f, t, 1)
                        vector_maps(f, t, 2)
                        residual(f, p)

                pipeline(dve, both)

            @block.sync
            def _(sp):
                def load(t, p):
                    rows = bass.ds(t * R, R)
                    sp.dma_start(xt[:, p, :], x[rows, :]).then_inc(here[p], 16)
                    for c in range(COPIES):
                        sp.dma_start(ag[:, p, c, :], sums[c][rows, :]).then_inc(here[p], 16)

                def store(t, p):
                    rows = bass.ds(t * R, R)
                    backed(sp, t, "x1")
                    sp.dma_start(X1[rows, :], y1[:, p, :]).then_inc(stored[p], 16)
                    ac_b.wait(sp, t, "out")
                    sp.dma_start(TS[rows, :], out[:, p, 0, :]).then_inc(stored[p], 16)
                    sp.dma_start(TD[rows, :], out[:, p, 1, :]).then_inc(stored[p], 16)
                load(0, 0)
                load(1, 1)
                with sp.Fori(0, NT // 2 - 1) as h:
                    for p in range(2):
                        t = 2 * h + p
                        fronted(sp, t, "end")
                        load(t + 2, p)
                        store(t, p)
                for p in range(2):
                    store(NT - 2 + p, p)
                for p in range(2):
                    sp.wait_ge(stored[p], 48 * (NT // 2))

            @block.tensor
            def _(pe):
                I = k["ident"]

                def front(t, p):
                    fronted(pe, t, "summed")
                    pe.transpose(ps[0:V, 0, 0:R], a[:, X:MSG0], I[0:R, 0:R])
                    pe.transpose(ps[0:S, 0, 128:128 + R], xt[:, p, 0:S], I[0:R, 0:R])
                    pe_f.done(pe.transpose(ps[0:V3, 0, 256:256 + R], xd[:], I[0:R, 0:R]), "turned")
                    ac_f.wait(pe, t, "turned")
                    pe_f.done(pe.matmul(ps[0:R, 2, 0:S], vrT[:], W["wvv"][:], start=True, stop=True), "vr")
                    fronted(pe, t, "a0")
                    pe_f.done(pe.transpose(ps[:, 0, 384:384 + R], a[:, 0:128], I[0:R, 0:R]), "a0")
                    ac_f.wait(pe, t, "a0")
                    for g in range(2):
                        pe.matmul(ps[0:R, 2 + g, :], sT[:], W["usv"][:, 512 * g:512 * g + 512], start=True, stop=True)
                    for g in range(2):
                        last = pe.matmul(ps[0:R, 4 + g, :], a0T[:], W["uvs"][:, 512 * g:512 * g + 512],
                                         start=True, stop=True)
                    pe_f.done(last, "g")
                    for b in range(10):
                        if b == 0:
                            fronted(pe, t, "z")
                            gate(pe, k)
                            pe.wait_ge(ac_b.sem, tables_read(t))
                        if b == 8:
                            fronted(pe, t, "zv")
                        if b >= 2:
                            ac_f.wait(pe, t, f"z{b - 2}")
                        for c in range(4):
                            src = z[:, 512 * b + 128 * c:512 * b + 128 * c + 128] if b < 8 else \
                                zv[:, 512 * (b - 8) + 128 * c:512 * (b - 8) + 128 * c + 128]
                            last = pe.transpose(ps[:, 6 + b % 2, R * c:R * c + R], src, I[0:R, 0:R])
                        pe_f.done(last, f"z{b}")
                    ac_f.wait(pe, t, "z9")
                    u0 = ps[0:R, 1, 128:128 + S]
                    for b in range(40):
                        w = W["uss"][:, b, :] if b < 32 else W["uvv"][:, b - 32, :]
                        pe.matmul(u0, zT[:, b, :], w, start=(b == 0), stop=False)
                    pe.matmul(u0, sT[:], W["lus"][:], start=False, stop=True)
                    pe_f.done(pe.matmul(ps[0:R, 1, 128 + S:128 + X], vT[:], W["luv"][:], start=True, stop=True), "u0")

                def tables_read(t):
                    return max(4 * t - 3, 0) if isinstance(t, int) else 4 * t - 3

                def back(t):
                    backed(pe, t, "norm")
                    pe.transpose(ps[0:V3, 0, 128:128 + R], norm[:, S:X], I[0:R, 0:R])
                    pe_b.done(pe.transpose(ps[0:S, 0, 0:R], norm[:, 0:S], I[0:R, 0:R]), "norm")
                    ac_b.wait(pe, t, "norm")
                    pe.matmul(ps[0:R, 6, 0:S], snT[:], W["msd"][:, 0:S], start=True, stop=True)
                    pe.matmul(ps[0:R, 6, S:2 * S], snT[:], W["msd"][:, S:2 * S], start=True, stop=False)
                    pe.matmul(ps[0:R, 6, S:2 * S], k["ones"][0:1, 0:R], W["rows"][0:1, 0:S], start=False, stop=True)
                    pe_b.done(pe.matmul(ps[0:R, 6, 128:320], vnT[:], W["mv"][:], start=True, stop=True), "tables")

                def both(new, old):
                    if new:
                        front(2 * new[0] + new[1], new[1])
                    if old:
                        back(2 * old[0] + old[1])

                pipeline(pe, both)

            @block.scalar
            def _(act):
                def both(new, old):
                    if new:
                        t = 2 * new[0] + new[1]
                        pe_f.wait(act, t, "turned")
                        act.activation(vrT[:], ps[0:V, 0, 0:R], ACT.Copy)
                        act.activation(sT[:], ps[0:S, 0, 128:128 + R], ACT.Copy)
                        ac_f.done(act.activation(vT[:], ps[0:V3, 0, 256:256 + R], ACT.Copy), "turned")
                    if old:
                        h2, p2, t2 = *old, 2 * old[0] + old[1]
                        backed(act, t2, "var1")
                        ac_b.done(act.activation(st2[:, 2:3], st2[:, 1:2], ACT.Sqrt, bias=W["eps"][0:R, :]), "root1")
                    if new:
                        pe_f.wait(act, t, "a0")
                        ac_f.done(act.activation(a0T[:], ps[0:S, 0, 384:384 + R], ACT.Copy), "a0")
                        for b in range(10):
                            pe_f.wait(act, t, f"z{b}")
                            ac_f.done(act.activation(zT[:, 4 * b:4 * b + 4, :].rearrange("q c n -> q (c n)"),
                                                     ps[:, 6 + b % 2, 0:4 * R], ACT.Copy), f"z{b}")
                    if old:
                        backed(act, t2, "var2")
                        ac_b.done(act.activation(st2[:, 8:10], st2[:, 5:7], ACT.Sqrt, bias=W["eps"][0:R, :]), "root2")
                        pe_b.wait(act, t2, "norm")
                        act.activation(snT[:], ps[0:S, 0, 0:R], ACT.Identity, bias=W["ln1"][0:S, 1:2],
                                       scale=W["ln1"][0:S, 0:1])
                        ac_b.done(act.activation(vnT[:], ps[0:V3, 0, 128:128 + R], ACT.Copy,
                                                 scale=W["ln1"][0:V3, 2:3]), "norm")
                        pe_b.wait(act, t2, "tables")
                        gate(act, k)
                        act.wait_ge(stored[p2], 48 * h2)
                        act.activation(out[:, p2, :, 0:S], ps[0:R, 6, 0:128].rearrange("n (a w) -> n a w", a=2), ACT.Copy)
                        ac_b.done(act.activation(out[:, p2, :, S:X],
                                                 ps[0:R, 6, 128:320].rearrange("n (a w) -> n a w", a=2), ACT.Copy), "out")

                pipeline(act, both)


INV_SQRT3, INV8, INV_SQRT32 = 0.5773502691896258, 0.125, 0.17677669529663687
INV64, INV32, INV_SQRT2048 = 0.015625, 0.03125, 0.022097086912079608
SQ3, SQ2 = float(np.sqrt(3.0)), float(np.sqrt(2.0))


def weights0(nc, m, k, w):
    W = dict(s=m.sb("w_s", [S, 160]), v=m.sb("w_v", [V3, 192]), wvv=m.sb("w_vv", [V, S]))
    loads = [(W["s"], W["s"][:, 0:64], w["Wm_ss"]), (W["s"], W["s"][:, 64:128], w["Lm_s"]),
             (W["s"], W["s"][:, 128:160], w["Wm_sv"]), (W["wvv"], W["wvv"][:], w["Wm_vv"])]
    loads += diagonal(W["v"], 0, w["Wm_vs"]) + diagonal(W["v"], 96, w["Lm_v"])
    load_weights(nc, m, k, "w0", loads)
    scale_all(nc, m, k, "w0", [(W["s"][:], INV8), (W["v"][:], INV_SQRT32), (W["wvv"][:], INV_SQRT3 * INV_SQRT32)])
    return W


def weights1(nc, m, k, w, W):
    own = ExitStack()
    with own:
        mm = Mem(nc, own)
        for n, shape in dict(uss=[128, V, S], uvv=[128, 8, S], usv=[S, 1024], uvs=[S, 1024], lus=[S, S],
                             luv=[V3, V3], msd=[S, 2 * S], mv=[V3, 2 * V3]).items():
            W[n] = m.sb("w_" + n, shape)
        rsv, rvs = mm.sb("raw_sv", [S, V, V]), mm.sb("raw_vs", [S, V, V])
        loads = [(W["uss"], W["uss"][:], w["Wu_ss"].rearrange("(k a) v w -> (a v) k w", a=2)),
                 (W["uvv"], W["uvv"][:], w["Wu_vv"].rearrange("(k a) v w -> (a v) k w", a=4)),
                 (rsv, rsv[:], w["Wu_sv"]), (rvs, rvs[:], w["Wu_vs"].rearrange("u v w -> v u w")),
                 (W["lus"], W["lus"][:], w["Lu_s"]), (W["msd"], W["msd"][:, 0:S], w["msrc_ws"]),
                 (W["msd"], W["msd"][:, S:2 * S], w["mdst_ws"])]
        loads += diagonal(W["luv"], 0, w["Lu_v"]) + diagonal(W["mv"], 0, w["msrc_wv"]) + \
            diagonal(W["mv"], V3, w["mdst_wv"])
        at = 0
        W["row_at"] = {}
        for n in ("mdst_bs", "proj_bs", "f1_bs", "f2_bs"):
            wide = w[n].shape[0]
            loads.append((W["rows"], W["rows"][0:1, at:at + wide], row_of(w[n], wide)))
            W["row_at"][n] = (at, at + wide)
            at += wide
        for n in ("ln1", "ln2"):
            loads += [(W[n], W[n][0:S, 0:1], col_of(w[n + "_w0"])), (W[n], W[n][0:S, 1:2], col_of(w[n + "_b0"]))]
            loads += [(W[n], W[n][V * i:V * i + V, 2:3], col_of(w[n + "_w1"])) for i in range(3)]
        load_weights(nc, m, k, "w1", loads)
        turned = mm.sem("w1_permuted")
        with nc.Block() as block:
            @block.vector
            def _(dve):
                dve.memset(W["eps"][:], EPS).then_inc(turned, 1)
                dve.tensor_copy(W["usv"][:].rearrange("u (w v) -> u w v", v=V),
                                rsv[:].rearrange("u v w -> u w v")).then_inc(turned, 1)
                dve.tensor_copy(W["uvs"][:].rearrange("v (w u) -> v w u", u=V),
                                rvs[:].rearrange("v u w -> v w u")).then_inc(turned, 1)
                dve.wait_ge(turned, 3)
        scale_all(nc, m, k, "w1", [(W["uss"][:], INV64), (W["uvv"][:], INV_SQRT3 * INV32),
                                   (W["usv"][:], INV_SQRT2048), (W["uvs"][:], INV_SQRT2048),
                                   (W["lus"][:], INV8), (W["luv"][:], INV_SQRT32)])
    return W


def weights2(nc, m, k, ps, w, W):
    for n, shape in dict(r1=[128, 128], r2=[128, 128], avg=[128, 128], rb=[128, 8], r3=[128, 224], ls=[97, 136],
                         la=[S, V], lb=[V3, V3], lc=[V3, 128], ad=[128, S]).items():
        W[n] = m.sb("w_" + n, shape)
    W["off3"], W["one3"] = m.sb("w_off3", [3, 224], BF16), m.sb("w_one3", [3, R], BF16)
    loads = []
    for h in range(2):
        lo = slice(S * h, S * h + S)
        loads += [(W["r1"], W["r1"][lo, lo], w["rw1"]), (W["r2"], W["r2"][lo, lo], w["rw2"]),
                  (W["r3"], W["r3"][lo, :], w["rw3"])]
        for j, n in enumerate(("rb1", "rg1", "rbe1", "rb2", "rg2", "rbe2")):
            loads.append((W["rb"], W["rb"][lo, j:j + 1], col_of(w[n])))
    loads += [(W["ls"], W["ls"][0:96, 0:128], w["lin_ws"]), (W["ls"], W["ls"][96:97, 0:128], row_of(w["lin_bs"], 128)),
              (W["la"], W["la"][:], w["lin_wv"][0:S, :]),
              (W["ad"], W["ad"][:], w["alpha_dot"].rearrange("(a h) k -> a (h k)", a=1).broadcast_to([128, S]))]
    loads += diagonal(W["lb"], 0, w["lin_wv"][S:S + V, :])
    for j, i in enumerate((1, 2, 0, 1)):
        loads.append((W["lc"], W["lc"][V * i:V * i + V, V * j:V * j + V], w["lin_wv"][S + V:S + 2 * V, :]))
    rest, part, total = (m.sb("w2_" + n, [3, 224]) for n in ("rest", "part", "total"))
    loads.append((rest, rest[:], w["roff"].rearrange("(a n) -> a n", a=1).broadcast_to([3, 224])))
    load_weights(nc, m, k, "w2", loads, [W["avg"]])
    scale_all(nc, m, k, "w2", [(W["la"][:], SQ3), (W["lc"][:], SQ3 / SQ2)])
    done, turned = m.sem("w2_done"), m.sem("w2_turned")
    mean = m.sb("w2_mean", [128, 8])
    tmp = m.sb("w2_tmp", [97, S])
    with nc.Block() as block:
        @block.vector
        def _(dve):
            n = 0

            def step(ins):
                nonlocal n
                n += 1
                ins.then_inc(done, 1)
                dve.wait_ge(done, n)
            for h in range(2):
                lo = slice(S * h, S * h + S)
                step(dve.memset(W["avg"][lo, lo], 1.0 / S))
            for j, r in enumerate(("r1", "r2")):
                step(dve.tensor_reduce(mean[:, j:j + 1], W[r][:], AX.X, ALU.add))
                step(dve.tensor_scalar(mean[:, j:j + 1], mean[:, j:j + 1], 1.0 / S, None, ALU.mult))
                for h in range(2):
                    lo = slice(S * h, S * h + S)
                    step(dve.tensor_scalar(W[r][lo, lo], W[r][lo, lo], mean[lo, j:j + 1], None, ALU.subtract))
            step(dve.tensor_tensor(tmp[:], W["ls"][:, 0:S], W["ad"][0:97, :], ALU.mult))
            step(dve.tensor_reduce(W["ls"][:, 128:136], tmp[:].rearrange("u (h k) -> u h k", h=HEADS), AX.X, ALU.add))
            step(dve.tensor_scalar(W["ls"][:, 128:136], W["ls"][:, 128:136], 0.2, None, ALU.mult))
            step(dve.tensor_scalar(W["ad"][:], W["ad"][:], 0.8, None, ALU.mult))
            step(dve.memset(W["one3"][:], 1.0))
            step(dve.memset(total[:], 0.0))
            for i in range(3):
                step(dve.tensor_copy(W["off3"][:], rest[:]))
                step(dve.tensor_copy(part[:], W["off3"][:]))
                step(dve.scalar_tensor_tensor(out=total[:], in0=part[:], scalar=k["ident"][0:3, i:i + 1], in1=total[:],
                                              op0=ALU.mult, op1=ALU.add))
                step(dve.tensor_tensor(rest[:], rest[:], part[:], ALU.subtract))
            step(dve.tensor_copy(W["off3"][:], total[:]))
            dve.wait_ge(turned, 1)
            step(dve.tensor_tensor(W["rb"][:, 0:6:3], W["rb"][:, 0:6:3], ps[:, 0, 0:6:3], ALU.subtract))

        @block.tensor
        def _(pe):
            pe.wait_ge(done, 2)
            pe.matmul(ps[:, 0, 0:6], W["avg"][:], W["rb"][:, 0:6], start=True, stop=True).then_inc(turned, 1)
            pe.wait_ge(turned, 1)


def directions(nc, m, k, W, a3, yx):
    own = ExitStack()
    with own:
        mm = Mem(nc, own)
        sq, tot = mm.sb("dir_sq", [R, 3, ET]), mm.sb("dir_tot", [R, 2, ET])
        tiny = mm.sb("dir_tiny", [R, 1])
        vec, root = mm.sem("dir_vec"), mm.sem("dir_root")
        with nc.Block() as block:
            @block.vector
            def _(dve):
                n = 0

                def step(ins):
                    nonlocal n
                    n += 1
                    ins.then_inc(vec, 1)
                    dve.wait_ge(vec, n)
                step(dve.memset(tiny[:], 1e-12))
                step(dve.tensor_tensor(sq[:], a3[:], a3[:], ALU.mult))
                step(dve.tensor_tensor(tot[:, 0, :], sq[:, 0, :], sq[:, 1, :], ALU.add))
                step(dve.tensor_tensor(tot[:, 0, :], tot[:, 0, :], sq[:, 2, :], ALU.add))
                dve.wait_ge(root, 1)
                step(dve.reciprocal(tot[:, 0, :], tot[:, 1, :]))
                for j in range(5):
                    step(dve.tensor_tensor(yx[:, j, :], a3[:, j % 3, :], tot[:, 0, :], ALU.mult))

            @block.scalar
            def _(act):
                act.wait_ge(vec, 4)
                act.activation(tot[:, 1, :], tot[:, 0, :], ACT.Sqrt, bias=tiny[:]).then_inc(root, 1)
                act.wait_ge(root, 1)


def layer1_edges(nc, m, k, ps, W, TS, TD, srcI, dstI, H, yx, a_sb, VAL):
    own = ExitStack()
    GP = ET // GT // 2
    with own:
        mm = Mem(nc, own)
        sb = mm.sb
        at = sb("e1_at", [R, 2, 2, GT], I32)
        rows = sb("e1_rows", [R, 2, 2, GT, X])
        hh = sb("e1_h", [128, 2, GT * R])
        m_ = sb("e1_m", [R, 2, GT, X])
        d1, d2 = sb("e1_d1", [R, GT, 97]), sb("e1_d2", [R, GT, S])
        d3, d5, dot = (sb("e1_" + n, [R, GT, 3, V]) for n in ("d3", "d5", "dot"))
        T = {n: sb("e1_T" + n, [r, GT * R]) for n, r in (("1", 97), ("2", S), ("3", V3), ("5", V3))}
        silu, asum = sb("e1_silu", [R, GT, S]), sb("e1_asum", [R, GT, HEADS])
        cA, cB, cC = (sb("e1_" + n, [R, GT, 3, V]) for n in ("cA", "cB", "cC"))
        val = sb("e1_val", [R, 2, GT, X])
        here = [[mm.sem(f"e1_here{p}{c}") for c in range(2 * GT)] for p in range(2)]
        at_ready = [mm.sem(f"e1_at_ready{p}") for p in range(2)]
        settle = [Settle(mm, k, f"e1_gather{p}") for p in range(2)]
        h_here = [mm.sem(f"e1_h_here{q}") for q in range(2)]
        stored = [mm.sem(f"e1_stored{p}") for p in range(2)]
        one = mm.sem("e1_one")
        added = [mm.sem(f"e1_added{p}") for p in range(2)]
        pe_s = [Steps(mm, k, f"e1_pe{p}", ["w", "t0", "t1", "t2", "ls", "lv"]) for p in range(2)]
        ac_s = [Steps(mm, k, f"e1_act{p}", ["t0", "t1", "t2", "t3", "silu", "vs"]) for p in range(2)]
        A_, B_ = 4, 8
        turned = [mm.sem(f"e1_turned{p}") for p in range(2)]
        sa, sc = [mm.sem(f"e1_front{p}") for p in range(2)], [mm.sem(f"e1_back{p}") for p in range(2)]

        def gather(pool, p, t):
            pool.wait_ge(added[p], t)
            for c in range(2 * GT):
                pool.wait_ge(here[p][c], 16 * t)
            settle[p](pool, 2 * t)
            pool.tensor_copy(at[:, p, 0, :], srcI[:, 0, bass.ds(8 * t + 4 * p, GT)])
            pool.tensor_copy(at[:, p, 1, :], dstI[:, 0, bass.ds(8 * t + 4 * p, GT)]).then_inc(at_ready[p], 1)
            pool.wait_ge(at_ready[p], t + 1)
            settle[p](pool, 2 * t + 1)
            for q, table in enumerate((TS, TD)):
                for c in range(GT):
                    pool.indirect_dma_start(rows[:, p, q, c, :], None, table, bass.IndirectOffsetOnAxis(
                        ap=at[:, p, q, c:c + 1], axis=0)).then_inc(here[p][GT * q + c], 16)

        def front(dve, p, t):
            v = Chain(dve, sa[p], A_, t)
            for c in range(2 * GT):
                dve.wait_ge(here[p][c], 16 * t + 16)
            dve.tensor_tensor(m_[:, p], rows[:, p, 0], rows[:, p, 1], ALU.add).then_inc(added[p], 1)
            dve.wait_ge(added[p], t + 1)
            s = m_[:, p, :, 0:S]
            vv = m_[:, p, :, S:X].rearrange("n c (i u) -> n c i u", i=3)
            yv = bc(yx[:, 0:3, bass.ds(8 * t + 4 * p, GT)].rearrange("n i c -> n c i"), V, 3)
            dve.wait_ge(turned[1 - p], t + p)
            v(dve.tensor_tensor(dot[:], vv, yv, ALU.mult))
            v.sync()
            v(dve.tensor_tensor(dot[:, :, 0, :], dot[:, :, 0, :], dot[:, :, 1, :], ALU.add))
            pe_s[p].wait(dve, t, "w")
            w = [ps[0:R, b, 0:448].rearrange("n (c w) -> n c w", c=2) for b in range(2)]
            cc = [slice(0, 2), slice(2, 4)]
            for b in range(2):
                dve.tensor_tensor(d1[:, cc[b], 0:S], w[b][:, :, 0:S], s[:, cc[b], :], ALU.mult)
                dve.tensor_tensor(d2[:, cc[b], :], w[b][:, :, S:2 * S], s[:, cc[b], :], ALU.mult)
            v.sync()
            v(dve.tensor_tensor(dot[:, :, 0, :], dot[:, :, 0, :], dot[:, :, 2, :], ALU.add))
            for b in range(2):
                dve.tensor_tensor(d3[:, cc[b]], bc(w[b][:, :, 128:160], 3, 2), vv[:, cc[b]], ALU.mult)
                dve.tensor_tensor(d5[:, cc[b]], bc(w[b][:, :, 192:224], 3, 2), vv[:, cc[b]], ALU.mult)
            v.sync()
            for b in range(2):
                last = dve.tensor_tensor(d1[:, cc[b], S:S + V], w[b][:, :, 160:192], dot[:, cc[b], 0, :], ALU.mult)
            v(last)
            v.end()

        def back(dve, p, t):
            v = Chain(dve, sc[p], B_, t)
            ac_s[p].wait(dve, t, "silu")
            v(dve.tensor_tensor(silu[:], silu[:], bc(W["ad"][0:R, :], GT, 1), ALU.mult))
            v.sync()
            v(dve.tensor_reduce(asum[:], silu[:].rearrange("n c (h k) -> n c h k", h=HEADS), AX.X, ALU.add))
            y = [bc(yx[:, j:j + 3, bass.ds(8 * t + 4 * p, GT)].rearrange("n i c -> n c i"), V, 3) for j in range(3)]
            pe_s[p].wait(dve, t, "lv")
            v.sync()
            v(dve.tensor_tensor(a_sb[:, bass.ds(8 * t + 4 * p, GT), :], asum[:],
                                ps[0:R, 7, 0:GT * HEADS].rearrange("n (c h) -> n c h", c=GT), ALU.add))
            lv = [ps[0:R, 5 + b, :].rearrange("n (c w) -> n c w", c=2) for b in range(2)]
            for b in range(2):
                cc = slice(2 * b, 2 * b + 2)
                part = lambda lo: lv[b][:, :, lo:lo + V3].rearrange("n c (i u) -> n c i u", i=3)
                dve.tensor_tensor(cC[:, cc], bc(lv[b][:, :, 0:V], 3, 2), y[0][:, cc], ALU.mult)
                dve.tensor_tensor(cA[:, cc], part(128), y[2][:, cc], ALU.mult)
                last = dve.tensor_tensor(cB[:, cc], part(160), y[1][:, cc], ALU.mult)
            v(last)
            v.sync()
            for b in range(2):
                cc = slice(2 * b, 2 * b + 2)
                part = lambda lo: lv[b][:, :, lo:lo + V3].rearrange("n c (i u) -> n c i u", i=3)
                v(dve.tensor_tensor(cC[:, cc], part(V), cC[:, cc], ALU.add))
            v(dve.tensor_tensor(cA[:], cA[:], cB[:], ALU.subtract))
            v.sync()
            dve.wait_ge(stored[p], 16 * t)
            ac_s[p].wait(dve, t, "vs")
            v(dve.tensor_tensor(val[:, p, :, S:X].rearrange("n c (i u) -> n c i u", i=3), cA[:], cC[:], ALU.add))
            v.end()

        with nc.Block() as block:
            @block.sync
            def _(sp):
                def load(q, t):
                    gate(sp, k)
                    sp.dma_start(hh[:, q, :], H[bass.ds(t, 1)].rearrange("g q n -> (g q) n")).then_inc(h_here[q], 16)
                load(0, 0)
                load(1, 1)

                def store(t):
                    for p in range(2):
                        gate(sp, k)
                        sp.wait_ge(sc[p], B_ * t + B_)
                        sp.dma_start(VAL[bass.ds(2 * t + p, 1)].rearrange("g r w -> (g r) w"),
                                     val[:, p].rearrange("r c w -> r (c w)")).then_inc(stored[p], 16)

                with sp.Fori(0, GP // 2 - 1) as t2:
                    for q in range(2):
                        store(2 * t2 + q)
                        load(q, 2 * t2 + q + 2)
                for q in range(2):
                    store(GP - 2 + q)
                for p in range(2):
                    sp.wait_ge(stored[p], 16 * GP)

            @block.gpsimd
            def _(pool):
                gather(pool, 0, 0)
                gather(pool, 1, 0)
                with pool.Fori(0, GP - 1) as t:
                    for p in range(2):
                        gather(pool, p, t + 1)

            @block.vector
            def _(dve):
                for c in range(GT):
                    last = dve.tensor_copy(d1[:, c, 96:97], k["ones"][0:R, 0:1])
                last.then_inc(one, 1)
                dve.wait_ge(one, 1)
                front(dve, 0, 0)
                with dve.Fori(0, GP - 1) as t:
                    front(dve, 1, t)
                    back(dve, 0, t)
                    front(dve, 0, t + 1)
                    back(dve, 1, t)
                front(dve, 1, GP - 1)
                back(dve, 0, GP - 1)
                back(dve, 1, GP - 1)

            @block.tensor
            def _(pe):
                I = k["ident"]

                def weights(p, t, q, t2):
                    if p == 0:
                        pe.wait_ge(h_here[q], 16 * t2 + 16)
                        pe.wait_ge(sa[1], A_ * t)
                    else:
                        pe.wait_ge(sa[0], A_ * t + A_)
                    for c in range(GT):
                        to = ps[0:R, c // 2, 224 * (c % 2):224 * (c % 2) + 224]
                        pe.matmul(to, hh[S * p:S * p + S, q, R * c:R * c + R], W["r3"][S * p:S * p + S, :],
                                  start=True, stop=False)
                        last = pe.matmul(to, W["one3"][:], W["off3"][:], start=False, stop=True)
                    pe_s[p].done(last, "w")

                def maps(p, t):
                    pe.wait_ge(sa[p], A_ * t + A_)
                    for j, d in enumerate((d1, d2, d3, d5)):
                        if j >= 2:
                            ac_s[p].wait(pe, t, f"t{j - 2}")
                        for c in range(GT):
                            src = d[:, c].rearrange("n i u -> n (i u)") if j > 1 else d[:, c, :]
                            wide = src.shape[1]
                            last = pe.transpose(ps[0:wide, 2 + j % 2, R * c:R * c + R], src, I[0:R, 0:R])
                        if j < 3:
                            pe_s[p].done(last, f"t{j}")
                        else:
                            last.then_inc(turned[p], 1)
                    ac_s[p].wait(pe, t, "t3")
                    if p == 0:
                        pe.wait_ge(sc[1], B_ * t)
                        pe.wait_ge(ac_s[1].sem, 6 * t)
                    else:
                        pe.wait_ge(sc[0], B_ * t + B_)
                        pe.wait_ge(ac_s[0].sem, 6 * t + 6)
                    for c in range(GT):
                        e = slice(R * c, R * c + R)
                        last = pe.matmul(ps[0:R, 4, 128 * c:128 * c + 128], T["1"][:, e], W["ls"][:, 0:128],
                                         start=True, stop=True)
                    pe_s[p].done(last, "ls")
                    for c in range(GT):
                        e = slice(R * c, R * c + R)
                        lv = ps[0:R, 5 + c // 2, 256 * (c % 2):256 * (c % 2) + 256]
                        pe.matmul(ps[0:R, 7, HEADS * c:HEADS * c + HEADS], T["1"][:, e], W["ls"][:, 128:136],
                                  start=True, stop=True)
                        pe.matmul(lv[:, 0:V], T["2"][:, e], W["la"][:], start=True, stop=True)
                        pe.matmul(lv[:, V:128], T["3"][:, e], W["lb"][:], start=True, stop=True)
                        last = pe.matmul(lv[:, 128:256], T["5"][:, e], W["lc"][:], start=True, stop=True)
                    pe_s[p].done(last, "lv")

                weights(0, 0, 0, 0)
                with pe.Fori(0, GP // 2 - 1) as t2:
                    for q in range(2):
                        weights(1, 2 * t2 + q, q, t2)
                        maps(0, 2 * t2 + q)
                        weights(0, 2 * t2 + q + 1, 1 - q, t2 + q)
                        maps(1, 2 * t2 + q)
                t2 = GP // 2 - 1
                for q in range(2):
                    weights(1, 2 * t2 + q, q, t2)
                    maps(0, 2 * t2 + q)
                    if q == 0:
                        weights(0, 2 * t2 + 1, 1, t2)
                    maps(1, 2 * t2 + q)

            @block.scalar
            def _(act):
                with act.Fori(0, GP) as t:
                    for p in range(2):
                        for j, n in enumerate("1235"):
                            if j < 3:
                                pe_s[p].wait(act, t, f"t{j}")
                            else:
                                act.wait_ge(turned[p], t + 1)
                            ac_s[p].done(act.activation(T[n][:], ps[0:T[n].shape[0], 2 + j % 2, 0:GT * R], ACT.Copy),
                                         f"t{j}")
                        pe_s[p].wait(act, t, "ls")
                        ls = ps[0:R, 4, :].rearrange("n (c w) -> n c w", c=GT)
                        if p == 0:
                            act.wait_ge(sc[1], B_ * t)
                        else:
                            act.wait_ge(sc[0], B_ * t + B_)
                        ac_s[p].done(act.activation(silu[:], ls[:, :, 0:S], ACT.Silu), "silu")
                        act.wait_ge(stored[p], 16 * t)
                        ac_s[p].done(act.activation(val[:, p, :, 0:S], ls[:, :, S:128], ACT.Copy), "vs")


def softmax_weights(nc, m, k, ps, a_sb, dst, scratch):
    own = ExitStack()
    TC = ET // CH
    NB = TC // GT
    HP = HEADS * CH
    with own:
        mm = Mem(nc, own)
        sb = mm.sb
        aT = sb("sm_aT", [HP, EC])
        d = sb("sm_dst", [HP, EC], I32)
        mask = d[:].bitcast(F32)
        stage = sb("sm_stage", [R, 2, GT, HP])
        penalty = sb("sm_penalty", [HP, 2, 1250])
        ends = sb("sm_ends", [HP, 4])
        flags = sb("sm_flags", [HEADS, 8, CH])
        marks = sb("sm_marks", [HEADS, 2, CH], I32)
        vec, turned, kept = mm.sem("sm_vec"), mm.sem("sm_turned"), mm.sem("sm_kept")
        here, moved, back, done = mm.sem("sm_here"), mm.sem("sm_moved"), mm.sem("sm_back"), mm.sem("sm_done")
        again = mm.sem("sm_again")
        chunk = dst.rearrange("(c n) -> c n", c=CH)

        def load_dst(sp, sem):
            for c in range(CH):
                sp.dma_start(d[HEADS * c:HEADS * c + HEADS, :], chunk[c:c + 1, :].broadcast_to([HEADS, EC])
                             ).then_inc(sem, 16)

        with nc.Block() as block:
            @block.sync
            def _(sp):
                load_dst(sp, here)
                for j, at in enumerate((0, EC - 1)):
                    sp.dma_start(marks[:, j, :], chunk[:, at:at + 1].rearrange("c n -> n c").broadcast_to([HEADS, CH]),
                                 allow_slow_non_contiguous=True).then_inc(here, 16)
                sp.wait_ge(here, 16 * (CH + 2))

            @block.vector
            def _(dve):
                v4 = a_sb[:].rearrange("r (c j) h -> r j c h", c=CH)
                for b in range(NB):
                    if b >= 2:
                        dve.wait_ge(turned, b - 1)
                    dve.tensor_copy(stage[:, b % 2].rearrange("r j (c h) -> r j c h", c=CH),
                                    v4[:, GT * b:GT * b + GT]).then_inc(vec, 1)
                dve.wait_ge(vec, NB)

            @block.tensor
            def _(pe):
                for b in range(NB):
                    pe.wait_ge(vec, b + 1)
                    if b >= 2:
                        pe.wait_ge(kept, b - 1)
                    for j in range(GT):
                        last = pe.transpose(ps[:, b % 2, R * j:R * j + R], stage[:, b % 2, j, :],
                                            k["ident"][0:R, 0:R])
                    last.then_inc(turned, 1)

            @block.scalar
            def _(act):
                for b in range(NB):
                    act.wait_ge(turned, b + 1)
                    act.activation(aT[:, GT * R * b:GT * R * b + GT * R], ps[:, b % 2, 0:GT * R], ACT.Copy
                                   ).then_inc(kept, 1)
                act.wait_ge(kept, NB)

        with nc.Block() as block:
            @block.vector
            def _(dve):
                n = NB

                def step(ins):
                    nonlocal n
                    n += 1
                    ins.then_inc(vec, 1)
                    dve.wait_ge(vec, n)
                step(dve.tensor_copy(ends[:, 0:1], d[:, 0:1]))
                step(dve.tensor_copy(ends[:, 1:2], d[:, EC - 1:EC]))
                step(dve.tensor_tensor(mask[:, 0:EC - 1], d[:, 0:EC - 1], d[:, 1:EC], ALU.not_equal))
                step(dve.tensor_scalar(mask[:, 0:EC - 1], mask[:, 0:EC - 1], -BIG, None, ALU.mult))
                step(dve.tensor_tensor_scan(aT[:, 1:EC], mask[:, 0:EC - 1], aT[:, 1:EC], aT[:, 0:1], ALU.add, ALU.max))
                step(dve.tensor_tensor_scan(aT[:, EC - 2::-1], mask[:, EC - 2::-1], aT[:, EC - 2::-1],
                                            aT[:, EC - 1:EC], ALU.add, ALU.max))
                step(dve.tensor_copy(ends[:, 2:3], aT[:, 0:1]))
                step(dve.tensor_copy(ends[:, 3:4], aT[:, EC - 1:EC]))
                dve.wait_ge(moved, 64)
                f = [flags[:, j, :] for j in range(8)]
                step(dve.memset(flags[:, 2:8, :], -BIG))
                step(dve.tensor_tensor(f[2][:, 1:CH], marks[:, 1, 0:CH - 1], marks[:, 0, 1:CH], ALU.not_equal))
                step(dve.tensor_scalar(f[2][:, 1:CH], f[2][:, 1:CH], -BIG, None, ALU.mult))
                step(dve.tensor_tensor(f[3], marks[:, 0, :], marks[:, 1, :], ALU.not_equal))
                step(dve.tensor_scalar(f[3], f[3], -BIG, None, ALU.mult))
                step(dve.tensor_tensor(f[6], f[2], f[3], ALU.add))
                step(dve.tensor_tensor_scan(f[4], f[6], f[1], -BIG, ALU.add, ALU.max))
                step(dve.tensor_tensor(f[7][:, 0:CH - 1], f[2][:, 1:CH], f[3][:, 0:CH - 1], ALU.add))
                step(dve.tensor_tensor_scan(f[5][:, ::-1], f[7][:, ::-1], f[0][:, ::-1], -BIG, ALU.add, ALU.max))
                step(dve.memset(flags[:, 6:8, :], -BIG))
                step(dve.tensor_tensor(f[6][:, 1:CH], f[4][:, 0:CH - 1], f[2][:, 1:CH], ALU.add))
                step(dve.tensor_tensor(f[7][:, 0:CH - 1], f[5][:, 1:CH], f[2][:, 1:CH], ALU.add))
                dve.wait_ge(back, 32)
                dve.wait_ge(again, 16 * CH)

            @block.sync
            def _(sp):
                sp.wait_ge(vec, NB + 8)
                for j in range(2):
                    sp.dma_start(scratch[j:j + 1, :].rearrange("a q -> q a"), ends[:, 2 + j:3 + j],
                                 allow_slow_non_contiguous=True).then_inc(moved, 16)
                sp.wait_ge(moved, 32)
                for j in range(2):
                    sp.dma_start(flags[:, j, :], scratch[j].rearrange("(c h) -> h c", c=CH),
                                 allow_slow_non_contiguous=True).then_inc(moved, 16)
                sp.wait_ge(moved, 64)
                load_dst(sp, again)
                sp.wait_ge(vec, NB + 20)
                for j in range(2):
                    sp.dma_start(scratch[2 + j].rearrange("(c h) -> h c", c=CH), flags[:, 6 + j, :],
                                 allow_slow_non_contiguous=True).then_inc(moved, 16)
                sp.wait_ge(moved, 96)
                for j in range(2):
                    sp.dma_start(ends[:, 2 + j:3 + j], scratch[2 + j:3 + j, :].rearrange("a q -> q a"),
                                 allow_slow_non_contiguous=True).then_inc(back, 16)
                sp.wait_ge(back, 32)

        with nc.Block() as block:
            @block.vector
            def _(dve):
                n = 0

                def step(ins):
                    nonlocal n
                    n += 1
                    ins.then_inc(done, 1)
                    dve.wait_ge(done, n)
                W_ = 1250
                for a in range(0, EC, W_):
                    for j in range(2):
                        p = penalty[:, j, :]
                        step(dve.tensor_scalar(p, d[:, a:a + W_], ends[:, j:j + 1], -BIG, ALU.not_equal, ALU.mult))
                        step(dve.scalar_tensor_tensor(out=aT[:, a:a + W_], in0=p, scalar=ends[:, 2 + j:3 + j],
                                                      in1=aT[:, a:a + W_], op0=ALU.add, op1=ALU.max))
                v4 = a_sb[:].rearrange("r (c j) h -> r j c h", c=CH)
                base = n
                for b in range(NB):
                    dve.wait_ge(turned, NB + b + 1)
                    dve.tensor_tensor(v4[:, GT * b:GT * b + GT], v4[:, GT * b:GT * b + GT],
                                      ps[0:R, b % 2, :].rearrange("r (j c h) -> r j c h", j=GT, c=CH), ALU.subtract
                                      ).then_inc(done, 1)
                dve.wait_ge(done, base + NB)

            @block.tensor
            def _(pe):
                fixed = 4 * (EC // 1250)
                for b in range(NB):
                    pe.wait_ge(done, fixed + max(b - 1, 0))
                    for j in range(GT):
                        at = GT * R * b + R * j
                        last = pe.transpose(ps[0:R, b % 2, HP * j:HP * j + HP], aT[:, at:at + R], k["ident"][:, :])
                    last.then_inc(turned, 1)

            @block.scalar
            def _(act):
                fixed = 4 * (EC // 1250)
                act.wait_ge(done, fixed + NB)
                per = ET // 4
                for q in range(4):
                    w = a_sb[:, per * q:per * q + per, :].rearrange("r t h -> r (t h)")
                    act.activation(w, w, ACT.Exp).then_inc(kept, 1)
                act.wait_ge(kept, NB + 4)


def layer1_sums(nc, m, k, ps, a_sb, dstF, dst, VAL, sums):
    own = ExitStack()
    with own:
        mm = Mem(nc, own)
        sc = Scatter(nc, mm, k, ps, "e2", MSG1, dstF, dst, sums, 0)
        val = mm.sb("e2_val", [R, 2, GT * X])
        here = [mm.sem(f"e2_here{p}") for p in range(2)]
        GP = ET // GT // 2

        def load(sp, p, t):
            gate(sp, k)
            sp.wait_ge(sc.u_ready[p], t)
            sp.dma_start(val[:, p, :], VAL[bass.ds(2 * t + p, 1)].rearrange("g r w -> (g r) w")
                         ).then_inc(here[p], 16)

        def messages(dve, p, t):
            sc.equal(dve, p, t)
            gate(dve, k)
            dve.wait_ge(here[p], 16 * t + 16)
            u, v = sc.u[:, p], val[:, p, :].rearrange("r (c w) -> r c w", c=GT)
            e = a_sb[:, bass.ds(8 * t + 4 * p, GT), :]
            for lo, per in ((0, 8), (S, 4), (S + V, 4), (S + 2 * V, 4)):
                at = slice(lo, lo + HEADS * per)
                dve.tensor_tensor(u[:, :, at].rearrange("r c (h q) -> r c h q", h=HEADS),
                                  v[:, :, at].rearrange("r c (h q) -> r c h q", h=HEADS), bc(e, per, 3), ALU.mult)
            dve.tensor_scalar(u[:, :, X:MSG1], e, 1.0, None, ALU.mult).then_inc(sc.u_ready[p], 1)

        run_edges(nc, sc, messages, GP, load)


PER2 = 29


def weights3(nc, m, k, w, W):
    for n, shape in dict(pws=[S, S], pwv=[V3, V3], f1s=[S, 192], f1v=[V3, 192], f2s=[128, S], f2a=[128, S],
                         f2b=[S, V]).items():
        W[n] = m.sb("w_" + n, shape)
    loads = [(W["pws"], W["pws"][:], w["proj_ws"]), (W["f1s"], W["f1s"][:], w["f1_ws"]),
             (W["f2s"], W["f2s"][:], w["f2_ws"]), (W["f2b"], W["f2b"][:], w["f2_wv"])]
    loads += diagonal(W["pwv"], 0, w["proj_wv"])
    loads += [(W["f1v"], W["f1v"][V * i:V * i + V, S * i:S * i + S], w["f1_wv"]) for i in range(3)]
    loads += [(W["f2a"], W["f2a"][S * i:S * i + S, V * i:V * i + V], w["f2_wv"]) for i in range(2)]
    load_weights(nc, m, k, "w3", loads)


def node_update1(nc, m, k, ps, W, X1, nodevec, sums, out):
    own = ExitStack()
    PAIRS = NT // 2
    with own:
        mm = Mem(nc, own)
        two = lambda name, r, *shape: mm.sb("n2_" + name, [r, 2, *shape])
        xt, ag = mm.sb("n2_x", [R, 2, 2, X]), mm.sb("n2_ag", [R, 2, 2, COPIES, MSG1])
        nv, y2 = mm.sb("n2_nv", [R, 2, 2, 2]), mm.sb("n2_y2", [R, 2, 2, X])
        a, rec = two("a", R, MSG1), two("rec", R, HEADS)
        x2, sq, norm = two("x2", R, X), two("sq", R, V3), two("norm", R, X)
        stat, st2 = two("stat", R, 2, 6), two("st2", R, 16)
        sT, vT, sT2, vT2 = two("sT", S, R), two("vT", V3, R), two("sT2", S, R), two("vT2", V3, R)
        sc, sg, fv = two("sc", R, 128), two("sg", R, S), two("fv", R, 192)
        scT, fvT, fwT = two("scT", 128, R), two("fvT", 128, R), two("fwT", S, R)
        y = two("y", R, X)
        here = [[mm.sem(f"n2_here{q}{p}") for p in range(2)] for q in range(2)]
        stored = [[mm.sem(f"n2_stored{q}{p}") for p in range(2)] for q in range(2)]
        vec, marks = [mm.sem(f"n2_vec{p}") for p in range(2)], {}
        pe_s = [Steps(mm, k, f"n2_pe{p}", ["turned", "proj", "norm", "f1", "mid", "f2"]) for p in range(2)]
        ac_s = [Steps(mm, k, f"n2_act{p}", ["turned", "root1", "norm", "gates", "mid", "root2"]) for p in range(2)]
        bank = [[ps[:, 4 * p + b, :] for b in range(4)] for p in range(2)]

        def got(eng, t, p, name):
            marked(eng, k, vec[p], PER2, marks, t, name)

        with nc.Block() as block:
            @block.vector
            def _(dve):
                def pair(t4, q):
                    t = 2 * t4 + q
                    vs = [Vector(k, vec[p], PER2, marks, t) for p in range(2)]
                    both = [(p, vs[p]) for p in range(2)]
                    for p, v in both:
                        v.eng = dve
                        gate(dve, k)
                        dve.wait_ge(here[q][p], 96 * t4 + 96)
                        v(dve.tensor_tensor(a[:, p, :], ag[:, q, p, 0, :], ag[:, q, p, 1, :], ALU.add))
                    for c in (2, 3):
                        for p, v in both:
                            v.sync()
                            v(dve.tensor_tensor(a[:, p, :], a[:, p, :], ag[:, q, p, c, :], ALU.add))
                    for p, v in both:
                        v(dve.tensor_scalar(nv[:, q, p, 1:2], nv[:, q, p, 0:1], 0.5, None, ALU.mult))
                        v.sync()
                        v(dve.tensor_scalar(rec[:, p, :], a[:, p, X:MSG1], 1e-12, None, ALU.add))
                    for p, v in both:
                        v.sync()
                        v(dve.reciprocal(rec[:, p, :], rec[:, p, :]))
                    for p, v in both:
                        v.sync()
                        at = a[:, p, 0:S].rearrange("n (h c) -> n h c", h=HEADS)
                        v(dve.tensor_tensor(at, at, bc(rec[:, p, :], 8, 2), ALU.mult))
                        for i in range(3):
                            at = a[:, p, S + V * i:S + V * i + V].rearrange("n (h c) -> n h c", h=HEADS)
                            v(dve.tensor_tensor(at, at, bc(rec[:, p, :], 4, 2), ALU.mult))
                        v.mark("weighted")
                    for p, v in both:
                        pe_s[p].wait(dve, t, "proj")
                        v(dve.tensor_tensor(x2[:, p, :], xt[:, q, p, :], bank[p][1][0:R, 0:X], ALU.add))
                    for p, v in both:
                        v.sync()
                        v(dve.tensor_tensor(sq[:, p, :], x2[:, p, S:X], x2[:, p, S:X], ALU.mult))
                        v(dve.bn_stats(stat[:, p, 0, :], x2[:, p, 0:S]))
                    for p, v in both:
                        v.sync()
                        v(dve.tensor_reduce(st2[:, p, 2:3], sq[:, p, :], AX.X, ALU.add))
                        v(dve.bn_aggr(st2[:, p, 0:2], stat[:, p, 0, :]))
                    for p, v in both:
                        v.sync()
                        v(dve.tensor_scalar(st2[:, p, 2:3], st2[:, p, 2:3], 1.0 / V3, None, ALU.mult))
                        v.mark("var1")
                    for p, v in both:
                        v(dve.tensor_tensor(y[:, p, :], xt[:, q, p, :], x2[:, p, :], ALU.add))
                    for p, v in both:
                        ac_s[p].wait(dve, t, "root1")
                        v(dve.reciprocal(st2[:, p, 6:8], st2[:, p, 4:6]))
                    for p, v in both:
                        v.sync()
                        v(dve.tensor_scalar(norm[:, p, 0:S], x2[:, p, 0:S], st2[:, p, 0:1], st2[:, p, 6:7],
                                            ALU.subtract, ALU.mult))
                        v(dve.tensor_scalar(norm[:, p, S:X], x2[:, p, S:X], st2[:, p, 7:8], None, ALU.mult))
                        v.mark("norm")
                    for p, v in both:
                        ac_s[p].wait(dve, t, "gates")
                        v(dve.tensor_scalar(sg[:, p, :], sg[:, p, :], 1.0, nv[:, q, p, 1:2], ALU.add, ALU.mult))
                    for p, v in both:
                        v.sync()
                        v(dve.tensor_tensor(fv[:, p, :].rearrange("n (i u) -> n i u", i=3),
                                            bank[p][3][0:R, 0:192].rearrange("n (i u) -> n i u", i=3),
                                            bc(sg[:, p, :], 3, 1), ALU.mult))
                        v.mark("gated")
                    for p, v in both:
                        pe_s[p].wait(dve, t, "f2")
                        v(dve.scalar_tensor_tensor(out=y[:, p, :], in0=bank[p][1][0:R, 256:256 + X],
                                                   scalar=nv[:, q, p, 0:1], in1=y[:, p, :], op0=ALU.mult, op1=ALU.add))
                    for p, v in both:
                        v.sync()
                        v(dve.bn_stats(stat[:, p, 1, :], y[:, p, :]))
                    for p, v in both:
                        v.sync()
                        v(dve.memset(st2[:, p, 14:15], 0.0))
                        v(dve.bn_aggr(st2[:, p, 8:10], stat[:, p, 1, :]))
                        v.mark("var2")
                    for p, v in both:
                        ac_s[p].wait(dve, t, "root2")
                        v(dve.reciprocal(st2[:, p, 11:12], st2[:, p, 10:11]))
                    for p, v in both:
                        v.sync()
                        gate(dve, k)
                        dve.wait_ge(stored[q][p], 16 * t4)
                        v(dve.tensor_scalar(y2[:, q, p, 0:S], y[:, p, 0:S], st2[:, p, 8:9], st2[:, p, 11:12],
                                            ALU.subtract, ALU.mult))
                        v(dve.tensor_scalar(y2[:, q, p, S:X].rearrange("n (u i) -> n i u", i=3),
                                            y[:, p, S:X].rearrange("n (i u) -> n i u", i=3), st2[:, p, 8:9],
                                            st2[:, p, 11:12], ALU.subtract, ALU.mult))
                        v.mark("out")
                        v.end()
                    for p, v in both:
                        v.sync()

                with dve.Fori(0, PAIRS // 2) as t4:
                    for q in range(2):
                        pair(t4, q)

            @block.sync
            def _(sp):
                def load(t, q):
                    for p in range(2):
                        rows = bass.ds((2 * t + p) * R, R)
                        sp.dma_start(xt[:, q, p, :], X1[rows, :]).then_inc(here[q][p], 16)
                        sp.dma_start(nv[:, q, p, 0:1], nodevec[rows, :]).then_inc(here[q][p], 16)
                        for c in range(COPIES):
                            sp.dma_start(ag[:, q, p, c, :], sums[c][rows, :]).then_inc(here[q][p], 16)

                def store(t, q):
                    for p in range(2):
                        got(sp, t, p, "out")
                        sp.dma_start(out[bass.ds((2 * t + p) * R, R), :], y2[:, q, p, :]).then_inc(stored[q][p], 16)
                load(0, 0)
                load(1, 1)
                with sp.Fori(0, PAIRS // 2 - 1) as t4:
                    for q in range(2):
                        store(2 * t4 + q, q)
                        load(2 * t4 + q + 2, q)
                for q in range(2):
                    store(PAIRS - 2 + q, q)
                for q in range(2):
                    for p in range(2):
                        sp.wait_ge(stored[q][p], 16 * (PAIRS // 2))

            @block.tensor
            def _(pe):
                I = k["ident"]
                one = k["ones"][0:1, 0:R]

                def bias(n):
                    lo, hi = W["row_at"][n]
                    return W["rows"][0:1, lo:hi]

                with pe.Fori(0, PAIRS) as t:
                    for p in range(2):
                        got(pe, t, p, "weighted")
                        pe.transpose(bank[p][0][0:V3, 128:128 + R], a[:, p, S:X], I[0:R, 0:R])
                        pe_s[p].done(pe.transpose(bank[p][0][0:S, 0:R], a[:, p, 0:S], I[0:R, 0:R]), "turned")
                    for p in range(2):
                        ac_s[p].wait(pe, t, "turned")
                        pe.matmul(bank[p][1][0:R, 0:S], sT[:, p, :], W["pws"][:], start=True, stop=False)
                        pe.matmul(bank[p][1][0:R, 0:S], one, bias("proj_bs"), start=False, stop=True)
                        pe_s[p].done(pe.matmul(bank[p][1][0:R, S:X], vT[:, p, :], W["pwv"][:], start=True,
                                               stop=True), "proj")
                    for p in range(2):
                        got(pe, t, p, "norm")
                        pe.transpose(bank[p][0][0:V3, 128:128 + R], norm[:, p, S:X], I[0:R, 0:R])
                        pe_s[p].done(pe.transpose(bank[p][0][0:S, 0:R], norm[:, p, 0:S], I[0:R, 0:R]), "norm")
                    for p in range(2):
                        ac_s[p].wait(pe, t, "norm")
                        pe.matmul(bank[p][2][0:R, 0:192], sT2[:, p, :], W["f1s"][:], start=True, stop=False)
                        pe.matmul(bank[p][2][0:R, 0:192], one, bias("f1_bs"), start=False, stop=True)
                        pe_s[p].done(pe.matmul(bank[p][3][0:R, 0:192], vT2[:, p, :], W["f1v"][:], start=True,
                                               stop=True), "f1")
                    for p in range(2):
                        got(pe, t, p, "gated")
                        pe.transpose(bank[p][0][:, 0:R], sc[:, p, :], I[0:R, 0:R])
                        pe.transpose(bank[p][0][:, 128:128 + R], fv[:, p, 0:128], I[0:R, 0:R])
                        pe_s[p].done(pe.transpose(bank[p][0][0:S, 256:256 + R], fv[:, p, 128:192], I[0:R, 0:R]), "mid")
                    for p in range(2):
                        ac_s[p].wait(pe, t, "mid")
                        f2 = bank[p][1][0:R, 256:256 + X]
                        pe.matmul(f2[:, 0:S], scT[:, p, :], W["f2s"][:], start=True, stop=False)
                        pe.matmul(f2[:, 0:S], one, bias("f2_bs"), start=False, stop=True)
                        pe.matmul(f2[:, S:S + 2 * V], fvT[:, p, :], W["f2a"][:], start=True, stop=True)
                        pe_s[p].done(pe.matmul(f2[:, S + 2 * V:X], fwT[:, p, :], W["f2b"][:], start=True, stop=True), "f2")

            @block.scalar
            def _(act):
                with act.Fori(0, PAIRS // 2) as t4:
                    for q in range(2):
                        t = 2 * t4 + q
                        for p in range(2):
                            pe_s[p].wait(act, t, "turned")
                            act.activation(sT[:, p, :], bank[p][0][0:S, 0:R], ACT.Copy)
                            ac_s[p].done(act.activation(vT[:, p, :], bank[p][0][0:V3, 128:128 + R], ACT.Copy), "turned")
                        for p in range(2):
                            got(act, t, p, "var1")
                            ac_s[p].done(act.activation(st2[:, p, 4:6], st2[:, p, 1:3], ACT.Sqrt, bias=W["eps"][0:R, :]),
                                         "root1")
                        for p in range(2):
                            pe_s[p].wait(act, t, "norm")
                            act.activation(sT2[:, p, :], bank[p][0][0:S, 0:R], ACT.Identity, bias=W["ln2"][0:S, 1:2],
                                           scale=W["ln2"][0:S, 0:1])
                            ac_s[p].done(act.activation(vT2[:, p, :], bank[p][0][0:V3, 128:128 + R], ACT.Copy,
                                                        scale=W["ln2"][0:V3, 2:3]), "norm")
                        for p in range(2):
                            pe_s[p].wait(act, t, "f1")
                            act.activation(sc[:, p, :], bank[p][2][0:R, 0:128], ACT.Silu, scale=nv[:, q, p, 0:1])
                            ac_s[p].done(act.activation(sg[:, p, :], bank[p][2][0:R, 128:192], ACT.Tanh,
                                                        scale=nv[:, q, p, 1:2]), "gates")
                        for p in range(2):
                            pe_s[p].wait(act, t, "mid")
                            act.activation(scT[:, p, :], bank[p][0][:, 0:R], ACT.Copy)
                            act.activation(fvT[:, p, :], bank[p][0][:, 128:128 + R], ACT.Copy)
                            ac_s[p].done(act.activation(fwT[:, p, :], bank[p][0][0:S, 256:256 + R], ACT.Copy), "mid")
                        for p in range(2):
                            got(act, t, p, "var2")
                            ac_s[p].done(act.activation(st2[:, p, 10:11], st2[:, p, 9:10], ACT.Sqrt,
                                                        bias=W["eps"][0:R, :]), "root2")


WEIGHTS0 = ["Wm_ss", "Wm_vv", "Wm_sv", "Wm_vs", "Lm_s", "Lm_v", "Wu_ss", "Wu_vv", "Wu_sv", "Wu_vs", "Lu_s", "Lu_v"]
WEIGHTS1 = ["ln1_w0", "ln1_b0", "ln1_w1", "ln2_w0", "ln2_b0", "ln2_w1", "msrc_ws", "msrc_wv", "mdst_ws", "mdst_bs",
            "mdst_wv", "rw1", "rb1", "rg1", "rbe1", "rw2", "rb2", "rg2", "rbe2", "rw3", "roff", "lin_ws", "lin_bs",
            "lin_wv", "alpha_dot", "proj_ws", "proj_bs", "proj_wv", "f1_ws", "f1_bs", "f1_wv", "f2_ws", "f2_bs",
            "f2_wv"]
ROWS = 12672


def program(nc, x, src, dst, ea3, ea4, ea64, nodevec, ranks, w, out):
    def table(name, *shape):
        return nc.dram_tensor(name, shape, F32, kind="Internal").ap()

    with ExitStack() as ctx:
        m = Mem(nc, ctx)
        ps = ctx.enter_context(nc.psum_tensor("ps", [128, 8, 512], F32))
        k = constants(nc, m, ranks)
        T0 = table("T0", N, 448)
        sums0 = [table(f"sums0_{c}", ROWS, MSG0) for c in range(COPIES)]
        sums1 = [table(f"sums1_{c}", ROWS, MSG1) for c in range(COPIES)]
        X1, TS, TD = (table(n, N, X) for n in ("X1", "TS", "TD"))
        H = table("H", ET // (2 * GT), 128, GT * R)
        VAL = table("VAL", ET // GT, R, GT * X)
        scratch = table("scratch", 4, HEADS * CH)
        for c in range(COPIES):
            clear(nc, m, k, f"clear0_{c}", sums0[c].rearrange("(a r) w -> a r w", a=1))
            clear(nc, m, k, f"clear1_{c}", sums1[c].rearrange("(a r) w -> a r w", a=1))
        src1, dst1 = (v.rearrange("(n a) -> n a", a=1) for v in (src, dst))
        dstI = m.sb("dstI", [R, 1, ET], I32)
        edge_rows(nc, m, k, ps, "dst", dst1, 1, I32, None, dstI)
        W = {n: m.sb("w_" + n, shape) for n, shape in dict(rows=[1, 1024], ln1=[V3, 3], ln2=[V3, 3],
                                                           eps=[128, 1]).items()}
        weights2(nc, m, k, ps, w, W)
        with ExitStack() as c0:
            m0 = Mem(nc, c0)
            W.update(weights0(nc, m0, k, w))
            weights1(nc, m0, k, w, W)
            layer0_tables(nc, m0, k, ps, x, W, T0)
            with ExitStack() as c1:
                m1 = Mem(nc, c1)
                srcF, attr = m1.sb("srcF", [R, 1, ET]), m1.sb("attr", [R, 4, ET])
                edge_rows(nc, m1, k, ps, "src", src1, 1, I32, srcF, None)
                edge_rows(nc, m1, k, ps, "ea4", ea4, 4, F32, attr, None)
                layer0_edges(nc, m1, k, ps, W, T0, dstI, srcF, src, attr, sums0, ea64, H)
            node_update0(nc, m0, k, ps, W, x, sums0, X1, TS, TD)
        with ExitStack() as c0:
            m0 = Mem(nc, c0)
            a_sb = m0.sb("logits", [R, ET, HEADS])
            with ExitStack() as c1:
                m1 = Mem(nc, c1)
                srcI, yx = m1.sb("srcI", [R, 1, ET], I32), m1.sb("yx", [R, 5, ET])
                edge_rows(nc, m1, k, ps, "src_again", src1, 1, I32, None, srcI)
                with ExitStack() as c2:
                    m2 = Mem(nc, c2)
                    a3 = m2.sb("a3", [R, 3, ET])
                    edge_rows(nc, m2, k, ps, "ea3", ea3, 3, F32, a3, None)
                    directions(nc, m2, k, W, a3, yx)
                layer1_edges(nc, m1, k, ps, W, TS, TD, srcI, dstI, H, yx, a_sb, VAL)
            softmax_weights(nc, m0, k, ps, a_sb, dst, scratch)
            dstF = m0.sb("dstF", [R, 1, ET])
            edge_rows(nc, m0, k, ps, "dst_again", dst1, 1, I32, dstF, None)
            layer1_sums(nc, m0, k, ps, a_sb, dstF, dst, VAL, sums1)
        with ExitStack() as c0:
            m0 = Mem(nc, c0)
            weights3(nc, m0, k, w, W)
            node_update1(nc, m0, k, ps, W, X1, nodevec, sums1, out)


def kernel(**inputs):
    import concourse.bacc as bacc
    from concourse.bass_utils import run_bass_kernel_spmd

    nc = bacc.Bacc("TRN2", target_bir_lowering=False, num_devices=1)
    arrays = {}

    def given(name, a):
        a = np.ascontiguousarray(a)
        arrays[name] = a
        return nc.dram_tensor(name, a.shape, mybir.dt.from_np(a.dtype), kind="ExternalInput").ap()

    plain = [given("in_" + n, inputs[n]) for n in
             ("x", "src", "dst", "edge_attr_3", "edge_attr_4", "edge_attr_64", "node_vec1")]
    ranks = given("ranks", strict_ranks())
    w = {n: given("in_" + n, inputs["L0_gnn_" + n]) for n in WEIGHTS0}
    w.update({n: given("in_" + n, inputs["L1_gnn_" + n]) for n in WEIGHTS1})
    out = nc.dram_tensor("out", (N, X), F32, kind="ExternalOutput").ap()
    program(nc, *plain, ranks, w, out)
    result = run_bass_kernel_spmd(nc, [arrays], core_ids=[0])
    return result.results[0]["out"]
```
